# Optimizing a Trainium2 kernel written in Bass

```python
import numpy as np
import jax
import jax.numpy as jnp

def _softmax(x, axis=-1):
    return jax.nn.softmax(x, axis=axis)

def _gelu(x):
    return jax.nn.gelu(x, approximate=True)

def _silu(x):
    return jax.nn.silu(x)

def _sigmoid(x):
    return jax.nn.sigmoid(x)

def _layernorm(x, axis=-1, eps=1e-05):
    m = jnp.mean(x, axis=axis, keepdims=True)
    v = jnp.var(x, axis=axis, keepdims=True)
    return (x - m) / jnp.sqrt(v + eps)

def _scatter_add(tgt, idx, src, axis=0):
    return tgt.at[idx].add(src)

def _segment_sum(src, seg, n):
    return jax.ops.segment_sum(src, seg, n)
kernel_name = 'mk_hybrid_d2_jaxref_r8_9a4760'

def setup_inputs(seed: int=0):
    np.random.seed(seed)
    _w = jnp.asarray

    def _L0_attn_a_setup():
        import jax, jax.numpy as jnp
        import numpy as np
        D_MODEL = 512
        NUM_HEADS = 32
        HEAD_DIM = D_MODEL // NUM_HEADS
        Q_LAT = 12
        KV_LAT = 4
        B, S = (2, 256)
        key = jax.random.key(seed)
        ks = jax.random.split(key, 6)
        sc = lambda fan_in: 1.0 / np.sqrt(fan_in)
        return {'x': jax.random.normal(ks[0], (B, S, D_MODEL), jnp.float32), 'Wq_d': jax.random.normal(ks[1], (D_MODEL, Q_LAT), jnp.float32) * sc(D_MODEL), 'bq_d': jnp.zeros((Q_LAT,), jnp.float32), 'W_qk': jax.random.normal(ks[2], (Q_LAT, NUM_HEADS * KV_LAT), jnp.float32) * sc(Q_LAT), 'b_qk': jnp.zeros((NUM_HEADS * KV_LAT,), jnp.float32), 'Wkv_d': jax.random.normal(ks[3], (D_MODEL, KV_LAT), jnp.float32) * sc(D_MODEL), 'bkv_d': jnp.zeros((KV_LAT,), jnp.float32), 'Wv_u': jax.random.normal(ks[4], (KV_LAT, NUM_HEADS * HEAD_DIM), jnp.float32) * sc(KV_LAT), 'bv_u': jnp.zeros((NUM_HEADS * HEAD_DIM,), jnp.float32), 'Wo': jax.random.normal(ks[5], (NUM_HEADS * HEAD_DIM, D_MODEL), jnp.float32) * sc(NUM_HEADS * HEAD_DIM), 'bo': jnp.zeros((D_MODEL,), jnp.float32)}
    _L0_attn_a_in = _L0_attn_a_setup()

    def _L0_attn_b_setup():
        import jax, jax.numpy as jnp
        import numpy as np
        HIDDEN = 512
        N_HEADS = 32
        KV_HEADS = 8
        HEAD_DIM = 128
        LOW_RANK = 64
        TOP_K_ROPE = 32
        ROPE_THETA = 10000.0
        B, S = (2, 256)
        GROUPS = N_HEADS // KV_HEADS
        _half = HEAD_DIM // 2
        _m = np.ones(_half, dtype=bool)
        _m[:TOP_K_ROPE] = False
        _m = np.concatenate([_m, _m])
        NOPE_MASK = np.tile(_m, KV_HEADS)
        ROPE_IDX = jnp.asarray(np.where(~NOPE_MASK)[0])
        NOPE_IDX = jnp.asarray(np.where(NOPE_MASK)[0])
        R_DIM = int((~NOPE_MASK).sum())
        C_DIM = LOW_RANK * KV_HEADS

        def _rope_tables(seq_len, dtype):
            inv_freq = 1.0 / ROPE_THETA ** (np.arange(0, HEAD_DIM, 2, dtype=np.float32) / HEAD_DIM)
            pos = np.arange(seq_len, dtype=np.float32)
            freqs = np.outer(pos, inv_freq)
            emb = np.concatenate([freqs, freqs], axis=-1)
            return (jnp.asarray(np.cos(emb), dtype), jnp.asarray(np.sin(emb), dtype))

        def _rotate_half(x):
            x1, x2 = (x[..., :HEAD_DIM // 2], x[..., HEAD_DIM // 2:])
            return jnp.concatenate([-x2, x1], axis=-1)
        key = jax.random.key(seed)
        ks = jax.random.split(key, 7)
        s = 0.02
        return {'hidden_states': jax.random.normal(ks[0], (B, S, HIDDEN), jnp.float32), 'Wq': jax.random.normal(ks[1], (N_HEADS * HEAD_DIM, HIDDEN), jnp.float32) * s, 'Wkr': jax.random.normal(ks[2], (R_DIM, HIDDEN), jnp.float32) * s, 'Wdk': jax.random.normal(ks[3], (C_DIM, HIDDEN), jnp.float32) * s, 'Wupk': jax.random.normal(ks[4], (KV_HEADS * HEAD_DIM - R_DIM, C_DIM), jnp.float32) * s, 'Wupv': jax.random.normal(ks[5], (KV_HEADS * HEAD_DIM, C_DIM), jnp.float32) * s, 'Wo': jax.random.normal(ks[6], (HIDDEN, N_HEADS * HEAD_DIM), jnp.float32) * s}
    _L0_attn_b_in = _L0_attn_b_setup()

    def _L0_ffn_setup():
        import jax, jax.numpy as jnp
        import numpy as np
        LORA_RANK = 16
        LORA_ALPHA = 16
        LORA_SCALE = LORA_ALPHA / LORA_RANK
        key = jax.random.key(seed)
        k1, k2, k3, k4, k5 = jax.random.split(key, 5)
        B, S, D_IN, D_OUT, N_LORA, R = (8, 256, 512, 512, 3, LORA_RANK)
        std = 1.0 / np.sqrt(D_IN)
        x = jax.random.normal(k1, (B, S, D_IN), dtype=jnp.float32)
        weight = jax.random.truncated_normal(k2, -3.0, 3.0, (D_OUT, D_IN), dtype=jnp.float32) * std
        bias = jax.random.normal(k3, (D_OUT,), dtype=jnp.float32) * 0.01
        lora_A = jax.random.normal(k4, (N_LORA, R, D_IN), dtype=jnp.float32) * std
        lora_B = jax.random.normal(k5, (N_LORA, D_OUT, R), dtype=jnp.float32) * 0.02
        lora_start_indices = jnp.arange(4, dtype=jnp.int64) * 2
        return {'x': x, 'weight': weight, 'bias': bias, 'lora_A': lora_A, 'lora_B': lora_B, 'lora_start_indices': lora_start_indices}
    _L0_ffn_in = _L0_ffn_setup()

    def _L1_attn_a_setup():
        import jax, jax.numpy as jnp
        import numpy as np
        B, S, H = (1, 256, 512)
        NH = 32
        QK_NOPE, QK_ROPE, V_DIM = (128, 64, 128)
        Q_LORA, KV_LORA = (192, 64)
        EPS = 1e-06

        def _rms_norm(x, w):
            return x * jax.lax.rsqrt(jnp.mean(x * x, axis=-1, keepdims=True) + EPS) * w

        def _rope_cos_sin(seqlen, dim):
            freqs = 1.0 / 10000.0 ** (jnp.arange(0, dim, 2, dtype=jnp.float32) / dim)
            t = jnp.arange(seqlen, dtype=jnp.float32)
            ang = jnp.outer(t, freqs)
            return (jnp.cos(ang), jnp.sin(ang))

        def _apply_rope(x, cos, sin):
            x1 = x[..., 0::2]
            x2 = x[..., 1::2]
            r1 = x1 * cos - x2 * sin
            r2 = x1 * sin + x2 * cos
            return jnp.stack([r1, r2], axis=-1).reshape(x.shape)
        key = jax.random.key(seed)
        ks = jax.random.split(key, 7)
        s = 0.02
        return {'x': jax.random.normal(ks[0], (B, S, H), jnp.float32), 'wq_a': jax.random.normal(ks[1], (Q_LORA, H), jnp.float32) * s, 'q_norm_w': jnp.ones((Q_LORA,), jnp.float32), 'wq_b': jax.random.normal(ks[2], (NH * (QK_NOPE + QK_ROPE), Q_LORA), jnp.float32) * s, 'wkv_a': jax.random.normal(ks[3], (KV_LORA + QK_ROPE, H), jnp.float32) * s, 'kv_norm_w': jnp.ones((KV_LORA,), jnp.float32), 'wkv_b': jax.random.normal(ks[4], (NH * (QK_NOPE + V_DIM), KV_LORA), jnp.float32) * s, 'wo': jax.random.normal(ks[5], (H, NH * V_DIM), jnp.float32) * s}
    _L1_attn_a_in = _L1_attn_a_setup()

    def _L1_attn_b_setup():
        import jax, jax.numpy as jnp
        import numpy as np
        B, S, E, H = (2, 256, 512, 32)
        D = E // H
        ROPE_BASE = 10000.0
        MASK_VAL = -66504.0

        def _rope(x, cos, sin):
            x1, x2 = jnp.split(x, 2, axis=-1)
            return jnp.concatenate([x1 * cos - x2 * sin, x2 * cos + x1 * sin], axis=-1)
        key = jax.random.key(seed)
        k1, k2, k3, k4, k5 = jax.random.split(key, 5)
        return {'hidden_states': jax.random.normal(k1, (B, S, E), dtype=jnp.float32), 'qkv_w': jax.random.normal(k2, (E, 3 * E), dtype=jnp.float32) * 0.02, 'qkv_b': jax.random.normal(k3, (3 * E,), dtype=jnp.float32) * 0.02, 'out_w': jax.random.normal(k4, (E, E), dtype=jnp.float32) * 0.02, 'out_b': jax.random.normal(k5, (E,), dtype=jnp.float32) * 0.02}
    _L1_attn_b_in = _L1_attn_b_setup()

    def _L1_ffn_setup():
        import jax, jax.numpy as jnp
        import numpy as np
        R = 16
        NUM_EXPERTS = 8
        TOP_K = 2
        LORA_ALPHA = 32
        SCALING = LORA_ALPHA / R
        key = jax.random.key(seed)
        ks = jax.random.split(key, 6)
        d_in, d_out = (512, 512)
        x = jax.random.normal(ks[0], (4, 256, d_in), dtype=jnp.float32)
        W_base = jax.random.normal(ks[1], (d_out, d_in), dtype=jnp.float32) * 0.02
        b_base = jax.random.normal(ks[2], (d_out,), dtype=jnp.float32) * 0.02
        W_router = jax.random.normal(ks[3], (NUM_EXPERTS, d_in), dtype=jnp.float32) * 0.01
        A = jax.random.normal(ks[4], (NUM_EXPERTS, R, d_in), dtype=jnp.float32) * 0.02
        B = jax.random.normal(ks[5], (NUM_EXPERTS, d_out, R), dtype=jnp.float32) * 0.02
        return {'x': x, 'W_base': W_base, 'b_base': b_base, 'W_router': W_router, 'A': A, 'B': B}
    _L1_ffn_in = _L1_ffn_setup()
    _d = {'L0_attn_a_x': _L0_attn_a_in['x'], 'L0_attn_a_Wq_d': _L0_attn_a_in['Wq_d'], 'L0_attn_a_bq_d': _L0_attn_a_in['bq_d'], 'L0_attn_a_W_qk': _L0_attn_a_in['W_qk'], 'L0_attn_a_b_qk': _L0_attn_a_in['b_qk'], 'L0_attn_a_Wkv_d': _L0_attn_a_in['Wkv_d'], 'L0_attn_a_bkv_d': _L0_attn_a_in['bkv_d'], 'L0_attn_a_Wv_u': _L0_attn_a_in['Wv_u'], 'L0_attn_a_bv_u': _L0_attn_a_in['bv_u'], 'L0_attn_a_Wo': _L0_attn_a_in['Wo'], 'L0_attn_a_bo': _L0_attn_a_in['bo'], 'L0_attn_b_Wq': _L0_attn_b_in['Wq'], 'L0_attn_b_Wkr': _L0_attn_b_in['Wkr'], 'L0_attn_b_Wdk': _L0_attn_b_in['Wdk'], 'L0_attn_b_Wupk': _L0_attn_b_in['Wupk'], 'L0_attn_b_Wupv': _L0_attn_b_in['Wupv'], 'L0_attn_b_Wo': _L0_attn_b_in['Wo'], 'L0_ffn_weight': _L0_ffn_in['weight'], 'L0_ffn_bias': _L0_ffn_in['bias'], 'L0_ffn_lora_A': _L0_ffn_in['lora_A'], 'L0_ffn_lora_B': _L0_ffn_in['lora_B'], 'L0_ffn_lora_start_indices': _L0_ffn_in['lora_start_indices'], 'L1_attn_a_wq_a': _L1_attn_a_in['wq_a'], 'L1_attn_a_q_norm_w': _L1_attn_a_in['q_norm_w'], 'L1_attn_a_wq_b': _L1_attn_a_in['wq_b'], 'L1_attn_a_wkv_a': _L1_attn_a_in['wkv_a'], 'L1_attn_a_kv_norm_w': _L1_attn_a_in['kv_norm_w'], 'L1_attn_a_wkv_b': _L1_attn_a_in['wkv_b'], 'L1_attn_a_wo': _L1_attn_a_in['wo'], 'L1_attn_b_qkv_w': _L1_attn_b_in['qkv_w'], 'L1_attn_b_qkv_b': _L1_attn_b_in['qkv_b'], 'L1_attn_b_out_w': _L1_attn_b_in['out_w'], 'L1_attn_b_out_b': _L1_attn_b_in['out_b'], 'L1_ffn_W_base': _L1_ffn_in['W_base'], 'L1_ffn_b_base': _L1_ffn_in['b_base'], 'L1_ffn_W_router': _L1_ffn_in['W_router'], 'L1_ffn_A': _L1_ffn_in['A'], 'L1_ffn_B': _L1_ffn_in['B']}
    _x0 = _d['L0_attn_a_x']
    _d['L0_attn_a_x'] = jax.random.normal(jax.random.fold_in(jax.random.key(seed), 1), (2, 512, 512), dtype=_x0.dtype)
    del _x0
    return _d

def reference(L0_attn_a_x, L0_attn_a_Wq_d, L0_attn_a_bq_d, L0_attn_a_W_qk, L0_attn_a_b_qk, L0_attn_a_Wkv_d, L0_attn_a_bkv_d, L0_attn_a_Wv_u, L0_attn_a_bv_u, L0_attn_a_Wo, L0_attn_a_bo, L0_attn_b_Wq, L0_attn_b_Wkr, L0_attn_b_Wdk, L0_attn_b_Wupk, L0_attn_b_Wupv, L0_attn_b_Wo, L0_ffn_weight, L0_ffn_bias, L0_ffn_lora_A, L0_ffn_lora_B, L0_ffn_lora_start_indices, L1_attn_a_wq_a, L1_attn_a_q_norm_w, L1_attn_a_wq_b, L1_attn_a_wkv_a, L1_attn_a_kv_norm_w, L1_attn_a_wkv_b, L1_attn_a_wo, L1_attn_b_qkv_w, L1_attn_b_qkv_b, L1_attn_b_out_w, L1_attn_b_out_b, L1_ffn_W_base, L1_ffn_b_base, L1_ffn_W_router, L1_ffn_A, L1_ffn_B):

    def _L0_attn_a_ref(x, Wq_d, bq_d, W_qk, b_qk, Wkv_d, bkv_d, Wv_u, bv_u, Wo, bo):
        import jax, jax.numpy as jnp
        import numpy as np
        D_MODEL = 512
        NUM_HEADS = 32
        HEAD_DIM = D_MODEL // NUM_HEADS
        Q_LAT = 12
        KV_LAT = 4
        B, S = (2, 256)
        b, s, _ = x.shape
        C_q = x @ Wq_d + bq_d
        C_kv = x @ Wkv_d + bkv_d
        q = (C_q @ W_qk + b_qk).reshape(b, s, NUM_HEADS, KV_LAT)
        scores = jnp.einsum('bqhd,bkd->bhqk', q, C_kv) / jnp.sqrt(jnp.asarray(KV_LAT, x.dtype))
        attn = jax.nn.softmax(scores, axis=-1)
        V = (C_kv @ Wv_u + bv_u).reshape(b, s, NUM_HEADS, HEAD_DIM)
        out = jnp.einsum('bhqk,bkhd->bqhd', attn, V).reshape(b, s, NUM_HEADS * HEAD_DIM)
        return out @ Wo + bo

    def _L0_attn_b_ref(hidden_states, Wq, Wkr, Wdk, Wupk, Wupv, Wo):
        import jax, jax.numpy as jnp
        import numpy as np
        HIDDEN = 512
        N_HEADS = 32
        KV_HEADS = 8
        HEAD_DIM = 128
        LOW_RANK = 64
        TOP_K_ROPE = 32
        ROPE_THETA = 10000.0
        B, S = (2, 256)
        GROUPS = N_HEADS // KV_HEADS
        _half = HEAD_DIM // 2
        _m = np.ones(_half, dtype=bool)
        _m[:TOP_K_ROPE] = False
        _m = np.concatenate([_m, _m])
        NOPE_MASK = np.tile(_m, KV_HEADS)
        ROPE_IDX = jnp.asarray(np.where(~NOPE_MASK)[0])
        NOPE_IDX = jnp.asarray(np.where(NOPE_MASK)[0])
        R_DIM = int((~NOPE_MASK).sum())
        C_DIM = LOW_RANK * KV_HEADS

        def _rope_tables(seq_len, dtype):
            inv_freq = 1.0 / ROPE_THETA ** (np.arange(0, HEAD_DIM, 2, dtype=np.float32) / HEAD_DIM)
            pos = np.arange(seq_len, dtype=np.float32)
            freqs = np.outer(pos, inv_freq)
            emb = np.concatenate([freqs, freqs], axis=-1)
            return (jnp.asarray(np.cos(emb), dtype), jnp.asarray(np.sin(emb), dtype))

        def _rotate_half(x):
            x1, x2 = (x[..., :HEAD_DIM // 2], x[..., HEAD_DIM // 2:])
            return jnp.concatenate([-x2, x1], axis=-1)
        bsz, q_len, _ = hidden_states.shape
        dt = hidden_states.dtype
        q = (hidden_states @ Wq.T).reshape(bsz, q_len, N_HEADS, HEAD_DIM).transpose(0, 2, 1, 3)
        k_r0 = hidden_states @ Wkr.T
        key_flat = jnp.zeros((bsz, q_len, KV_HEADS * HEAD_DIM), dt).at[..., ROPE_IDX].set(k_r0)
        k = key_flat.reshape(bsz, q_len, KV_HEADS, HEAD_DIM).transpose(0, 2, 1, 3)
        cos, sin = _rope_tables(q_len, dt)
        cos, sin = (cos[None, None], sin[None, None])
        q = q * cos + _rotate_half(q) * sin
        k = k * cos + _rotate_half(k) * sin
        k_r = k.transpose(0, 2, 1, 3).reshape(bsz, q_len, KV_HEADS * HEAD_DIM)[..., ROPE_IDX]
        c_kv = hidden_states @ Wdk.T
        k_c = c_kv @ Wupk.T
        v = (c_kv @ Wupv.T).reshape(bsz, q_len, KV_HEADS, HEAD_DIM).transpose(0, 2, 1, 3)
        key_full = jnp.zeros((bsz, q_len, KV_HEADS * HEAD_DIM), dt).at[..., NOPE_IDX].set(k_c).at[..., ROPE_IDX].set(k_r)
        k = key_full.reshape(bsz, q_len, KV_HEADS, HEAD_DIM).transpose(0, 2, 1, 3)
        k = jnp.repeat(k, GROUPS, axis=1)
        v = jnp.repeat(v, GROUPS, axis=1)
        scale = 1.0 / jnp.sqrt(jnp.asarray(HEAD_DIM, dt))
        scores = jnp.einsum('bhqd,bhkd->bhqk', q, k) * scale
        causal = jnp.tril(jnp.ones((q_len, q_len), bool))
        scores = jnp.where(causal[None, None], scores, jnp.asarray(-1000000000.0, dt))
        attn = jax.nn.softmax(scores, axis=-1)
        out = jnp.einsum('bhqk,bhkd->bhqd', attn, v)
        out = out.transpose(0, 2, 1, 3).reshape(bsz, q_len, N_HEADS * HEAD_DIM)
        return out @ Wo.T

    def _L0_ffn_ref(x, weight, bias, lora_A, lora_B, lora_start_indices):
        import jax, jax.numpy as jnp
        import numpy as np
        LORA_RANK = 16
        LORA_ALPHA = 16
        LORA_SCALE = LORA_ALPHA / LORA_RANK
        y = jnp.einsum('bsd,od->bso', x, weight) + bias
        B = x.shape[0]
        seg = jnp.searchsorted(lora_start_indices, jnp.arange(B), side='right') - 1
        adapter_idx = jnp.clip(seg - 1, 0, lora_A.shape[0] - 1)
        A = lora_A[adapter_idx]
        Bw = lora_B[adapter_idx]
        lo = jnp.einsum('bsr,bor->bso', jnp.einsum('bsd,brd->bsr', x, A), Bw) * LORA_SCALE
        use_lora = (seg > 0)[:, None, None]
        return y + jnp.where(use_lora, lo, jnp.zeros((), dtype=y.dtype))

    def _L1_attn_a_ref(x, wq_a, q_norm_w, wq_b, wkv_a, kv_norm_w, wkv_b, wo):
        import jax, jax.numpy as jnp
        import numpy as np
        B, S, H = (1, 256, 512)
        NH = 32
        QK_NOPE, QK_ROPE, V_DIM = (128, 64, 128)
        Q_LORA, KV_LORA = (192, 64)
        EPS = 1e-06

        def _rms_norm(x, w):
            return x * jax.lax.rsqrt(jnp.mean(x * x, axis=-1, keepdims=True) + EPS) * w

        def _rope_cos_sin(seqlen, dim):
            freqs = 1.0 / 10000.0 ** (jnp.arange(0, dim, 2, dtype=jnp.float32) / dim)
            t = jnp.arange(seqlen, dtype=jnp.float32)
            ang = jnp.outer(t, freqs)
            return (jnp.cos(ang), jnp.sin(ang))

        def _apply_rope(x, cos, sin):
            x1 = x[..., 0::2]
            x2 = x[..., 1::2]
            r1 = x1 * cos - x2 * sin
            r2 = x1 * sin + x2 * cos
            return jnp.stack([r1, r2], axis=-1).reshape(x.shape)
        b, s, _ = x.shape
        cos, sin = _rope_cos_sin(s, QK_ROPE)
        q = _rms_norm(x @ wq_a.T, q_norm_w) @ wq_b.T
        q = q.reshape(b, s, NH, QK_NOPE + QK_ROPE)
        q_nope, q_pe = (q[..., :QK_NOPE], q[..., QK_NOPE:])
        q_pe = _apply_rope(q_pe, cos[None, :, None, :], sin[None, :, None, :])
        kv = x @ wkv_a.T
        kv_c, k_pe = (kv[..., :KV_LORA], kv[..., KV_LORA:])
        k_pe = _apply_rope(k_pe, cos[None, :, :], sin[None, :, :])
        kv_up = _rms_norm(kv_c, kv_norm_w) @ wkv_b.T
        kv_up = kv_up.reshape(b, s, NH, QK_NOPE + V_DIM)
        k_nope, v = (kv_up[..., :QK_NOPE], kv_up[..., QK_NOPE:])
        scale = 1.0 / jnp.sqrt(jnp.float32(QK_NOPE + QK_ROPE))
        scores = (jnp.einsum('bshd,bthd->bhst', q_nope, k_nope) + jnp.einsum('bshd,btd->bhst', q_pe, k_pe)) * scale
        causal = jnp.tril(jnp.ones((s, s), bool))
        scores = jnp.where(causal[None, None], scores, jnp.finfo(scores.dtype).min)
        probs = jax.nn.softmax(scores, axis=-1)
        out = jnp.einsum('bhst,bthd->bshd', probs, v).reshape(b, s, NH * V_DIM)
        return out @ wo.T

    def _L1_attn_b_ref(hidden_states, qkv_w, qkv_b, out_w, out_b):
        import jax, jax.numpy as jnp
        import numpy as np
        B, S, E, H = (2, 256, 512, 32)
        D = E // H
        ROPE_BASE = 10000.0
        MASK_VAL = -66504.0

        def _rope(x, cos, sin):
            x1, x2 = jnp.split(x, 2, axis=-1)
            return jnp.concatenate([x1 * cos - x2 * sin, x2 * cos + x1 * sin], axis=-1)
        b, s, e = hidden_states.shape
        qkv = hidden_states @ qkv_w + qkv_b
        q, k, v = jnp.split(qkv, 3, axis=-1)
        q = q.reshape(b, s, H, D)
        k = k.reshape(b, s, H, D)
        v = v.reshape(b, s, H, D)
        half = D // 2
        inv_freq = 1.0 / ROPE_BASE ** (jnp.arange(0, half, dtype=jnp.float32) / half)
        ang = jnp.arange(s, dtype=jnp.float32)[:, None] * inv_freq[None, :]
        cos = jnp.cos(ang)[None, :, None, :]
        sin = jnp.sin(ang)[None, :, None, :]
        q = _rope(q, cos, sin)
        k = _rope(k, cos, sin)
        scale = 1.0 / jnp.sqrt(jnp.asarray(D, dtype=hidden_states.dtype))
        scores = jnp.einsum('bqhd,bkhd->bhqk', q, k) * scale
        causal = jnp.tril(jnp.ones((s, s), dtype=scores.dtype))
        scores = scores + (1.0 - causal) * MASK_VAL
        probs = jax.nn.softmax(scores, axis=-1)
        ctx = jnp.einsum('bhqk,bkhd->bqhd', probs, v).reshape(b, s, e)
        return ctx @ out_w + out_b

    def _L1_ffn_ref(x, W_base, b_base, W_router, A, B):
        import jax, jax.numpy as jnp
        import numpy as np
        R = 16
        NUM_EXPERTS = 8
        TOP_K = 2
        LORA_ALPHA = 32
        SCALING = LORA_ALPHA / R
        orig_shape = x.shape
        d_in = x.shape[-1]
        x_flat = x.reshape(-1, d_in)
        logits = x_flat @ W_router.T
        probs = jax.nn.softmax(logits, axis=-1)
        topk_probs, topk_idx = jax.lax.top_k(probs, TOP_K)
        topk_probs = topk_probs / jnp.sum(topk_probs, axis=-1, keepdims=True)
        onehot = jax.nn.one_hot(topk_idx, NUM_EXPERTS, dtype=x.dtype)
        combine = jnp.einsum('nk,nke->ne', topk_probs, onehot)
        h = jnp.einsum('nd,erd->ner', x_flat, A)
        hw = h * combine[:, :, None]
        expert_out = jnp.einsum('ner,eor->no', hw, B) * SCALING
        base_out = x_flat @ W_base.T + b_base
        out = base_out + expert_out
        return out.reshape(*orig_shape[:-1], W_base.shape[0])
    x = L0_attn_a_x
    x = x + _L0_attn_a_ref(_layernorm(x, axis=-1), L0_attn_a_Wq_d, L0_attn_a_bq_d, L0_attn_a_W_qk, L0_attn_a_b_qk, L0_attn_a_Wkv_d, L0_attn_a_bkv_d, L0_attn_a_Wv_u, L0_attn_a_bv_u, L0_attn_a_Wo, L0_attn_a_bo)
    x = x + _L0_ffn_ref(_layernorm(x, axis=-1), L0_ffn_weight, L0_ffn_bias, L0_ffn_lora_A, L0_ffn_lora_B, L0_ffn_lora_start_indices)
    x = x + _L0_attn_b_ref(_layernorm(x, axis=-1), L0_attn_b_Wq, L0_attn_b_Wkr, L0_attn_b_Wdk, L0_attn_b_Wupk, L0_attn_b_Wupv, L0_attn_b_Wo)
    x = x + _L0_ffn_ref(_layernorm(x, axis=-1), L0_ffn_weight, L0_ffn_bias, L0_ffn_lora_A, L0_ffn_lora_B, L0_ffn_lora_start_indices)
    x = x + _L1_attn_a_ref(_layernorm(x, axis=-1), L1_attn_a_wq_a, L1_attn_a_q_norm_w, L1_attn_a_wq_b, L1_attn_a_wkv_a, L1_attn_a_kv_norm_w, L1_attn_a_wkv_b, L1_attn_a_wo)
    x = x + _L1_ffn_ref(_layernorm(x, axis=-1), L1_ffn_W_base, L1_ffn_b_base, L1_ffn_W_router, L1_ffn_A, L1_ffn_B)
    x = x + _L1_attn_b_ref(_layernorm(x, axis=-1), L1_attn_b_qkv_w, L1_attn_b_qkv_b, L1_attn_b_out_w, L1_attn_b_out_b)
    x = x + _L1_ffn_ref(_layernorm(x, axis=-1), L1_ffn_W_base, L1_ffn_b_base, L1_ffn_W_router, L1_ffn_A, L1_ffn_B)
    return x

_drawn_inputs = setup_inputs


def setup_inputs(seed=0):
    import zlib

    import numpy as np

    out = dict(_drawn_inputs(seed))
    spreads = {'L0_attn_a_bq_d': (0.0, 0.1),
     'L0_attn_a_b_qk': (0.0, 0.1),
     'L0_attn_a_bkv_d': (0.0, 0.1),
     'L0_attn_a_bv_u': (0.0, 0.1),
     'L0_attn_a_bo': (0.0, 0.1),
     'L1_attn_a_q_norm_w': (1.0, 0.6),
     'L1_attn_a_kv_norm_w': (1.0, 0.6)}
    factors = {'L0_attn_b_Wq': 8.0,
     'L0_attn_b_Wkr': 8.0,
     'L0_attn_b_Wupk': 8.0,
     'L0_ffn_bias': 6.877,
     'L1_attn_a_wq_a': 8.0,
     'L1_attn_a_wq_b': 8.0,
     'L1_attn_a_wkv_a': 3.94,
     'L1_attn_a_wkv_b': 3.82,
     'L1_attn_a_wo': 4.0,
     'L1_attn_b_qkv_w': 4.26,
     'L1_attn_b_qkv_b': 8.0,
     'L1_attn_b_out_w': 4.233,
     'L1_attn_b_out_b': 8.0,
     'L1_ffn_b_base': 4.331}
    for name, (base, spread) in spreads.items():
        noise = np.random.default_rng([zlib.crc32(name.encode()), seed]).standard_normal(out[name].shape)
        drawn = base * np.exp(spread * noise) if base else spread * noise
        out[name] = jnp.asarray(drawn.astype(out[name].dtype))
    for name, factor in factors.items():
        out[name] = (out[name] * factor).astype(out[name].dtype)
    return out
```

```python
from contextlib import ExitStack

import numpy as np
import concourse.bass as bass
from concourse import mybir

F32 = mybir.dt.float32
F32R = mybir.dt.float32r
BF16 = mybir.dt.bfloat16
I32 = mybir.dt.int32
U16 = mybir.dt.uint16
U32 = mybir.dt.uint32
ALU = mybir.AluOpType
ACT = mybir.ActivationFunctionType
AX = mybir.AxisListType

P = 128
BATCH, SEQ, DIM = 2, 512, 512
TILES = BATCH * SEQ // P
QT = SEQ // P
KT = DIM // P
HEADS = 32
LN_EPS = 1e-5


def mm3(pe, out, lhs, rhs, start, stop):
    pe.matmul(out, lhs[0], rhs[0], start=start, stop=False)
    pe.matmul(out, lhs[1], rhs[0], start=False, stop=False)
    return pe.matmul(out, lhs[0], rhs[1], start=False, stop=stop)


def pair(hi, lo, *idx):
    return hi[idx], lo[idx]


class Names:

    def __init__(self, nc, ctx, prefix):
        self.nc, self.ctx, self.prefix, self.sems = nc, ctx, prefix, []
        ctx.callback(self.release)

    def sb(self, name, shape, dt=F32):
        return self.ctx.enter_context(self.nc.sbuf_tensor(f"{self.prefix}_{name}", shape, dt))

    def ps(self, name, shape, dt=F32):
        return self.ctx.enter_context(self.nc.psum_tensor(f"{self.prefix}_{name}", shape, dt))

    def sem(self, name):
        self.sems.append(self.nc.alloc_semaphore(f"{self.prefix}_{name}"))
        return self.sems[-1]

    def release(self):
        self.nc.clear_and_free_semaphores(self.sems)
        self.nc.all_engine_barrier()


def load_block(nc, m, d):
    with ExitStack() as ctx:
        n = Names(nc, ctx, "load")
        loaded = n.sem("loaded")
        block = ctx.enter_context(nc.Block())

        @block.sync
        def _(sp):
            sp.dma_start(m.x[:, :, :], d["x"].rearrange("b (t p) c -> p (b t) c", p=P)).then_inc(loaded, 16)
            sp.dma_start(m.ident[:, :], d["ident"]).then_inc(loaded, 16)
            sp.dma_start(m.ident16[:, :].bitcast(U16), d["ident16"]).then_inc(loaded, 16)
            sp.dma_start(m.mask[:, :, :].bitcast(U16), d["mask"]).then_inc(loaded, 16)
            sp.wait_ge(loaded, 64)


def layernorm_block(nc, m, prefix):
    with ExitStack() as ctx:
        n = Names(nc, ctx, prefix)
        stats = n.sb("stats", [P, TILES, 6])
        meanvar = n.sb("meanvar", [P, TILES, 2])
        var_eps = n.sb("var_eps", [P, TILES])
        std = n.sb("std", [P, TILES])
        rstd = n.sb("rstd", [P, TILES])
        xn = n.sb("xn", [P, 2, DIM])
        turned = [n.ps(f"turned{i}", [P, KT, P]) for i in range(2)]
        s_stats, s_aggr, s_var, s_std, s_rstd = [n.sem(k) for k in ("stats", "aggr", "var", "std", "rstd")]
        s_xn, s_turned, s_hi, s_lo = [n.sem(k) for k in ("xn", "turned", "hi", "lo")]
        block = ctx.enter_context(nc.Block())

        @block.vector
        def _(dve):
            for t in range(TILES):
                dve.bn_stats(stats[:, t, :], m.x[:, t, :]).then_inc(s_stats, 1)
            for t in range(TILES):
                dve.wait_ge(s_stats, t + 1)
                dve.bn_aggr(meanvar[:, t, :], stats[:, t, :]).then_inc(s_aggr, 1)
            dve.wait_ge(s_aggr, TILES)
            dve.tensor_scalar(var_eps[:, :], meanvar[:, :, 1], LN_EPS, None, ALU.add).then_inc(s_var, 1)
            dve.wait_ge(s_std, 1)
            dve.reciprocal(rstd[:, :], std[:, :]).then_inc(s_rstd, 1)
            dve.wait_ge(s_rstd, 1)

            def normalise(t):
                if t >= 2:
                    dve.wait_ge(s_turned, t - 1)
                dve.tensor_scalar(xn[:, t % 2, :], m.x[:, t, :], meanvar[:, t, 0:1], rstd[:, t:t + 1],
                                  ALU.subtract, ALU.mult).then_inc(s_xn, 1)

            normalise(0)
            for t in range(TILES):
                if t + 1 < TILES:
                    normalise(t + 1)
                dve.wait_ge(s_turned, t + 1)
                dve.wait_ge(s_hi, t + 1)
                dve.tensor_tensor(m.xnT_lo[:, :, t * P:(t + 1) * P], turned[t % 2][:, :, :],
                                  m.xnT_hi[:, :, t * P:(t + 1) * P].bitcast(F32), ALU.subtract).then_inc(s_lo, 1)

        @block.scalar
        def _(act):
            act.wait_ge(s_var, 1)
            act.activation(std[:, :], var_eps[:, :], ACT.Sqrt).then_inc(s_std, 1)
            for t in range(TILES):
                act.wait_ge(s_turned, t + 1)
                act.activation(m.xnT_hi[:, :, t * P:(t + 1) * P], turned[t % 2][:, :, :],
                               ACT.Copy).then_inc(s_hi, 1)

        @block.tensor
        def _(pe):
            for t in range(TILES):
                pe.wait_ge(s_xn, t + 1)
                if t >= 2:
                    pe.wait_ge(s_lo, t - 1)
                for k in range(KT):
                    last = pe.transpose(turned[t % 2][:, k, :], xn[:, t % 2, k * P:(k + 1) * P], m.ident[:, :])
                last.then_inc(s_turned, 1)


def store_block(nc, m, d):
    with ExitStack() as ctx:
        n = Names(nc, ctx, "store")
        stored = n.sem("stored")
        block = ctx.enter_context(nc.Block())

        @block.sync
        def _(sp):
            sp.dma_start(d["out"].rearrange("b (t p) c -> p (b t) c", p=P), m.x[:, :, :]).then_inc(stored, 16)
            sp.wait_ge(stored, 16)


def ffn0_block(nc, m, d, prefix):
    ADAPTERS, RANK = 3, 16
    AR = ADAPTERS * RANK
    STARTS = 4
    CHUNKS = BATCH * KT
    with ExitStack() as ctx:
        n = Names(nc, ctx, prefix)
        w = n.sb("w", [P, KT, DIM])
        bias = n.sb("bias", [P, DIM])
        lora_a = n.sb("lora_a", [AR, DIM])
        lora_b = n.sb("lora_b", [AR, DIM])
        starts_i = n.sb("starts_i", [AR, STARTS], I32)
        starts = n.sb("starts", [AR, STARTS])
        adapter_of_row = n.sb("adapter_of_row", [AR, 1])
        begun = n.sb("begun", [AR, BATCH, STARTS])
        count = n.sb("count", [AR, BATCH])
        clipped = n.sb("clipped", [AR, BATCH])
        chosen = n.sb("chosen", [AR, BATCH])
        used = n.sb("used", [AR, BATCH])
        gate = n.sb("gate", [AR, BATCH])
        gated_a = n.sb("gated_a", [AR, BATCH, DIM])
        merged = n.sb("merged", [P, 2, DIM])
        w_hi = n.sb("w_hi", [P, BATCH, KT, DIM], F32R)
        w_lo = n.sb("w_lo", [P, BATCH, KT, DIM], F32R)
        delta = [n.ps(f"delta{i}", [P, DIM]) for i in range(2)]
        y = [n.ps(f"y{i}", [P, DIM]) for i in range(2)]
        s_load, s_gate, s_ga, s_delta, s_merged, s_hi, s_lo = [
            n.sem(k) for k in ("load", "gate", "ga", "delta", "merged", "hi", "lo")]
        s_bias, s_y, s_x = [n.sem(k) for k in ("bias", "y", "x")]
        block = ctx.enter_context(nc.Block())

        @block.sync
        def _(sp):
            sp.dma_start(starts_i[:, :], d["lora_starts"].partition_broadcast(AR)).then_inc(s_load, 16)
            sp.dma_start(adapter_of_row[:, :], d["adapter_of_row"]).then_inc(s_load, 16)
            sp.dma_start(lora_a[:, :], d["lora_a"]).then_inc(s_load, 16)
            sp.dma_start(lora_b[:, :], d["lora_b"]).then_inc(s_load, 16)
            sp.dma_start(w[:, :, :], d["ffn0_w"].rearrange("(k p) o -> p k o", p=P)).then_inc(s_load, 16)
            sp.dma_start(bias[:, :], d["ffn0_bias"].partition_broadcast(P)).then_inc(s_load, 16)

        @block.gpsimd
        def _(pool):
            pool.wait_ge(s_load, 96)
            for t in range(TILES):
                pool.tensor_tensor(m.x[:, t, :], m.x[:, t, :], bias[:, :], ALU.add).then_inc(s_bias, 1)

        @block.vector
        def _(dve):
            step = [0]

            def then(ins):
                ins.then_inc(s_gate, 1)
                step[0] += 1
                dve.wait_ge(s_gate, step[0])

            dve.wait_ge(s_load, 96)
            then(dve.tensor_copy(starts[:, :], starts_i[:, :]))
            for b in range(BATCH):
                then(dve.tensor_scalar(begun[:, b, :], starts[:, :], float(b), None, ALU.is_le))
                then(dve.tensor_reduce(count[:, b:b + 1], begun[:, b, :], AX.X, ALU.add))
            then(dve.tensor_scalar(clipped[:, :], count[:, :], -2.0, 0.0, ALU.add, ALU.max))
            then(dve.tensor_scalar(clipped[:, :], clipped[:, :], float(ADAPTERS - 1), None, ALU.min))
            then(dve.tensor_scalar(chosen[:, :], clipped[:, :], adapter_of_row[:, 0:1], None, ALU.is_equal))
            then(dve.tensor_scalar(used[:, :], count[:, :], 2.0, None, ALU.is_ge))
            then(dve.tensor_tensor(gate[:, :], chosen[:, :], used[:, :], ALU.mult))
            for b in range(BATCH):
                dve.tensor_scalar(gated_a[:, b, :], lora_a[:, :], gate[:, b:b + 1], None,
                                  ALU.mult).then_inc(s_ga, 1)

            def merge(c):
                dve.wait_ge(s_delta, c + 1)
                if c >= 2:
                    dve.wait_ge(s_hi, c - 1)
                    dve.wait_ge(s_lo, c - 1)
                dve.tensor_tensor(merged[:, c % 2, :], w[:, c % KT, :], delta[c % 2][:, :],
                                  ALU.add).then_inc(s_merged, 1)

            merge(0)
            for c in range(CHUNKS):
                if c + 1 < CHUNKS:
                    merge(c + 1)
                dve.wait_ge(s_hi, c + 1)
                dve.wait_ge(s_merged, c + 1)
                dve.tensor_tensor(w_lo[:, c // KT, c % KT, :], merged[:, c % 2, :],
                                  w_hi[:, c // KT, c % KT, :].bitcast(F32), ALU.subtract).then_inc(s_lo, 1)
            for t in range(TILES):
                dve.wait_ge(s_bias, t + 1)
                dve.wait_ge(s_y, t + 1)
                dve.tensor_tensor(m.x[:, t, :], m.x[:, t, :], y[t % 2][:, :], ALU.add).then_inc(s_x, 1)

        @block.scalar
        def _(act):
            for c in range(CHUNKS):
                act.wait_ge(s_merged, c + 1)
                act.activation(w_hi[:, c // KT, c % KT, :], merged[:, c % 2, :], ACT.Copy).then_inc(s_hi, 1)

        @block.tensor
        def _(pe):
            for c in range(CHUNKS):
                b, k = divmod(c, KT)
                pe.wait_ge(s_ga, b + 1)
                if c >= 2:
                    pe.wait_ge(s_merged, c - 1)
                pe.matmul(delta[c % 2][:, :], gated_a[:, b, k * P:(k + 1) * P], lora_b[:, :],
                          start=True, stop=True).then_inc(s_delta, 1)
            for t in range(TILES):
                b = t // QT
                pe.wait_ge(s_lo, KT * (b + 1))
                if t >= 2:
                    pe.wait_ge(s_x, t - 1)
                for k in range(KT):
                    last = mm3(pe, y[t % 2][:, :], pair(m.xnT_hi, m.xnT_lo, slice(None), k, bass.ts(t, P)),
                               pair(w_hi, w_lo, slice(None), b, k), start=k == 0, stop=k == KT - 1)
                last.then_inc(s_y, 1)


def ffn1_block(nc, m, d, prefix):
    EXPERTS, RANK, SCALING = 8, 16, 2.0
    ER = EXPERTS * RANK
    NA = ER + EXPERTS
    GAP = 7 * TILES + 3
    with ExitStack() as ctx:
        n = Names(nc, ctx, prefix)
        w = n.sb("w", [P, KT, DIM])
        wa = n.sb("wa", [P, KT, NA])
        wb = n.sb("wb", [ER, DIM])
        bias = n.sb("bias", [P, DIM])
        expert_no = n.sb("expert_no", [P, EXPERTS])
        w_hi, w_lo = n.sb("w_hi", [P, KT, DIM], F32R), n.sb("w_lo", [P, KT, DIM], F32R)
        wa_hi, wa_lo = n.sb("wa_hi", [P, KT, NA], F32R), n.sb("wa_lo", [P, KT, NA], F32R)
        wb_hi, wb_lo = n.sb("wb_hi", [ER, DIM], F32R), n.sb("wb_lo", [ER, DIM], F32R)
        logit = n.sb("logit", [P, TILES, EXPERTS])
        rest = n.sb("rest", [P, TILES, EXPERTS])
        top1, top2 = n.sb("top1", [P, TILES, 8]), n.sb("top2", [P, TILES, 8])
        at1, at2 = n.sb("at1", [P, TILES, 8], U32), n.sb("at2", [P, TILES, 8], U32)
        at1f, at2f = n.sb("at1f", [P, TILES, 1]), n.sb("at2f", [P, TILES, 1])
        hot1, hot2 = n.sb("hot1", [P, TILES, EXPERTS]), n.sb("hot2", [P, TILES, EXPERTS])
        gap, ratio = n.sb("gap", [P, TILES, 1]), n.sb("ratio", [P, TILES, 1])
        denom, first = n.sb("denom", [P, TILES, 1]), n.sb("first", [P, TILES, 1])
        second = n.sb("second", [P, TILES, 1])
        combine = n.sb("combine", [P, TILES, EXPERTS])
        h = n.sb("h", [P, TILES, ER])
        hw = n.sb("hw", [P, TILES, ER])
        hwT_hi, hwT_lo = n.sb("hwT_hi", [ER, 2, P], F32R), n.sb("hwT_lo", [ER, 2, P], F32R)
        proj = [n.ps(f"proj{i}", [P, DIM]) for i in range(2)]
        turned = [n.ps(f"turned{i}", [P, DIM]) for i in range(2)]
        y = [n.ps(f"y{i}", [P, DIM]) for i in range(2)]
        s_load, s_whi, s_wlo, s_proj, s_h, s_r, s_ratio, s_hw, s_turned, s_thi, s_tlo, s_bias, s_y, s_x = [
            n.sem(k) for k in ("load", "whi", "wlo", "proj", "h", "route", "ratio", "hw", "turned", "thi", "tlo",
                               "bias", "y", "x")]
        block = ctx.enter_context(nc.Block())

        @block.sync
        def _(sp):
            sp.dma_start(wa[:, :, :], d["ffn1_a"].rearrange("(k p) o -> p k o", p=P)).then_inc(s_load, 16)
            sp.dma_start(wb[:, :], d["ffn1_b"]).then_inc(s_load, 16)
            sp.dma_start(w[:, :, :], d["ffn1_w"].rearrange("(k p) o -> p k o", p=P)).then_inc(s_load, 16)
            sp.dma_start(bias[:, :], d["ffn1_bias"].partition_broadcast(P)).then_inc(s_load, 16)
            sp.dma_start(expert_no[:, :], d["expert_no"].partition_broadcast(P)).then_inc(s_load, 16)

        @block.gpsimd
        def _(pool):
            pool.wait_ge(s_load, 80)
            for t in range(TILES):
                pool.tensor_tensor(m.x[:, t, :], m.x[:, t, :], bias[:, :], ALU.add).then_inc(s_bias, 1)

        @block.scalar
        def _(act):
            act.wait_ge(s_load, 80)
            act.activation(wa_hi[:, :, :], wa[:, :, :], ACT.Copy).then_inc(s_whi, 1)
            act.activation(wb_hi[:, :], wb[:, :], ACT.Copy).then_inc(s_whi, 1)
            act.activation(w_hi[:, :, :], w[:, :, :], ACT.Copy).then_inc(s_whi, 1)
            for t in range(TILES):
                act.wait_ge(s_proj, t + 1)
                act.activation(h[:, t, :], proj[t % 2][:, 0:ER], ACT.Copy, scale=SCALING).then_inc(s_h, 1)
                act.wait_ge(s_h, 2 * t + 1)
                act.activation(logit[:, t, :], proj[t % 2][:, ER:NA], ACT.Copy).then_inc(s_h, 1)
            act.wait_ge(s_r, GAP)
            act.activation(ratio[:, :, :], gap[:, :, :], ACT.Exp).then_inc(s_ratio, 1)
            for t in range(TILES):
                act.wait_ge(s_turned, t + 1)
                if t >= 2:
                    act.wait_ge(s_y, t - 1)
                act.activation(hwT_hi[:, t % 2, :], turned[t % 2][:, 0:P], ACT.Copy).then_inc(s_thi, 1)

        @block.vector
        def _(dve):
            step = [0]

            def note(ins):
                ins.then_inc(s_r, 1)
                step[0] += 1

            def settle():
                dve.wait_ge(s_r, step[0])

            for i, (lo, full, hi) in enumerate(((wa_lo, wa, wa_hi), (wb_lo, wb, wb_hi), (w_lo, w, w_hi))):
                dve.wait_ge(s_whi, i + 1)
                dve.tensor_tensor(lo[:], full[:], hi[:].bitcast(F32), ALU.subtract).then_inc(s_wlo, 1)
            dve.wait_ge(s_h, 2 * TILES)
            for t in range(TILES):
                note(dve.max(top1[:, t, :], logit[:, t, :]))
            settle()
            for t in range(TILES):
                note(dve.max_index(at1[:, t, :], top1[:, t, :], logit[:, t, :]))
            settle()
            note(dve.tensor_copy(at1f[:, :, :], at1[:, :, 0:1]))
            settle()
            for t in range(TILES):
                note(dve.tensor_scalar(hot1[:, t, :], expert_no[:, :], at1f[:, t, :], None, ALU.is_equal))
            settle()
            for t in range(TILES):
                note(dve.scalar_tensor_tensor(rest[:, t, :], hot1[:, t, :], -3.0e38, logit[:, t, :],
                                              ALU.mult, ALU.add))
            settle()
            for t in range(TILES):
                note(dve.max(top2[:, t, :], rest[:, t, :]))
            settle()
            for t in range(TILES):
                note(dve.max_index(at2[:, t, :], top2[:, t, :], rest[:, t, :]))
            settle()
            note(dve.tensor_copy(at2f[:, :, :], at2[:, :, 0:1]))
            settle()
            for t in range(TILES):
                note(dve.tensor_scalar(hot2[:, t, :], expert_no[:, :], at2f[:, t, :], None, ALU.is_equal))
            note(dve.tensor_tensor(gap[:, :, :], top2[:, :, 0:1], top1[:, :, 0:1], ALU.subtract))
            assert step[0] == GAP
            settle()
            dve.wait_ge(s_ratio, 1)
            note(dve.tensor_scalar(denom[:, :, :], ratio[:, :, :], 1.0, None, ALU.add))
            settle()
            note(dve.reciprocal(first[:, :, :], denom[:, :, :]))
            settle()
            note(dve.tensor_tensor(second[:, :, :], first[:, :, :], ratio[:, :, :], ALU.mult))
            settle()
            for t in range(TILES):
                note(dve.tensor_scalar(hot1[:, t, :], hot1[:, t, :], first[:, t, :], None, ALU.mult))
            settle()
            for t in range(TILES):
                note(dve.scalar_tensor_tensor(combine[:, t, :], hot2[:, t, :], second[:, t, :], hot1[:, t, :],
                                              ALU.mult, ALU.add))
            settle()
            for t in range(TILES):
                dve.tensor_tensor(hw[:, t, :].rearrange("p (e r) -> p e r", e=EXPERTS),
                                  h[:, t, :].rearrange("p (e r) -> p e r", e=EXPERTS),
                                  combine[:, t, :].unsqueeze(2).broadcast_to([P, EXPERTS, RANK]),
                                  ALU.mult).then_inc(s_hw, 1)

            def add_y(t):
                dve.wait_ge(s_y, t + 1)
                dve.wait_ge(s_bias, t + 1)
                dve.tensor_tensor(m.x[:, t, :], m.x[:, t, :], y[t % 2][:, :], ALU.add).then_inc(s_x, 1)

            for t in range(TILES):
                dve.wait_ge(s_thi, t + 1)
                if t >= 2:
                    dve.wait_ge(s_y, t - 1)
                dve.tensor_tensor(hwT_lo[:, t % 2, :], turned[t % 2][:, 0:P], hwT_hi[:, t % 2, :].bitcast(F32),
                                  ALU.subtract).then_inc(s_tlo, 1)
                if t >= 1:
                    add_y(t - 1)
            add_y(TILES - 1)

        @block.tensor
        def _(pe):
            pe.wait_ge(s_wlo, 1)
            for t in range(TILES):
                if t >= 2:
                    pe.wait_ge(s_h, 2 * (t - 1))
                for k in range(KT):
                    last = mm3(pe, proj[t % 2][:, 0:NA], pair(m.xnT_hi, m.xnT_lo, slice(None), k, bass.ts(t, P)),
                               pair(wa_hi, wa_lo, slice(None), k), start=k == 0, stop=k == KT - 1)
                last.then_inc(s_proj, 1)

            def turn(t):
                pe.wait_ge(s_hw, t + 1)
                if t >= 2:
                    pe.wait_ge(s_tlo, t - 1)
                pe.transpose(turned[t % 2][:, 0:P], hw[:, t, :], m.ident[:, :]).then_inc(s_turned, 1)

            pe.wait_ge(s_wlo, 3)
            for t in range(TILES):
                if t >= 2:
                    pe.wait_ge(s_x, t - 1)
                for k in range(KT):
                    mm3(pe, y[t % 2][:, :], pair(m.xnT_hi, m.xnT_lo, slice(None), k, bass.ts(t, P)),
                        pair(w_hi, w_lo, slice(None), k), start=k == 0, stop=False)
                turn(t)
                pe.wait_ge(s_tlo, t + 1)
                mm3(pe, y[t % 2][:, :], pair(hwT_hi, hwT_lo, slice(None), t % 2), (wb_hi[:, :], wb_lo[:, :]),
                    start=False, stop=True).then_inc(s_y, 1)


HEAD = 8


def done(step):
    return step + (1 + HEAD)


class Units:

    def __init__(self, n, per_turn, vdim, sums):
        self.per_turn, self.vdim, self.sums = per_turn, vdim, sums
        self.scores = [n.ps(f"scores{i}", [P, SEQ]) for i in range(2)]
        self.turned = [n.ps(f"probsT_ps{i}", [P, QT, P]) for i in range(2)]
        self.out = [n.ps(f"attended{i}", [P, QT * vdim]) for i in range(2)]
        self.negmax = n.sb("negmax", [P, 4])
        self.probs = n.sb("probs", [P, 4, SEQ])
        self.probsT = n.sb("probsT", [P, 4, QT, P])
        self.sum = n.sb("sum", [P, 2, QT]) if sums else None
        self.recip = n.sb("recip", [P, 2, QT])
        self.s_scores, self.s_max, self.s_exp, self.s_turned = [n.sem(k) for k in ("scores", "max", "exp", "turned")]
        self.s_copied = [n.sem("copied_even"), n.sem("copied_odd")]
        self.s_pv, self.s_recip, self.s_norm = [n.sem(k) for k in ("pv", "recip", "norm")]

    def pe_start(self, pe):
        for s in (self.s_scores, self.s_turned, self.s_pv):
            pe.sem_inc(s, HEAD)

    def dve_start(self, dve):
        for s in (self.s_max, self.s_copied[0], self.s_recip, self.s_norm):
            dve.sem_inc(s, HEAD)

    def act_start(self, act):
        for s in (self.s_exp, self.s_copied[1]):
            act.sem_inc(s, HEAD)

    def wait_scores_bank(self, pe, i, u):
        pe.wait_ge(self.s_exp, done(i * self.per_turn + u - 2))

    def turn(self, pe, m, i, u, keys):
        pe.wait_ge(self.s_exp, done(i * self.per_turn + u))
        pe.wait_ge(self.s_copied[u % 2], done(i * (self.per_turn // 2) + (u // 2 - 1)))
        for k in range(keys):
            last = pe.transpose(self.turned[u % 2][:, k, :], self.probs[:, u % 4, k * P:(k + 1) * P], m.ident[:, :])
        last.then_inc(self.s_turned, 1)

    def times_v(self, pe, i, u, keys, v_of):
        pe.wait_ge(self.s_copied[u % 2], done(i * (self.per_turn // 2) + u // 2))
        if u % QT == 0:
            pe.wait_ge(self.s_norm, done(i * (self.per_turn // QT) + (u // QT - 2)))
        o = self.out[u // QT % 2][:, u % QT * self.vdim:(u % QT + 1) * self.vdim]
        for k in range(keys):
            last = pe.matmul(o, self.probsT[:, u % 4, k, :], v_of(k), start=k == 0, stop=k == keys - 1)
        last.then_inc(self.s_pv, 1)

    def maximum(self, dve, i, u, keys):
        dve.wait_ge(self.s_scores, done(i * self.per_turn + u))
        dve.wait_ge(self.s_exp, done(i * self.per_turn + u - 4))
        dve.tensor_reduce(self.negmax[:, u % 4:u % 4 + 1], self.scores[u % 2][:, 0:keys * P], AX.X, ALU.max,
                          negate=True).then_inc(self.s_max, 1)

    def copy(self, eng, copy, i, u, keys):
        eng.wait_ge(self.s_turned, done(i * self.per_turn + u))
        eng.wait_ge(self.s_pv, done(i * self.per_turn + u - 4))
        copy(self.probsT[:, u % 4, 0:keys, :], self.turned[u % 2][:, 0:keys, :]).then_inc(self.s_copied[u % 2], 1)

    def normalise(self, dve, i, h, out_of):
        o = self.out[h % 2][:, :].rearrange("p (t v) -> p t v", v=self.vdim)
        batch = i * (self.per_turn // QT) + h
        dve.wait_ge(self.s_pv, done(i * self.per_turn + QT * h + QT - 1))
        total = self.sum[:, h % 2, :] if self.sums else o[:, :, self.vdim - 1]
        dve.reciprocal(self.recip[:, h % 2, :], total).then_inc(self.s_recip, 1)
        dve.wait_ge(self.s_recip, done(batch))
        v = self.vdim if self.sums else self.vdim - 1
        return dve.tensor_tensor(out_of, o[:, :, 0:v],
                                 self.recip[:, h % 2, :].unsqueeze(2).broadcast_to([P, QT, v]), ALU.mult)\
            .then_inc(self.s_norm, 1)

    def exponential(self, act, i, u, keys):
        act.wait_ge(self.s_max, done(i * self.per_turn + u))
        act.wait_ge(self.s_turned, done(i * self.per_turn + u - 4))
        if self.sums and u % QT == 0:
            act.wait_ge(self.s_norm, done(i * (self.per_turn // QT) + (u // QT - 2)))
        into = {"accum_out": self.sum[:, u // QT % 2, u % QT:u % QT + 1]} if self.sums else {}
        act.activation(self.probs[:, u % 4, 0:keys * P], self.scores[u % 2][:, 0:keys * P], ACT.Exp,
                       bias=self.negmax[:, u % 4:u % 4 + 1], **into).then_inc(self.s_exp, 1)


def project_block(nc, m, d, prefix, w_name, bias_name):
    with ExitStack() as ctx:
        n = Names(nc, ctx, prefix)
        w = n.sb("w", [P, KT, DIM])
        w_hi, w_lo = n.sb("w_hi", [P, KT, DIM], F32R), n.sb("w_lo", [P, KT, DIM], F32R)
        bias = n.sb("bias", [P, DIM])
        turned = [n.ps(f"turned{i}", [P, KT, P]) for i in range(2)]
        y = [n.ps(f"y{i}", [P, DIM]) for i in range(2)]
        s_load, s_whi, s_wlo, s_turned, s_hi, s_lo, s_bias, s_y, s_x = [
            n.sem(k) for k in ("load", "whi", "wlo", "turned", "hi", "lo", "bias", "y", "x")]
        block = ctx.enter_context(nc.Block())

        @block.sync
        def _(sp):
            sp.dma_start(w[:, :, :], d[w_name].rearrange("(k p) o -> p k o", p=P)).then_inc(s_load, 16)
            sp.dma_start(bias[:, :], d[bias_name].partition_broadcast(P)).then_inc(s_load, 16)

        @block.gpsimd
        def _(pool):
            pool.wait_ge(s_load, 32)
            for t in range(TILES):
                pool.tensor_tensor(m.x[:, t, :], m.x[:, t, :], bias[:, :], ALU.add).then_inc(s_bias, 1)

        @block.scalar
        def _(act):
            act.wait_ge(s_load, 32)
            act.activation(w_hi[:, :, :], w[:, :, :], ACT.Copy).then_inc(s_whi, 1)
            for t in range(TILES):
                act.wait_ge(s_turned, t + 1)
                act.activation(m.xnT_hi[:, :, t * P:(t + 1) * P], turned[t % 2][:, :, :],
                               ACT.Copy).then_inc(s_hi, 1)

        @block.vector
        def _(dve):
            dve.wait_ge(s_whi, 1)
            dve.tensor_tensor(w_lo[:, :, :], w[:, :, :], w_hi[:, :, :].bitcast(F32), ALU.subtract).then_inc(s_wlo, 1)

            def add_y(t):
                dve.wait_ge(s_y, t + 1)
                dve.wait_ge(s_bias, t + 1)
                dve.tensor_tensor(m.x[:, t, :], m.x[:, t, :], y[t % 2][:, :], ALU.add).then_inc(s_x, 1)

            for t in range(TILES):
                dve.wait_ge(s_hi, t + 1)
                dve.tensor_tensor(m.xnT_lo[:, :, t * P:(t + 1) * P], turned[t % 2][:, :, :],
                                  m.xnT_hi[:, :, t * P:(t + 1) * P].bitcast(F32), ALU.subtract).then_inc(s_lo, 1)
                if t >= 1:
                    add_y(t - 1)
            add_y(TILES - 1)

        @block.tensor
        def _(pe):
            def turn(t):
                if t >= 2:
                    pe.wait_ge(s_lo, t - 1)
                for k in range(KT):
                    last = pe.transpose(turned[t % 2][:, k, :], m.tok[:, t, k * P:(k + 1) * P], m.ident[:, :])
                last.then_inc(s_turned, 1)

            turn(0)
            pe.wait_ge(s_wlo, 1)
            for t in range(TILES):
                if t + 1 < TILES:
                    turn(t + 1)
                pe.wait_ge(s_lo, t + 1)
                if t >= 2:
                    pe.wait_ge(s_x, t - 1)
                for k in range(KT):
                    last = mm3(pe, y[t % 2][:, :], pair(m.xnT_hi, m.xnT_lo, slice(None), k, bass.ts(t, P)),
                               pair(w_hi, w_lo, slice(None), k), start=k == 0, stop=k == KT - 1)
                last.then_inc(s_y, 1)


def attn0a_block(nc, m, d, prefix):
    QLAT, KVLAT, HD = 12, 4, 16
    ROWS = 3 * KVLAT
    TURNS, PER = HEADS // 4, 4 * BATCH * QT
    N = BATCH * SEQ
    VW = HD + 1
    with ExitStack() as ctx:
        n = Names(nc, ctx, prefix)
        down = n.sb("down", [P, KT, 2 * P])
        down_hi, down_lo = n.sb("down_hi", [P, KT, 2 * P], F32R), n.sb("down_lo", [P, KT, 2 * P], F32R)
        down_bias = n.sb("down_bias", [P, 2])
        wqk = n.sb("wqk", [QLAT + 1, TURNS * P])
        wqk_hi, wqk_lo = n.sb("wqk_hi", [QLAT + 1, TURNS * P], F32R), n.sb("wqk_lo", [QLAT + 1, TURNS * P], F32R)
        wqk_now_hi, wqk_now_lo = n.sb("wqk_now_hi", [QLAT + 1, P], F32R), n.sb("wqk_now_lo", [QLAT + 1, P], F32R)
        wv = n.sb("wv", [P, DIM])
        wv_hi, wv_lo = n.sb("wv_hi", [P, DIM], F32R), n.sb("wv_lo", [P, DIM], F32R)
        bv = n.sb("bv", [P, DIM])
        row_kind = n.sb("row_kind", [P, 4])
        lat = n.sb("lat", [P, 2, N])
        lat_hi, lat_lo = n.sb("lat_hi", [P, N], F32R), n.sb("lat_lo", [P, N], F32R)
        part_hi = n.sb("part_hi", [P, N], F32R)
        part_sel = n.sb("part_sel", [P, N], F32R)
        part_lo = n.sb("part_lo", [P, N])
        keys = n.sb("keys", [P, N], F32R)
        queries = n.sb("queries", [P, N], F32R)
        v = n.sb("v", [P, TILES, HEADS, VW])
        c = Units(n, PER, VW, sums=False)
        proj = [n.ps(f"proj{i}", [P, SEQ]) for i in range(2)]
        s_load, s_ones, s_hi, s_lo, s_lat, s_latev, s_kmix, s_vps, s_v = [
            n.sem(k) for k in ("load", "ones", "hi", "lo", "lat", "latev", "kmix", "vps", "vready")]
        s_now, s_qps, s_qhi, s_qlo, s_q = [n.sem(k) for k in ("now", "qps", "qhi", "qlo", "q")]
        block = ctx.enter_context(nc.Block())
        LOADS = 6

        @block.sync
        def _(sp):
            for dst, name in ((down[:, :, :], "a0_down"), (down_bias[:, :], "a0_down_bias"), (wqk[:, :], "a0_wqk"),
                              (wv[32:32 + KVLAT, :], "a0_wv"), (row_kind[:, :], "a0_row_kind")):
                src = d[name].rearrange("(k p) o -> p k o", p=P) if name == "a0_down" else d[name]
                sp.dma_start(dst, src).then_inc(s_load, 16)
            sp.dma_start(bv[:, :], d["a0_bv"].partition_broadcast(P)).then_inc(s_load, 16)

        @block.gpsimd
        def _(pool):
            pool.memset(v[:, :, :, HD:VW], 1.0).then_inc(s_ones, 1)
            pool.wait_ge(s_lo, 3)
            pool.sem_inc(s_now, HEAD)
            with pool.Fori(0, TURNS) as i:
                pool.wait_ge(s_qps, 2 * i + HEAD)
                pool.tensor_copy(wqk_now_hi[:, :], wqk_hi[:, bass.ds(i * P, P)].bitcast(F32)).then_inc(s_now, 1)
                pool.tensor_copy(wqk_now_lo[:, :], wqk_lo[:, bass.ds(i * P, P)].bitcast(F32)).then_inc(s_now, 1)

        @block.scalar
        def _(act):
            act.wait_ge(s_load, 16 * LOADS)
            act.activation(down_hi[:, :, :], down[:, :, :], ACT.Copy).then_inc(s_hi, 1)
            act.activation(wqk_hi[:, :], wqk[:, :], ACT.Copy).then_inc(s_hi, 1)
            act.activation(wv_hi[32:32 + KVLAT, :], wv[32:32 + KVLAT, :], ACT.Copy).then_inc(s_hi, 1)
            for g in range(4):
                act.wait_ge(s_lat, g + 1)
                act.activation(lat[:, g // 2, bass.ts(g % 2, SEQ)], proj[g % 2][:, :], ACT.Identity,
                               bias=down_bias[:, g // 2:g // 2 + 1]).then_inc(s_latev, 1)
            act.wait_ge(s_latev, 4)
            act.activation(lat_hi[:, :], lat[:, 1, :], ACT.Copy).then_inc(s_hi, 1)
            act.activation(part_hi[:, :], lat[:, 0, :], ACT.Copy).then_inc(s_hi, 1)
            act.activation(part_sel[:, :], lat[:, 0, :], ACT.Copy, scale=row_kind[:, 0:1]).then_inc(s_hi, 1)
            act.wait_ge(s_kmix, 2)
            c.act_start(act)
            act.sem_inc(s_qhi, HEAD)

            def split_queries(i):
                for b in range(BATCH):
                    act.wait_ge(s_qps, 2 * i + (b + 1 + HEAD))
                    act.wait_ge(s_q, 2 * i + (b - 1 + HEAD))
                    act.activation(part_hi[:, bass.ts(b, SEQ)], proj[b][:, :], ACT.Copy, scale=0.5).then_inc(s_qhi, 1)
                    act.activation(part_sel[:, bass.ts(b, SEQ)], proj[b][:, :], ACT.Copy,
                                   scale=row_kind[:, 2:3]).then_inc(s_qhi, 1)

            def units(i, last):
                for u in range(PER + 2):
                    if u == 8 and not last:
                        split_queries(i + 1)
                    if u < PER:
                        c.exponential(act, i, u, QT)
                    if u >= 2 and u % 2:
                        c.copy(act, lambda o, s: act.activation(o, s, ACT.Copy), i, u - 2, QT)

            split_queries(0)
            with act.Fori(0, TURNS - 1) as i:
                units(i, False)
            units(TURNS - 1, True)

        @block.vector
        def _(dve):
            for g, (lo, full, hi) in enumerate(((down_lo[:, :, :], down[:, :, :], down_hi[:, :, :]),
                                                (wqk_lo[:, :], wqk[:, :], wqk_hi[:, :]),
                                                (wv_lo[32:32 + KVLAT, :], wv[32:32 + KVLAT, :],
                                                 wv_hi[32:32 + KVLAT, :]))):
                dve.wait_ge(s_hi, g + 1)
                dve.tensor_tensor(lo, full, hi.bitcast(F32), ALU.subtract).then_inc(s_lo, 1)
            dve.wait_ge(s_hi, 4)
            dve.tensor_tensor(lat_lo[:, :], lat[:, 1, :], lat_hi[:, :].bitcast(F32), ALU.subtract).then_inc(s_lo, 1)
            dve.wait_ge(s_hi, 5)
            dve.tensor_tensor(part_lo[:, :], lat[:, 0, :], part_hi[:, :].bitcast(F32),
                              ALU.subtract).then_inc(s_kmix, 1)
            dve.wait_ge(s_kmix, 1)
            dve.wait_ge(s_hi, 6)
            dve.scalar_tensor_tensor(keys[:, :], part_lo[:, :], row_kind[:, 1:2], part_sel[:, :].bitcast(F32),
                                     ALU.mult, ALU.add).then_inc(s_kmix, 1)
            dve.wait_ge(s_ones, 1)
            for t in range(TILES):
                dve.wait_ge(s_vps, t + 1)
                dve.tensor_tensor(v[:, t, :, 0:HD], proj[t % 2][:, :].rearrange("p (h e) -> p h e", e=HD),
                                  bv[:, :].rearrange("p (h e) -> p h e", e=HD), ALU.add).then_inc(s_v, 1)
            dve.wait_ge(s_kmix, 2)
            c.dve_start(dve)
            dve.sem_inc(s_qlo, HEAD)
            dve.sem_inc(s_q, HEAD)

            def split_queries(i):
                for b in range(BATCH):
                    dve.wait_ge(s_qhi, 4 * i + (2 * b + 2 + HEAD))
                    dve.wait_ge(s_q, 2 * i + (b - 1 + HEAD))
                    dve.scalar_tensor_tensor(part_lo[:, bass.ts(b, SEQ)], proj[b][:, :], 0.5,
                                             part_hi[:, bass.ts(b, SEQ)].bitcast(F32),
                                             ALU.mult, ALU.subtract).then_inc(s_qlo, 1)

            def mix_queries(i):
                for b in range(BATCH):
                    dve.wait_ge(s_qlo, 2 * i + (b + 1 + HEAD))
                    dve.scalar_tensor_tensor(queries[:, bass.ts(b, SEQ)], part_lo[:, bass.ts(b, SEQ)],
                                             row_kind[:, 3:4], part_sel[:, bass.ts(b, SEQ)].bitcast(F32),
                                             ALU.mult, ALU.add).then_inc(s_q, 1)

            def store(i, h):
                j, b = divmod(h, BATCH)
                c.normalise(dve, i, h, m.tok[:, b * QT:(b + 1) * QT, bass.ds(i * (4 * HD) + j * HD, HD)])

            def units(i, last):
                for u in range(PER + 4):
                    if u == 9 and not last:
                        split_queries(i + 1)
                    if u < PER:
                        c.maximum(dve, i, u, QT)
                    if u == PER and not last:
                        mix_queries(i + 1)
                    if 2 <= u < PER + 2 and u % 2 == 0:
                        c.copy(dve, dve.tensor_copy, i, u - 2, QT)
                    if u >= QT + 3 and (u - QT - 3) % QT == 0:
                        store(i, (u - QT - 3) // QT)

            split_queries(0)
            mix_queries(0)
            with dve.Fori(0, TURNS - 1) as i:
                units(i, False)
            units(TURNS - 1, True)

        @block.tensor
        def _(pe):
            pe.wait_ge(s_lo, 1)
            for g in range(4):
                if g >= 2:
                    pe.wait_ge(s_latev, g - 1)
                for k in range(KT):
                    last = mm3(pe, proj[g % 2][:, :], pair(down_hi, down_lo, slice(None), k, bass.ts(g // 2, P)),
                               pair(m.xnT_hi, m.xnT_lo, slice(None), k, bass.ts(g % 2, SEQ)),
                               start=k == 0, stop=k == KT - 1)
                last.then_inc(s_lat, 1)
            pe.wait_ge(s_lo, 4)
            pe.wait_ge(s_latev, 4)
            for t in range(TILES):
                if t >= 2:
                    pe.wait_ge(s_v, t - 1)
                mm3(pe, proj[t % 2][:, :], pair(lat_hi, lat_lo, slice(32, 32 + KVLAT), bass.ts(t, P)),
                    pair(wv_hi, wv_lo, slice(32, 32 + KVLAT)), start=True, stop=True).then_inc(s_vps, 1)
            pe.wait_ge(s_v, TILES)
            c.pe_start(pe)
            pe.sem_inc(s_qps, HEAD)

            def project_queries(i):
                pe.wait_ge(s_now, 2 * i + (2 + HEAD))
                for b in range(BATCH):
                    pe.wait_ge(s_q, 2 * i + (b - 1 + HEAD))
                    mm3(pe, proj[b][:, :], (wqk_now_hi[:, :], wqk_now_lo[:, :]),
                        pair(lat_hi, lat_lo, slice(0, QLAT + 1), bass.ts(b, SEQ)), start=True, stop=True)\
                        .then_inc(s_qps, 1)

            def units(i, last):
                for u in range(PER + 3):
                    if u == 6 and not last:
                        project_queries(i + 1)
                    if u < PER:
                        j, r = divmod(u, BATCH * QT)
                        rows = slice(32 * j, 32 * j + ROWS)
                        c.wait_scores_bank(pe, i, u)
                        if u == 0:
                            pe.wait_ge(s_q, 2 * i + (2 + HEAD))
                        pe.matmul(c.scores[u % 2][:, :], queries[rows, bass.ts(r, P)],
                                  keys[rows, bass.ts(r // QT, SEQ)], start=True, stop=True).then_inc(c.s_scores, 1)
                    if 2 <= u < PER + 2:
                        c.turn(pe, m, i, u - 2, QT)
                    if u >= 3:
                        j, r = divmod(u - 3, BATCH * QT)
                        c.times_v(pe, i, u - 3, QT, lambda k: v[:, r // QT * QT + k, :, :].rearrange(
                            "p h e -> p (h e)")[:, bass.ds(i * (4 * VW) + j * VW, VW)])

            project_queries(0)
            with pe.Fori(0, TURNS - 1) as i:
                units(i, False)
            units(TURNS - 1, True)


class CausalUnits:
    def __init__(self, n, per_turn, fills, together, vdim):
        self.per_turn, self.fills, self.together, self.vdim = per_turn, fills, together, vdim
        self.SLOTS = 4 if together == 1 else 8
        self.scores = [n.ps(f"scores{i}", [P, SEQ]) for i in range(2)]
        self.turned = [n.ps(f"probsT_ps{i}", [P, QT, P]) for i in range(2)]
        self.out = [n.ps(f"out{i}", [P, QT, P]) for i in range(2)]
        self.negmax = n.sb("negmax", [P, 4])
        self.sum, self.recip = n.sb("sum", [P, 4]), n.sb("recip", [P, 4])
        self.probs = n.sb("probs", [P, 4, SEQ])
        self.probsT = n.sb("probsT", [P, self.SLOTS, QT, P])
        self.s_scores, self.s_max, self.s_exp, self.s_recip, self.s_scaled, self.s_turned = [
            n.sem(k) for k in ("scores", "max", "exp", "recip", "scaled", "turned")]
        self.s_copied = [n.sem("copied_even"), n.sem("copied_odd")]
        self.s_pv, self.s_fill, self.s_hi, self.s_lo = [n.sem(k) for k in ("pv", "fill", "outhi", "outlo")]

    def pe_start(self, pe):
        for s in (self.s_scores, self.s_turned, self.s_pv, self.s_fill):
            pe.sem_inc(s, HEAD)

    def dve_start(self, dve):
        for s in (self.s_max, self.s_recip, self.s_scaled, self.s_copied[0], self.s_lo):
            dve.sem_inc(s, HEAD)

    def act_start(self, act):
        for s in (self.s_exp, self.s_copied[1], self.s_hi):
            act.sem_inc(s, HEAD)

    def score(self, pe, m, i, u, qt, q, k_of, mask, mask_by):
        pe.wait_ge(self.s_exp, done(i * self.per_turn + u - 2))
        width = (qt + 1) * P
        s, k = self.scores[u % 2][:, 0:width], k_of(width)
        pe.matmul(s, q[0], k[0], start=True, stop=False)
        pe.matmul(s[:, qt * P:width], mask_by, mask, start=False, stop=False)
        if q[1] is not None:
            pe.matmul(s, q[1], k[0], start=False, stop=False)
        pe.matmul(s, q[0], k[1], start=False, stop=True).then_inc(self.s_scores, 1)

    def turn(self, pe, m, i, u, qt):
        pe.wait_ge(self.s_scaled, done(i * self.per_turn + u))
        pe.wait_ge(self.s_copied[u % 2], done(i * (self.per_turn // 2) + (u // 2 - 1)))
        for k in range(qt + 1):
            last = pe.transpose(self.turned[u % 2][:, k, :], self.probs[:, u % 4, k * P:(k + 1) * P], m.ident[:, :])
        last.then_inc(self.s_turned, 1)

    def times_v(self, pe, i, u, qt, fill, v_of):
        g = self.together
        for w in range(max(0, u - 1), u + 1) if g > 1 else (u,):
            pe.wait_ge(self.s_copied[w % 2], done(i * (self.per_turn // 2) + w // 2))
        bank = self.out[fill % 2]
        if qt == 0:
            pe.wait_ge(self.s_lo, done(i * self.fills + fill - 2))
        for k in range(qt + 1):
            for e in range(g):
                w = u - g + 1 + e
                last = pe.matmul(bank[e * self.vdim:(e + 1) * self.vdim, qt, :], v_of(e, k),
                                 self.probsT[:, w % self.SLOTS, k, :], start=k == 0, stop=k == qt)
        last.then_inc(self.s_fill if qt == QT - 1 else self.s_pv, 1)

    def maximum(self, dve, i, u, qt):
        dve.wait_ge(self.s_scores, done(i * self.per_turn + u))
        dve.wait_ge(self.s_exp, done(i * self.per_turn + u - 4))
        dve.tensor_reduce(self.negmax[:, u % 4:u % 4 + 1], self.scores[u % 2][:, 0:(qt + 1) * P], AX.X, ALU.max,
                          negate=True).then_inc(self.s_max, 1)

    def scale(self, dve, i, u, qt):
        dve.wait_ge(self.s_exp, done(i * self.per_turn + u))
        dve.reciprocal(self.recip[:, u % 4:u % 4 + 1], self.sum[:, u % 4:u % 4 + 1]).then_inc(self.s_recip, 1)
        dve.wait_ge(self.s_recip, done(i * self.per_turn + u))
        p = self.probs[:, u % 4, 0:(qt + 1) * P]
        dve.tensor_scalar(p, p, self.recip[:, u % 4:u % 4 + 1], None, ALU.mult).then_inc(self.s_scaled, 1)

    def copy(self, eng, copy, i, u, qt, wait_slot):
        eng.wait_ge(self.s_turned, done(i * self.per_turn + u))
        wait_slot(eng)
        copy(self.probsT[:, u % self.SLOTS, 0:qt + 1, :],
             self.turned[u % 2][:, 0:qt + 1, :]).then_inc(self.s_copied[u % 2], 1)

    def lo(self, dve, i, fill, into_lo, into_hi, full):
        dve.wait_ge(self.s_hi, done(i * self.fills + fill))
        dve.tensor_tensor(into_lo, full, into_hi.bitcast(F32), ALU.subtract).then_inc(self.s_lo, 1)

    def exponential(self, act, i, u, qt):
        act.wait_ge(self.s_max, done(i * self.per_turn + u))
        act.wait_ge(self.s_turned, done(i * self.per_turn + u - 4))
        act.activation(self.probs[:, u % 4, 0:(qt + 1) * P], self.scores[u % 2][:, 0:(qt + 1) * P], ACT.Exp,
                       bias=self.negmax[:, u % 4:u % 4 + 1],
                       accum_out=self.sum[:, u % 4:u % 4 + 1]).then_inc(self.s_exp, 1)

    def hi(self, act, i, fill, into_hi, full):
        act.wait_ge(self.s_fill, done(i * self.fills + fill))
        act.activation(into_hi, full, ACT.Copy).then_inc(self.s_hi, 1)


def attn0b_block(nc, m, d, prefix):
    G = HEADS // 8
    HD, ROT = 128, 64
    KV = 2 * HD
    UP = KV - ROT
    TURNS, PER = 8, BATCH * G * QT
    STEPS = [("W", k) for k in range(KT)] + [("B", t) for t in range(6)] + [("K", 0), ("B", 6), ("B", 7)]
    STEPS += [("C", 0), ("C", 1), ("K", 1)]
    for t in range(2, TILES):
        STEPS += [("C", t), ("Q", t - 2)]
    STEPS += [("Q", TILES - 2), ("Q", TILES - 1)]
    PROJ = {s: n for n, s in enumerate([s for s in STEPS if s[0] in "WBC"] + [("E", t) for t in range(TILES)])}
    order = sorted(PROJ, key=PROJ.get)
    ROTATED = {s: n for n, s in enumerate([s for s in order if s[0] in "BC"])}
    FREES = {s: n for n, s in enumerate([s for s in order if s[0] in "WE"])}
    FILL = {s: n for n, s in enumerate([s for s in STEPS if s[0] in "KQ"] + [("O", h) for h in range(BATCH * G)])}
    units = [(b, j, qt) for b in range(BATCH) for j in range(G) for qt in range(QT)]
    with ExitStack() as ctx:
        n = Names(nc, ctx, prefix)
        down = n.sb("down", [P, KT, DIM])
        down_hi, down_lo = n.sb("down_hi", [P, KT, DIM], F32R), n.sb("down_lo", [P, KT, DIM], F32R)
        up_in, rot_in = n.sb("up_in", [P, KT, UP]), n.sb("rot_in", [P, KT, ROT])
        big_in = down
        up_hi, up_lo = n.sb("up_hi", [P, KT, UP], F32R), n.sb("up_lo", [P, KT, UP], F32R)
        wkv_hi, wkv_lo = n.sb("wkv_hi", [P, KT, KV], F32R), n.sb("wkv_lo", [P, KT, KV], F32R)
        wq_hi, wq_lo = n.sb("wq_hi", [P, KT, DIM], F32R), n.sb("wq_lo", [P, KT, DIM], F32R)
        wo_hi, wo_lo = n.sb("wo_hi", [P, G, DIM], F32R), n.sb("wo_lo", [P, G, DIM], F32R)
        cos_q, sin_q = n.sb("cos_q", [P, QT, HD]), n.sb("sin_q", [P, QT, HD])
        cos_k, sin_k = n.sb("cos_k", [P, QT, ROT]), n.sb("sin_k", [P, QT, ROT])
        part_a, part_b = n.sb("part_a", [P, 2, DIM]), n.sb("part_b", [P, 2, DIM])
        kv_tok = n.sb("kv_tok", [P, TILES, KV])
        q_tok = n.sb("q_tok", [P, 2, DIM])
        kT_hi, kT_lo = n.sb("kT_hi", [P, TILES * P], F32R), n.sb("kT_lo", [P, TILES * P], F32R)
        qT_hi, qT_lo = n.sb("qT_hi", [P, G, TILES * P], F32R), n.sb("qT_lo", [P, G, TILES * P], F32R)
        oT_hi, oT_lo = qT_hi, qT_lo
        c = CausalUnits(n, PER, len(FILL), 1, HD)
        proj = [n.ps(f"proj{i}", [P, DIM]) for i in range(2)]
        s_down, s_tables, s_small, s_big, s_dhi, s_dlo = [
            n.sem(k) for k in ("down", "tables", "small_in", "big_in", "down_hi", "down_lo")]
        s_shi, s_slo, s_bhi, s_blo = [n.sem(k) for k in ("small_hi", "small_lo", "big_hi", "big_lo")]
        s_proj, s_projfree, s_projhi, s_rope, s_added = [
            n.sem(k) for k in ("proj", "projfree", "projhi", "rope", "added")]
        block = ctx.enter_context(nc.Block())
        NP = len(PROJ)

        @block.sync
        def _(sp):
            sp.dma_start(down[:, :, :], d["b0_down"].rearrange("(k p) o -> p k o", p=P)).then_inc(s_down, 16)
            for dst, name in ((cos_q, "b0_cos_q"), (sin_q, "b0_sin_q"), (cos_k, "b0_cos_k"), (sin_k, "b0_sin_k")):
                sp.dma_start(dst[:, :, :], d[name]).then_inc(s_tables, 16)

            def load(dst, src, i, s):
                sp.dma_start(dst[:, :, :], src[bass.ds(i, 1)].rearrange("g (k p) o -> p (g k) o", p=P)).then_inc(s, 16)

            with sp.Fori(0, TURNS) as i:
                sp.wait_ge(s_slo, 2 * i + 1)
                load(rot_in, d["b0_rot"], i, s_small)
                load(up_in, d["b0_up"], i, s_small)
                sp.wait_ge(s_dlo, 1)
                sp.wait_ge(s_blo, 2 * i + 1)
                load(big_in, d["b0_q"], i, s_big)
                sp.wait_ge(s_blo, 2 * i + 2)
                load(big_in, d["b0_o"], i, s_big)

        def split_small_hi(act, i):
            act.wait_ge(s_small, 32 * i + 32)
            act.activation(wkv_hi[:, :, 0:ROT], rot_in[:, :, :], ACT.Copy).then_inc(s_shi, 1)
            act.activation(up_hi[:, :, :], up_in[:, :, :], ACT.Copy).then_inc(s_shi, 1)

        def split_small_lo(pool, i):
            pool.wait_ge(s_shi, 2 * i + 2)
            pool.tensor_tensor(wkv_lo[:, :, 0:ROT], rot_in[:, :, :], wkv_hi[:, :, 0:ROT].bitcast(F32),
                               ALU.subtract).then_inc(s_slo, 1)
            pool.tensor_tensor(up_lo[:, :, :], up_in[:, :, :], up_hi[:, :, :].bitcast(F32),
                               ALU.subtract).then_inc(s_slo, 1)

        @block.gpsimd
        def _(pool):
            pool.sem_inc(s_added, HEAD)
            pool.sem_inc(s_slo, 1)
            pool.sem_inc(s_blo, 1)

            def prepare(i):
                for kind, t in STEPS:
                    if kind in "BC":
                        pool.wait_ge(s_rope, i * (3 * len(ROTATED)) + 3 * (ROTATED[kind, t] + 1))
                        if kind == "B":
                            pool.tensor_tensor(kv_tok[:, t, 0:ROT], part_a[:, t % 2, 0:ROT], part_b[:, t % 2, 0:ROT],
                                               ALU.add).then_inc(s_added, 1)
                        else:
                            pool.wait_ge(c.s_fill, done(i * c.fills + FILL["Q", 0] + t - 2))
                            pool.tensor_tensor(q_tok[:, t % 2, :], part_a[:, t % 2, :], part_b[:, t % 2, :],
                                               ALU.add).then_inc(s_added, 1)

            def split_big_lo(i, which, hi, lo):
                pool.wait_ge(s_bhi, 2 * i + (which + 1))
                pool.tensor_tensor(lo[:, :, :], big_in[:, :, :], hi[:, :, :].bitcast(F32),
                                   ALU.subtract).then_inc(s_blo, 1)

            def turn(i, last):
                prepare(i)
                split_big_lo(i, 1, wo_hi, wo_lo)
                if not last:
                    split_small_lo(pool, i + 1)
                    split_big_lo(i + 1, 0, wq_hi, wq_lo)

            split_small_lo(pool, 0)
            split_big_lo(0, 0, wq_hi, wq_lo)
            with pool.Fori(0, TURNS - 1) as i:
                turn(i, False)
            turn(TURNS - 1, True)

        def slot_free(eng, i, u):
            w = u - c.SLOTS
            q = PER // QT
            batch, r = divmod(w, QT)
            if r == QT - 1:
                last_fill = FILL["O", batch] if batch >= 0 else FILL["O", q + batch] - c.fills
                eng.wait_ge(c.s_fill, done(i * c.fills + last_fill))
            else:
                eng.wait_ge(c.s_pv, i * (q * (QT - 1)) + (batch * (QT - 1) + r + 1 + HEAD))

        def output(eng, i, h, high):
            b, j = divmod(h, G)
            f = FILL["O", h]
            view = lambda x: x[:, j, bass.ts(b, SEQ)].rearrange("p (t q) -> p t q", q=P)
            if high:
                c.hi(eng, i, f, view(oT_hi), c.out[f % 2][:, :, :])
            else:
                c.lo(eng, i, f, view(oT_lo), view(oT_hi), c.out[f % 2][:, :, :])

        @block.scalar
        def _(act):
            def split_big_hi(i, which, hi):
                act.wait_ge(s_big, 32 * i + 16 * (which + 1))
                act.activation(hi[:, :, :], big_in[:, :, :], ACT.Copy).then_inc(s_bhi, 1)

            def prepare(i):
                for kind, t in STEPS:
                    if kind == "W":
                        act.wait_ge(s_proj, i * NP + (PROJ[kind, t] + 1))
                        act.activation(wkv_hi[:, t, ROT:KV], proj[t % 2][:, 0:UP], ACT.Copy).then_inc(s_projhi, 1)
                    elif kind == "B":
                        act.wait_ge(s_proj, i * NP + (PROJ[kind, t] + 1))
                        act.activation(kv_tok[:, t, ROT:KV], proj[t % 2][:, ROT:KV], ACT.Copy).then_inc(s_projhi, 1)
                    elif kind == "K":
                        c.hi(act, i, FILL[kind, t], kT_hi[:, bass.ts(t, SEQ)].rearrange("p (t q) -> p t q", q=P),
                             c.out[FILL[kind, t] % 2][:, :, :])
                    elif kind == "Q":
                        c.hi(act, i, FILL[kind, t], qT_hi[:, :, bass.ts(t, P)], c.out[FILL[kind, t] % 2][:, :, :])

            def turn(i, last):
                prepare(i)
                for s in range(PER + 5):
                    if s < PER:
                        c.exponential(act, i, s, units[s][2])
                    if s == 4:
                        act.wait_ge(s_projfree, done(i * len(FREES) - 1))
                        split_big_hi(i, 1, wo_hi)
                    if s == 12 and not last:
                        split_small_hi(act, i + 1)
                    if s == 16 and not last:
                        split_big_hi(i + 1, 0, wq_hi)
                    if 3 <= s < PER + 3 and (s - 3) % 2:
                        c.copy(act, lambda o, x: act.activation(o, x, ACT.Copy), i, s - 3, units[s - 3][2],
                               lambda e: slot_free(e, i, s - 3))
                    if s >= 8 and s % QT == 0:
                        output(act, i, s // QT - 2, True)

            act.wait_ge(s_down, 16)
            act.activation(down_hi[:, :, :], down[:, :, :], ACT.Copy).then_inc(s_dhi, 1)
            split_small_hi(act, 0)
            split_big_hi(0, 0, wq_hi)
            c.act_start(act)
            with act.Fori(0, TURNS - 1) as i:
                turn(i, False)
            turn(TURNS - 1, True)

        @block.vector
        def _(dve):
            dve.wait_ge(s_dhi, 1)
            dve.tensor_tensor(down_lo[:, :, :], down[:, :, :], down_hi[:, :, :].bitcast(F32),
                              ALU.subtract).then_inc(s_dlo, 1)
            dve.wait_ge(s_tables, 64)
            c.dve_start(dve)
            dve.sem_inc(s_projfree, HEAD)

            def rotate(i, kind, t, heads, width, cos, sin):
                n_rot = ROTATED[kind, t]
                if kind == "B":
                    dve.wait_ge(s_projhi, i * (KT + TILES) + (KT + t + 1))
                dve.wait_ge(s_added, done(i * len(ROTATED) + n_rot - 2))
                flat = lambda x: x[:, 0:heads * width].rearrange("p (g x) -> p g x", g=heads)
                x, a, b = proj[t % 2], part_a[:, t % 2, :], part_b[:, t % 2, :]
                dve.tensor_tensor(flat(a), flat(x), cos[:, t % QT, :].unsqueeze(1).broadcast_to([P, heads, width]),
                                  ALU.mult).then_inc(s_rope, 1)
                half = lambda y, h: y[:, 0:heads * width].rearrange("p (g r h x) -> p g r h x", g=heads, h=2,
                                                                    x=32)[:, :, :, h, :]
                runs = width // 64
                for h in range(2):
                    table = sin[:, t % QT, :].rearrange("p (r h x) -> p r h x", h=2, x=32)[:, :, h, :]
                    dve.tensor_tensor(half(b, h), half(x, 1 - h),
                                      table.unsqueeze(1).broadcast_to([P, heads, runs, 32]),
                                      ALU.mult).then_inc(s_rope, 1)

            def prepare(i):
                for kind, t in STEPS:
                    if kind in "WBC":
                        dve.wait_ge(s_proj, i * NP + (PROJ[kind, t] + 1))
                    if kind == "W":
                        dve.wait_ge(s_projhi, i * (KT + TILES) + (t + 1))
                        dve.tensor_tensor(wkv_lo[:, t, ROT:KV], proj[t % 2][:, 0:UP],
                                          wkv_hi[:, t, ROT:KV].bitcast(F32), ALU.subtract).then_inc(s_projfree, 1)
                    elif kind == "B":
                        rotate(i, kind, t, 1, ROT, cos_k, sin_k)
                    elif kind == "C":
                        rotate(i, kind, t, G, HD, cos_q, sin_q)
                    elif kind == "K":
                        view = lambda x: x[:, bass.ts(t, SEQ)].rearrange("p (t q) -> p t q", q=P)
                        c.lo(dve, i, FILL[kind, t], view(kT_lo), view(kT_hi), c.out[FILL[kind, t] % 2][:, :, :])
                    elif kind == "Q":
                        c.lo(dve, i, FILL[kind, t], qT_lo[:, :, bass.ts(t, P)], qT_hi[:, :, bass.ts(t, P)],
                             c.out[FILL[kind, t] % 2][:, :, :])

            def add_output(i, t):
                f = PROJ["E", t]
                dve.wait_ge(s_proj, i * NP + (f + 1))
                dve.tensor_tensor(m.x[:, t, :], m.x[:, t, :], proj[f % 2][:, :], ALU.add).then_inc(s_projfree, 1)

            def turn(i):
                prepare(i)
                for s in range(PER + 5):
                    if s < PER:
                        c.maximum(dve, i, s, units[s][2])
                    if 1 <= s < PER + 1:
                        c.scale(dve, i, s - 1, units[s - 1][2])
                    if 3 <= s < PER + 3 and (s - 3) % 2 == 0:
                        c.copy(dve, dve.tensor_copy, i, s - 3, units[s - 3][2], lambda e: slot_free(e, i, s - 3))
                    if s >= 8 and s % QT == 0:
                        output(dve, i, s // QT - 2, False)
                    if s >= 27 and s % 3 == 0 and (s - 27) // 3 < QT - 1:
                        add_output(i, (s - 27) // 3)
                for t in range(QT - 1, TILES):
                    add_output(i, t)

            with dve.Fori(0, TURNS) as i:
                turn(i)

        @block.tensor
        def _(pe):
            pe.wait_ge(s_dlo, 1)
            c.pe_start(pe)

            def project(i, kind, t, width, lhs, rhs, n_k):
                f = PROJ[kind, t]
                projection_taken(i, f - 2)
                for k in range(n_k):
                    last = mm3(pe, proj[f % 2][:, 0:width], lhs(k), rhs(k), start=k == 0, stop=k == n_k - 1)
                last.then_inc(s_proj, 1)

            def projection_taken(i, f):
                back = 1 if f < 0 else 0
                kind, t = order[f % NP]
                if kind in "WE":
                    pe.wait_ge(s_projfree, done(i * len(FREES) + (FREES[kind, t] - back * len(FREES))))
                else:
                    pe.wait_ge(s_rope, i * (3 * len(ROTATED)) + 3 * (ROTATED[kind, t] + 1))

            def prepare(i):
                for kind, t in STEPS:
                    if kind == "W":
                        if t == 0:
                            pe.wait_ge(s_slo, 2 * i + 3)
                        project(i, kind, t, UP, lambda k: pair(down_hi, down_lo, slice(None), k, bass.ts(t, P)),
                                lambda k: pair(up_hi, up_lo, slice(None), k), KT)
                    elif kind == "B":
                        if t == 0:
                            pe.wait_ge(s_projfree, done(i * len(FREES) + FREES["W", KT - 1]))
                        project(i, kind, t, KV, lambda k: pair(m.xnT_hi, m.xnT_lo, slice(None), k, bass.ts(t, P)),
                                lambda k: pair(wkv_hi, wkv_lo, slice(None), k), KT)
                    elif kind == "C":
                        if t == 0:
                            pe.wait_ge(s_blo, 2 * i + 2)
                        project(i, kind, t, DIM, lambda k: pair(m.xnT_hi, m.xnT_lo, slice(None), k, bass.ts(t, P)),
                                lambda k: pair(wq_hi, wq_lo, slice(None), k), KT)
                    else:
                        f = FILL[kind, t]
                        pe.wait_ge(c.s_lo, done(i * c.fills + f - 2))
                        if kind == "K":
                            pe.wait_ge(s_added, done(i * (2 * TILES) + (QT * t + QT - 1)))
                            pe.wait_ge(s_projhi, i * (KT + TILES) + (KT + QT * t + QT))
                            for r in range(QT):
                                last = pe.transpose(c.out[f % 2][:, r, :], kv_tok[:, QT * t + r, 0:HD], m.ident[:, :])
                        else:
                            pe.wait_ge(s_added, done(i * (2 * TILES) + (TILES + t)))
                            for r in range(G):
                                last = pe.transpose(c.out[f % 2][:, r, :], q_tok[:, t % 2, r * HD:(r + 1) * HD],
                                                    m.ident[:, :])
                        last.then_inc(c.s_fill, 1)

            def project_output(i, t):
                if t == 0:
                    pe.wait_ge(s_blo, 2 * i + 3)
                if t % QT == 0:
                    pe.wait_ge(c.s_lo, done(i * c.fills + FILL["O", G * (t // QT) + G - 1]))
                project(i, "E", t, DIM, lambda j: pair(oT_hi, oT_lo, slice(None), j, bass.ts(t, P)),
                        lambda j: pair(wo_hi, wo_lo, slice(None), j), G)

            def turn(i):
                prepare(i)
                for s in range(PER + 4):
                    if s < PER:
                        b, j, qt = units[s]
                        if s == 0:
                            pe.wait_ge(c.s_lo, done(i * c.fills + FILL["Q", TILES - 1]))
                        c.score(pe, m, i, s, qt,
                                pair(qT_hi, qT_lo, slice(None), j, bass.ts(b * QT + qt, P)),
                                lambda w: pair(kT_hi, kT_lo, slice(None), bass.ds(b * SEQ, w)),
                                m.mask[:, 0, :], m.ident16[:, :])
                    if 2 <= s < PER + 2:
                        c.turn(pe, m, i, s - 2, units[s - 2][2])
                    if s >= 4:
                        b, j, qt = units[s - 4]
                        c.times_v(pe, i, s - 4, qt, FILL["O", b * G + j],
                                  lambda e, k: kv_tok[:, b * QT + k, HD:KV])
                    if s >= 26 and (s - 26) % 3 == 0 and (s - 26) // 3 < QT - 1:
                        project_output(i, (s - 26) // 3)
                for t in range(QT - 1, TILES):
                    project_output(i, t)

            with pe.Fori(0, TURNS) as i:
                turn(i)


def attn1a_block(nc, m, d, prefix):
    G, TURNS = 4, HEADS // 4
    QLORA, LAT, ROT, HD = 192, 64, 64, 128
    Q2 = QLORA - P
    NA = QLORA + LAT + ROT
    RMS_EPS = 1e-6
    PER = BATCH * G * QT
    STEPS = [("W", 0), ("W", 1), ("C", 0), ("C", 1)]
    for t in range(2, TILES):
        STEPS += [("C", t), ("Q", t - 2)] + ([("G", t - 3)] if t in (3, 4) else [])
    STEPS += [("Q", TILES - 2), ("Q", TILES - 1)]
    PROJ = {s: n for n, s in enumerate([s for s in STEPS if s[0] != "Q"] + [("E", t) for t in range(TILES)])}
    order = sorted(PROJ, key=PROJ.get)
    ACTS = {s: n for n, s in enumerate([s for s in order if s[0] in "WCG"])}
    FREES = {s: n for n, s in enumerate([s for s in order if s[0] in "WGE"])}
    FILL = {s: n for n, s in enumerate([("Q", t) for t in range(TILES)] + [("O", h) for h in range(BATCH * 2)])}
    NP = len(PROJ)
    units = [(b, 2 * pr + e, qt) for b in range(BATCH) for pr in range(2) for qt in range(QT) for e in range(2)]
    SCALE = float(1.0 / np.sqrt(np.float32(HD + ROT)))
    with ExitStack() as ctx:
        n = Names(nc, ctx, prefix)
        wa = n.sb("wa", [P, KT, NA])
        wa_hi, wa_lo = n.sb("wa_hi", [P, KT, NA], F32R), n.sb("wa_lo", [P, KT, NA], F32R)
        q_norm, kv_norm = n.sb("q_norm", [P, 2]), n.sb("kv_norm", [P, LAT])
        cos_q, sin_q = n.sb("cos_q", [P, QT, ROT]), n.sb("sin_q", [P, QT, ROT])
        cos_k, sin_k = n.sb("cos_k", [P, QT, ROT]), n.sb("sin_k", [P, QT, ROT])
        lat_tok = n.sb("lat_tok", [P, TILES, NA])
        squares = n.sb("squares", [P, 2, QLORA])
        sumsq, meansq = n.sb("sumsq", [P, 2, TILES]), n.sb("meansq", [P, 2, TILES])
        rms, rrms = n.sb("rms", [P, 2, TILES]), n.sb("rrms", [P, 2, TILES])
        wn_in, wk_in = n.sb("wn_in", [P, G, QLORA]), n.sb("wk_in", [P, G, LAT])
        wr_in = n.sb("wr_in", [P, 2, G, ROT])
        wv_in, wo_in = n.sb("wv_in", [P, G, LAT]), n.sb("wo_in", [P, G, DIM])
        wq_hi, wq_lo = n.sb("wq_hi", [P, 2, G, HD], F32R), n.sb("wq_lo", [P, 2, G, HD], F32R)
        wo_hi, wo_lo = n.sb("wo_hi", [P, 2, DIM], F32R), n.sb("wo_lo", [P, 2, DIM], F32R)
        part_a, part_b = n.sb("part_a", [P, 2, G * ROT]), n.sb("part_b", [P, 2, G * ROT])
        q_tok = n.sb("q_tok", [P, 2, G, HD])
        qT_hi, qT_lo = n.sb("qT_hi", [P, G, TILES * P], F32R), n.sb("qT_lo", [P, G, TILES * P], F32R)
        c = CausalUnits(n, PER, len(FILL), 2, LAT)
        proj = [n.ps(f"proj{i}", [P, DIM]) for i in range(2)]
        latT_hi, latT_lo = m.xnT_hi, m.xnT_lo
        s_wa, s_tables, s_wahi, s_walo, s_a, s_acopy, s_sq, s_ms, s_rms, s_rrms, s_ln, s_krot, s_kadd, s_lat, s_lhi, \
            s_llo = [n.sem(k) for k in ("wa", "tables", "wahi", "walo", "a", "acopy", "sq", "ms", "rms", "rrms",
                                        "ln", "krot", "kadd", "lat", "lhi", "llo")]
        s_in, s_rhi, s_rlo, s_proj, s_projhi, s_free, s_rope, s_added = [
            n.sem(k) for k in ("in", "rhi", "rlo", "proj", "projhi", "free", "rope", "added")]
        block = ctx.enter_context(nc.Block())
        IN = 6

        def half(y, heads, h):
            return y.rearrange("p (g h x) -> p g h x", g=heads, h=2)[:, :, h, :]

        @block.sync
        def _(sp):
            sp.dma_start(wa[:, :, :], d["b1_down"].rearrange("(k p) o -> p k o", p=P)).then_inc(s_wa, 16)
            for dst, name in ((cos_q, "b1_cos_q"), (sin_q, "b1_sin_q"), (cos_k, "b1_cos_k"), (sin_k, "b1_sin_k")):
                sp.dma_start(dst[:, :, :], d[name]).then_inc(s_tables, 16)
            sp.dma_start(q_norm[:, :], d["b1_q_norm"]).then_inc(s_tables, 16)
            sp.dma_start(kv_norm[:, :], d["b1_kv_norm"].partition_broadcast(P)).then_inc(s_tables, 16)
            with sp.Fori(0, TURNS) as i:
                sp.wait_ge(s_free, done(i * len(FREES) + FREES["G", 1] - len(FREES)))
                sp.wait_ge(s_rlo, 2 * i + 1)
                one = bass.ds(i, 1)
                for dst, name in ((wn_in, "b1_qn"), (wk_in, "b1_k"), (wv_in, "b1_v"), (wo_in, "b1_o")):
                    sp.dma_start(dst[:, :, :], d[name][one].rearrange("g p j o -> p (g j) o")).then_inc(s_in, 16)
                sp.dma_start(wr_in[:, 0, :, :], d["b1_qr"][one, 0:P].rearrange("g p j o -> p (g j) o"))\
                    .then_inc(s_in, 16)
                sp.dma_start(wr_in[0:Q2, 1, :, :], d["b1_qr"][one, P:QLORA].rearrange("g p j o -> p (g j) o"))\
                    .then_inc(s_in, 16)

        @block.gpsimd
        def _(pool):
            pool.sem_inc(s_added, HEAD)
            for t in range(TILES):
                pool.wait_ge(s_krot, 3 * t + 3)
                pool.tensor_tensor(lat_tok[:, t, QLORA + LAT:NA], part_a[:, t % 2, 0:ROT], part_b[:, t % 2, 0:ROT],
                                   ALU.add).then_inc(s_kadd, 1)
            with pool.Fori(0, TURNS) as i:
                for t in range(TILES):
                    pool.wait_ge(s_rope, i * (3 * TILES) + 3 * (t + 1))
                    pool.wait_ge(c.s_fill, done(i * c.fills + FILL["Q", 0] + t - 2))
                    pool.tensor_tensor(q_tok[:, t % 2, :, HD - ROT:HD],
                                       part_a[:, t % 2, :].rearrange("p (g x) -> p g x", g=G),
                                       part_b[:, t % 2, :].rearrange("p (g x) -> p g x", g=G),
                                       ALU.add).then_inc(s_added, 1)

        def slot_free(eng, i, u):
            batch, r = divmod((u - c.SLOTS) // 2, QT)
            if r == QT - 1:
                last_fill = FILL["O", batch % (2 * BATCH)] - (c.fills if batch < 0 else 0)
                eng.wait_ge(c.s_fill, done(i * c.fills + last_fill))
            else:
                eng.wait_ge(c.s_pv, i * (2 * BATCH * (QT - 1)) + (batch * (QT - 1) + r + 1 + HEAD))

        def out_view(x, h):
            b, pr = divmod(h, 2)
            return x[:, 2 * pr, bass.ts(b, SEQ)].rearrange("p (t q) -> p t q", q=P)

        @block.scalar
        def _(act):
            act.wait_ge(s_wa, 16)
            act.activation(wa_hi[:, :, :], wa[:, :, :], ACT.Copy).then_inc(s_wahi, 1)
            for t in range(TILES):
                act.wait_ge(s_a, t + 1)
                act.activation(lat_tok[:, t, :], proj[t % 2][:, 0:NA], ACT.Copy).then_inc(s_acopy, 1)
                act.wait_ge(s_acopy, t + 1)
                if t >= 1:
                    act.wait_ge(s_sq, 2 * t)
                act.activation(squares[:, 0, :], lat_tok[:, t, 0:QLORA], ACT.Square,
                               accum_out=sumsq[:, 0, t:t + 1]).then_inc(s_sq, 1)
                act.activation(squares[:, 1, 0:LAT], lat_tok[:, t, QLORA:QLORA + LAT], ACT.Square,
                               accum_out=sumsq[:, 1, t:t + 1]).then_inc(s_sq, 1)
            act.wait_ge(s_ms, 2)
            act.activation(rms[:, :, :], meansq[:, :, :], ACT.Sqrt).then_inc(s_rms, 1)
            for t in range(TILES):
                act.wait_ge(s_lat, t + 1)
                act.activation(latT_hi[:, 0:3, bass.ts(t, P)], c.out[t % 2][:, 0:3, :], ACT.Copy).then_inc(s_lhi, 1)
            c.act_start(act)

            def split_rotary(i):
                act.wait_ge(s_in, i * (16 * IN) + 16 * IN)
                for k, rows in ((0, P), (1, Q2)):
                    act.activation(wq_hi[0:rows, k, :, LAT:HD], wr_in[0:rows, k, :, :], ACT.Copy,
                                   scale=q_norm[0:rows, k:k + 1]).then_inc(s_rhi, 1)

            with act.Fori(0, TURNS) as i:
                split_rotary(i)
                for kind, t in STEPS:
                    if kind != "Q":
                        f = PROJ[kind, t]
                        act.wait_ge(s_proj, i * NP + (f + 1))
                    if kind == "W":
                        rows = (P, Q2)[t]
                        act.activation(wq_hi[0:rows, t, :, 0:LAT], proj[f % 2][0:rows, 0:G * LAT].rearrange(
                            "p (g x) -> p g x", g=G), ACT.Copy, scale=q_norm[0:rows, t:t + 1]).then_inc(s_projhi, 1)
                    elif kind == "G":
                        act.activation(wo_hi[:, t, :], proj[f % 2][:, :], ACT.Copy).then_inc(s_projhi, 1)
                    elif kind == "C":
                        act.wait_ge(c.s_fill, done(i * c.fills + FILL["Q", 0] + t - 2))
                        act.activation(q_tok[:, t % 2, :, 0:LAT], proj[f % 2][:, :].rearrange(
                            "p (g x) -> p g x", g=G)[:, :, 0:LAT], ACT.Copy, scale=SCALE).then_inc(s_projhi, 1)
                    else:
                        c.hi(act, i, FILL[kind, t], qT_hi[:, :, bass.ts(t, P)], c.out[FILL[kind, t] % 2][:, :, :])
                for s in range(PER + 5):
                    if s < PER:
                        c.exponential(act, i, s, units[s][2])
                    if 3 <= s < PER + 3 and (s - 3) % 2:
                        c.copy(act, lambda o, x: act.activation(o, x, ACT.Copy), i, s - 3, units[s - 3][2],
                               lambda e: slot_free(e, i, s - 3))
                    if s >= 12 and (s - 12) % 8 == 0:
                        h = (s - 12) // 8
                        c.hi(act, i, FILL["O", h], out_view(qT_hi, h), c.out[FILL["O", h] % 2][:, :, :])

        @block.vector
        def _(dve):
            dve.wait_ge(s_wahi, 1)
            dve.tensor_tensor(wa_lo[:, :, :], wa[:, :, :], wa_hi[:, :, :].bitcast(F32), ALU.subtract).then_inc(s_walo, 1)
            dve.wait_ge(s_tables, 96)
            dve.wait_ge(s_sq, 2 * TILES)
            for k, size in ((0, QLORA), (1, LAT)):
                dve.tensor_scalar(meansq[:, k, :], sumsq[:, k, :], 1.0 / size, RMS_EPS, ALU.mult,
                                  ALU.add).then_inc(s_ms, 1)
            dve.wait_ge(s_rms, 1)
            dve.reciprocal(rrms[:, :, :], rms[:, :, :]).then_inc(s_rrms, 1)
            dve.wait_ge(s_rrms, 1)

            def rotate_key(t):
                x, a, b = lat_tok[:, t, QLORA + LAT:NA], part_a[:, t % 2, 0:ROT], part_b[:, t % 2, 0:ROT]
                if t >= 2:
                    dve.wait_ge(s_kadd, t - 1)
                dve.tensor_tensor(a, x, cos_k[:, t % QT, :], ALU.mult).then_inc(s_krot, 1)
                for h in range(2):
                    dve.tensor_tensor(half(b, 1, h), half(x, 1, 1 - h), half(sin_k[:, t % QT, :], 1, h),
                                      ALU.mult).then_inc(s_krot, 1)

            def transposed_lo(t):
                dve.wait_ge(s_lhi, t + 1)
                dve.tensor_tensor(latT_lo[:, 0:3, bass.ts(t, P)], c.out[t % 2][:, 0:3, :],
                                  latT_hi[:, 0:3, bass.ts(t, P)].bitcast(F32), ALU.subtract).then_inc(s_llo, 1)

            for t in range(TILES):
                dve.tensor_scalar(lat_tok[:, t, 0:QLORA], lat_tok[:, t, 0:QLORA], rrms[:, 0, t:t + 1], None,
                                  ALU.mult).then_inc(s_ln, 1)
                dve.scalar_tensor_tensor(lat_tok[:, t, QLORA:QLORA + LAT], lat_tok[:, t, QLORA:QLORA + LAT],
                                         rrms[:, 1, t:t + 1], kv_norm[:, :], ALU.mult, ALU.mult).then_inc(s_ln, 1)
                rotate_key(t)
                if t >= 1:
                    transposed_lo(t - 1)
            transposed_lo(TILES - 1)
            c.dve_start(dve)
            dve.sem_inc(s_free, HEAD)
            dve.sem_inc(s_rlo, 1)

            def rotate(i, t):
                f = PROJ["C", t]
                dve.wait_ge(s_projhi, i * len(ACTS) + (ACTS["C", t] + 1))
                dve.wait_ge(s_added, done(i * TILES + t - 2))
                x = proj[f % 2][:, :].rearrange("p (g x) -> p g x", g=G)[:, :, LAT:HD]
                a, b = part_a[:, t % 2, :], part_b[:, t % 2, :]
                dve.tensor_tensor(a.rearrange("p (g x) -> p g x", g=G), x,
                                  cos_q[:, t % QT, :].unsqueeze(1).broadcast_to([P, G, ROT]),
                                  ALU.mult).then_inc(s_rope, 1)
                for h in range(2):
                    dve.tensor_tensor(half(b, G, h), x[:, :, (1 - h) * 32:(2 - h) * 32],
                                      sin_q[:, t % QT, h * 32:h * 32 + 32].unsqueeze(1).broadcast_to([P, G, 32]),
                                      ALU.mult).then_inc(s_rope, 1)

            def add_output(i, t):
                f = PROJ["E", t]
                dve.wait_ge(s_proj, i * NP + (f + 1))
                dve.tensor_tensor(m.x[:, t, :], m.x[:, t, :], proj[f % 2][:, :], ALU.add).then_inc(s_free, 1)

            with dve.Fori(0, TURNS) as i:
                dve.wait_ge(s_rhi, 2 * i + 2)
                for k, rows in ((0, P), (1, Q2)):
                    dve.scalar_tensor_tensor(wq_lo[0:rows, k, :, LAT:HD], wr_in[0:rows, k, :, :],
                                             q_norm[0:rows, k:k + 1], wq_hi[0:rows, k, :, LAT:HD].bitcast(F32),
                                             ALU.mult, ALU.subtract).then_inc(s_rlo, 1)
                for kind, t in STEPS:
                    if kind == "C":
                        rotate(i, t)
                    elif kind == "Q":
                        c.lo(dve, i, FILL[kind, t], qT_lo[:, :, bass.ts(t, P)], qT_hi[:, :, bass.ts(t, P)],
                             c.out[FILL[kind, t] % 2][:, :, :])
                    else:
                        f = PROJ[kind, t]
                        dve.wait_ge(s_projhi, i * len(ACTS) + (ACTS[kind, t] + 1))
                        if kind == "W":
                            rows = (P, Q2)[t]
                            dve.scalar_tensor_tensor(
                                wq_lo[0:rows, t, :, 0:LAT],
                                proj[f % 2][0:rows, 0:G * LAT].rearrange("p (g x) -> p g x", g=G),
                                q_norm[0:rows, t:t + 1], wq_hi[0:rows, t, :, 0:LAT].bitcast(F32),
                                ALU.mult, ALU.subtract).then_inc(s_free, 1)
                        else:
                            dve.tensor_tensor(wo_lo[:, t, :], proj[f % 2][:, :], wo_hi[:, t, :].bitcast(F32),
                                              ALU.subtract).then_inc(s_free, 1)
                for s in range(PER + 5):
                    if s < PER:
                        c.maximum(dve, i, s, units[s][2])
                    if 1 <= s < PER + 1:
                        c.scale(dve, i, s - 1, units[s - 1][2])
                    if 3 <= s < PER + 3 and (s - 3) % 2 == 0:
                        c.copy(dve, dve.tensor_copy, i, s - 3, units[s - 3][2], lambda e: slot_free(e, i, s - 3))
                    if s >= 12 and (s - 12) % 8 == 0:
                        h = (s - 12) // 8
                        c.lo(dve, i, FILL["O", h], out_view(qT_lo, h), out_view(qT_hi, h),
                             c.out[FILL["O", h] % 2][:, :, :])
                    if s >= 27 and s % 3 == 0 and (s - 27) // 3 < QT - 1:
                        add_output(i, (s - 27) // 3)
                for t in range(QT - 1, TILES):
                    add_output(i, t)

        @block.tensor
        def _(pe):
            pe.wait_ge(s_walo, 1)
            for t in range(TILES):
                if t >= 2:
                    pe.wait_ge(s_acopy, t - 1)
                for k in range(KT):
                    last = mm3(pe, proj[t % 2][:, 0:NA], pair(m.xnT_hi, m.xnT_lo, slice(None), k, bass.ts(t, P)),
                               pair(wa_hi, wa_lo, slice(None), k), start=k == 0, stop=k == KT - 1)
                last.then_inc(s_a, 1)
            for t in range(TILES):
                pe.wait_ge(s_ln, 2 * t + 2)
                pe.wait_ge(s_kadd, t + 1)
                if t >= 2:
                    pe.wait_ge(s_llo, t - 1)
                for r, at in enumerate((0, P, QLORA)):
                    last = pe.transpose(c.out[t % 2][:, r, :], lat_tok[:, t, at:at + P], m.ident[:, :])
                last.then_inc(s_lat, 1)
            pe.wait_ge(s_llo, TILES)
            c.pe_start(pe)

            def bank_taken(i, f):
                back = len(FREES) if f < 0 else 0
                kind, t = order[f % NP]
                if kind == "C":
                    pe.wait_ge(s_rope, i * (3 * TILES) + 3 * (t + 1))
                else:
                    pe.wait_ge(s_free, done(i * len(FREES) + (FREES[kind, t] - back)))

            def project(i, kind, t, rows):
                f = PROJ[kind, t]
                bank_taken(i, f - 2)
                for k, (lhs, rhs) in enumerate(rows):
                    last = mm3(pe, proj[f % 2][:, :], lhs, rhs, start=k == 0, stop=k == len(rows) - 1)
                last.then_inc(s_proj, 1)

            def project_output(i, t):
                if t % QT == 0:
                    pe.wait_ge(c.s_lo, done(i * c.fills + FILL["O", 2 * (t // QT) + 1]))
                project(i, "E", t, [(pair(qT_hi, qT_lo, slice(None), 2 * p, bass.ts(t, P)),
                                     pair(wo_hi, wo_lo, slice(None), p)) for p in range(2)])

            with pe.Fori(0, TURNS) as i:
                pe.wait_ge(s_in, i * (16 * IN) + 16 * IN)
                for kind, t in STEPS:
                    if kind == "W":
                        f = PROJ[kind, t]
                        bank_taken(i, f - 2)
                        rows = (P, Q2)[t]
                        for j in range(G):
                            last = pe.matmul(proj[f % 2][0:rows, j * LAT:(j + 1) * LAT],
                                             wn_in[:, j, t * P:t * P + rows], wk_in[:, j, :], start=True, stop=True)
                        last.then_inc(s_proj, 1)
                    elif kind == "G":
                        f = PROJ[kind, t]
                        bank_taken(i, f - 2)
                        for e in range(2):
                            last = pe.matmul(proj[f % 2][e * LAT:(e + 1) * LAT, :], wv_in[:, 2 * t + e, :],
                                             wo_in[:, 2 * t + e, :], start=True, stop=True)
                        last.then_inc(s_proj, 1)
                    elif kind == "C":
                        if t == 0:
                            pe.wait_ge(s_free, done(i * len(FREES) + FREES["W", 1]))
                            pe.wait_ge(s_rlo, 2 * i + 3)
                        project(i, kind, t, [
                            (pair(latT_hi, latT_lo, slice(0, rows), k, bass.ts(t, P)),
                             (wq_hi[0:rows, k, :, :].rearrange("p g x -> p (g x)"),
                              wq_lo[0:rows, k, :, :].rearrange("p g x -> p (g x)")))
                            for k, rows in ((0, P), (1, Q2))])
                    else:
                        f = FILL[kind, t]
                        pe.wait_ge(c.s_lo, done(i * c.fills + f - 2))
                        pe.wait_ge(s_projhi, i * len(ACTS) + (ACTS["C", t] + 1))
                        pe.wait_ge(s_added, done(i * TILES + t))
                        for r in range(G):
                            last = pe.transpose(c.out[f % 2][:, r, :], q_tok[:, t % 2, r, :], m.ident[:, :])
                        last.then_inc(c.s_fill, 1)
                for s in range(PER + 4):
                    if s < PER:
                        b, j, qt = units[s]
                        if s == 0:
                            pe.wait_ge(c.s_lo, done(i * c.fills + FILL["Q", TILES - 1]))
                        c.score(pe, m, i, s, qt, pair(qT_hi, qT_lo, slice(None), j, bass.ts(b * QT + qt, P)),
                                lambda w: pair(latT_hi, latT_lo, slice(None), 2, bass.ds(b * SEQ, w)),
                                m.mask[:, 0, :], m.ident16[:, :])
                    if 2 <= s < PER + 2:
                        c.turn(pe, m, i, s - 2, units[s - 2][2])
                    if s >= 4 and s % 2:
                        b, j, qt = units[s - 4]
                        c.times_v(pe, i, s - 4, qt, FILL["O", b * 2 + j // 2],
                                  lambda e, k: lat_tok[:, b * QT + k, QLORA:QLORA + LAT])
                    if s >= 26 and (s - 26) % 3 == 0 and (s - 26) // 3 < QT - 1:
                        project_output(i, (s - 26) // 3)
                for t in range(QT - 1, TILES):
                    project_output(i, t)


def attn1b_block(nc, m, d, prefix):
    G, TURNS, HD = 4, HEADS // 4, 16
    PER = BATCH * QT * G
    THIRDS = 3
    units = [(b, qt, j) for b in range(BATCH) for qt in range(QT) for j in range(G)]
    FILL = {s: n for n, s in enumerate([("K", 0), ("Q", 0), ("K", 1), ("Q", 1), ("O", 0), ("T", 0), ("O", 1),
                                        ("T", 1)])}
    with ExitStack() as ctx:
        n = Names(nc, ctx, prefix)
        w_in = n.sb("w_in", [P, KT, DIM])
        w_hi, w_lo = n.sb("w_hi", [P, KT, DIM], F32R), n.sb("w_lo", [P, KT, DIM], F32R)
        bias = n.sb("bias", [P, THIRDS * DIM])
        cos_sin = n.sb("cos_sin", [P, 2, QT, 3, HD // 2])
        row_kind = n.sb("row_kind", [P, 2])
        ident408 = n.sb("ident408", [P, P], BF16)
        raw = n.sb("raw", [P, 2, DIM])
        part_a, part_b = n.sb("part_a", [P, 2, DIM]), n.sb("part_b", [P, 2, DIM])
        k_tok, v_tok = n.sb("k_tok", [P, TILES, DIM]), n.sb("v_tok", [P, TILES, DIM])
        twice = {"Q": n.sb("q_twice", [P, TILES, G, 2, HD]), "K": n.sb("k_twice", [P, TILES, G, 2, HD])}
        v_now = n.sb("v_now", [P, TILES, G, 2 * HD])
        q_part_hi, q_part_sel = n.sb("q_part_hi", [P, TILES, P], F32R), n.sb("q_part_sel", [P, TILES, P], F32R)
        q_part_lo = n.sb("q_part_lo", [P, TILES, P])
        q_mixed = n.sb("q_mixed", [P, TILES, P], F32R)
        kT_hi, kT_lo = n.sb("kT_hi", [P, TILES, P], F32R), n.sb("kT_lo", [P, TILES, P], F32R)
        o_sb = n.sb("o_sb", [P, BATCH, QT, P])
        c = CausalUnits(n, PER, len(FILL), G, 2 * HD)
        proj = [n.ps(f"proj{i}", [P, DIM]) for i in range(2)]
        s_load, s_w, s_whi, s_wlo, s_proj, s_raw, s_rope, s_tok, s_zero, s_vnow = [
            n.sem(k) for k in ("load", "w", "whi", "wlo", "proj", "raw", "rope", "tok", "zero", "vnow")]
        s_twice, s_split, s_mixed = [n.sem(k) for k in ("twice", "split", "mixed")]
        block = ctx.enter_context(nc.Block())

        @block.sync
        def _(sp):
            for dst, name in ((cos_sin[:, :, :, :, :], "c1_cos_sin"), (row_kind[:, :], "c1_row_kind"),
                              (ident408[:, :].bitcast(U16), "ident408")):
                sp.dma_start(dst, d[name]).then_inc(s_load, 16)
            sp.dma_start(bias[:, :], d["c1_bias"].partition_broadcast(P)).then_inc(s_load, 16)
            for third in range(THIRDS):
                if third:
                    sp.wait_ge(s_wlo, third)
                sp.dma_start(w_in[:, :, :], d["c1_w"][third].rearrange("(k p) o -> p k o", p=P)).then_inc(s_w, 16)

        @block.gpsimd
        def _(pool):
            pool.memset(v_now[:, :, :, HD:2 * HD], 0.0).then_inc(s_zero, 1)
            for n_rot in range(2 * TILES):
                third, t = divmod(n_rot, TILES)
                into = (m.tok, k_tok)[third]
                pool.wait_ge(s_rope, 3 * n_rot + 3)
                pool.tensor_tensor(into[:, t, :], part_a[:, n_rot % 2, :], part_b[:, n_rot % 2, :],
                                   ALU.add).then_inc(s_tok, 1)
            pool.wait_ge(s_tok, 2 * TILES)
            pool.wait_ge(s_raw, 3 * TILES)
            pool.sem_inc(s_twice, HEAD)
            with pool.Fori(0, TURNS) as i:
                columns = bass.ds(i * (G * HD), G * HD)
                for kind, src in (("K", k_tok), ("Q", m.tok)):
                    pool.wait_ge(c.s_fill, done(i * c.fills + FILL[kind, 1] - c.fills))
                    for copy in range(2):
                        pool.tensor_copy(twice[kind][:, :, :, copy, :],
                                         src[:, :, columns].rearrange("p t (g x) -> p t g x", g=G))\
                            .then_inc(s_twice, 1)
                pool.wait_ge(c.s_fill, done(i * c.fills + FILL["O", 1] - c.fills))
                pool.tensor_copy(v_now[:, :, :, 0:HD],
                                 v_tok[:, :, columns].rearrange("p t (g x) -> p t g x", g=G)).then_inc(s_vnow, 1)

        def slot_free(eng, i, u):
            batch, r = divmod((u - c.SLOTS) // G, QT)
            if r == QT - 1:
                last_fill = FILL["O", batch % BATCH] - (c.fills if batch < 0 else 0)
                eng.wait_ge(c.s_fill, done(i * c.fills + last_fill))
            else:
                eng.wait_ge(c.s_pv, i * (BATCH * (QT - 1)) + (batch * (QT - 1) + r + 1 + HEAD))

        SPLITS = [("K", 0), ("Qhi", 0), ("Qsel", 0), ("K", 1), ("Qhi", 1), ("Qsel", 1)]

        @block.scalar
        def _(act):
            for third in range(THIRDS):
                act.wait_ge(s_w, 16 * (third + 1))
                if third:
                    act.wait_ge(s_proj, TILES * third)
                act.activation(w_hi[:, :, :], w_in[:, :, :], ACT.Copy).then_inc(s_whi, 1)
            c.act_start(act)
            with act.Fori(0, TURNS) as i:
                for b in range(BATCH):
                    tiles = slice(b * QT, (b + 1) * QT)
                    k_bank, q_bank = c.out[FILL["K", b] % 2], c.out[FILL["Q", b] % 2]
                    act.wait_ge(c.s_fill, done(i * c.fills + FILL["K", b]))
                    act.activation(kT_hi[:, tiles, :], k_bank[:, :, :], ACT.Copy).then_inc(s_split, 1)
                    act.wait_ge(c.s_fill, done(i * c.fills + FILL["Q", b]))
                    act.activation(q_part_hi[:, tiles, :], q_bank[:, :, :], ACT.Copy).then_inc(s_split, 1)
                    act.activation(q_part_sel[:, tiles, :], q_bank[:, :, :], ACT.Copy,
                                   scale=row_kind[:, 0:1]).then_inc(s_split, 1)
                for s in range(PER + 3):
                    if s < PER:
                        c.exponential(act, i, s, units[s][1])
                    if s >= 3 and (s - 3) % 2:
                        c.copy(act, lambda o, x: act.activation(o, x, ACT.Copy), i, s - 3, units[s - 3][1],
                               lambda e: slot_free(e, i, s - 3))

        @block.vector
        def _(dve):
            dve.wait_ge(s_load, 64)

            def split_weights(third):
                dve.wait_ge(s_whi, third + 1)
                dve.tensor_tensor(w_lo[:, :, :], w_in[:, :, :], w_hi[:, :, :].bitcast(F32),
                                  ALU.subtract).then_inc(s_wlo, 1)

            def take(step):
                third, t = divmod(step, TILES)
                dve.wait_ge(s_proj, step + 1)
                into = v_tok[:, t, :] if third == 2 else raw[:, step % 2, :]
                dve.tensor_tensor(into, proj[step % 2][:, :], bias[:, bass.ts(third, DIM)], ALU.add).then_inc(s_raw, 1)
                if third == 2:
                    return
                if step >= 2:
                    dve.wait_ge(s_tok, step - 1)
                dve.wait_ge(s_raw, step + 1)
                x, a, b = raw[:, step % 2, :], part_a[:, step % 2, :], part_b[:, step % 2, :]
                table = cos_sin[:, third, t % QT, :, :]
                dve.tensor_tensor(a.rearrange("p (g x) -> p g x", x=HD // 2), x.rearrange("p (g x) -> p g x", x=HD // 2),
                                  table[:, 0, :].unsqueeze(1).broadcast_to([P, 2 * HEADS, HD // 2]),
                                  ALU.mult).then_inc(s_rope, 1)
                halves = lambda y, h: y.rearrange("p (g h x) -> p g h x", h=2, x=HD // 2)[:, :, h, :]
                for h in range(2):
                    dve.tensor_tensor(halves(b, h), halves(x, 1 - h),
                                      table[:, 1 + h, :].unsqueeze(1).broadcast_to([P, HEADS, HD // 2]),
                                      ALU.mult).then_inc(s_rope, 1)

            for third in range(THIRDS):
                split_weights(third)
                for t in range(TILES):
                    take(third * TILES + t)
            c.dve_start(dve)

            def output(i, b):
                dve.wait_ge(c.s_fill, done(i * c.fills + FILL["O", b]))
                dve.tensor_copy(o_sb[:, b, :, :], c.out[FILL["O", b] % 2][:, :, :]).then_inc(c.s_lo, 1)

            def to_tokens(i, b):
                dve.wait_ge(c.s_fill, done(i * c.fills + FILL["T", b]))
                x = c.out[FILL["T", b] % 2][:, :, :].rearrange("p t (g x) -> p t g x", g=G)[:, :, :, 0:HD]
                dve.tensor_copy(m.tok[:, b * QT:(b + 1) * QT, bass.ds(i * (G * HD), G * HD)].rearrange(
                    "p t (g x) -> p t g x", g=G), x).then_inc(c.s_lo, 1)

            with dve.Fori(0, TURNS) as i:
                for b in range(BATCH):
                    tiles = slice(b * QT, (b + 1) * QT)
                    k_bank, q_bank = c.out[FILL["K", b] % 2], c.out[FILL["Q", b] % 2]
                    dve.wait_ge(s_split, i * len(SPLITS) + (3 * b + 1))
                    dve.tensor_tensor(kT_lo[:, tiles, :], k_bank[:, :, :], kT_hi[:, tiles, :].bitcast(F32),
                                      ALU.subtract).then_inc(c.s_lo, 1)
                    dve.wait_ge(s_split, i * len(SPLITS) + (3 * b + 3))
                    dve.tensor_tensor(q_part_lo[:, tiles, :], q_bank[:, :, :], q_part_hi[:, tiles, :].bitcast(F32),
                                      ALU.subtract).then_inc(c.s_lo, 1)
                    dve.wait_ge(c.s_lo, done(i * c.fills + FILL["Q", b]))
                    dve.scalar_tensor_tensor(q_mixed[:, tiles, :], q_part_lo[:, tiles, :], row_kind[:, 1:2],
                                             q_part_sel[:, tiles, :].bitcast(F32), ALU.mult,
                                             ALU.add).then_inc(s_mixed, 1)
                for s in range(PER + 8):
                    if s < PER:
                        c.maximum(dve, i, s, units[s][1])
                    if 1 <= s < PER + 1:
                        c.scale(dve, i, s - 1, units[s - 1][1])
                    if 3 <= s < PER + 3 and (s - 3) % 2 == 0:
                        c.copy(dve, dve.tensor_copy, i, s - 3, units[s - 3][1], lambda e: slot_free(e, i, s - 3))
                    if s in (20, 36):
                        output(i, (s - 20) // 16)
                    if s in (23, 39):
                        to_tokens(i, (s - 23) // 16)

        @block.tensor
        def _(pe):
            for step in range(THIRDS * TILES):
                third, t = divmod(step, TILES)
                if t == 0:
                    pe.wait_ge(s_wlo, third + 1)
                if step >= 2:
                    pe.wait_ge(s_raw, step - 1)
                for k in range(KT):
                    last = mm3(pe, proj[step % 2][:, :], pair(m.xnT_hi, m.xnT_lo, slice(None), k, bass.ts(t, P)),
                               pair(w_hi, w_lo, slice(None), k), start=k == 0, stop=k == KT - 1)
                last.then_inc(s_proj, 1)
            pe.wait_ge(s_zero, 1)
            c.pe_start(pe)

            def back_to_tokens(i, b):
                f = FILL["T", b]
                pe.wait_ge(c.s_lo, done(i * c.fills + FILL["O", b]))
                pe.wait_ge(c.s_lo, done(i * c.fills + f - 2))
                for qt in range(QT):
                    last = pe.transpose(c.out[f % 2][:, qt, :], o_sb[:, b, qt, :], m.ident[:, :])
                last.then_inc(c.s_fill, 1)

            with pe.Fori(0, TURNS) as i:
                for b in range(BATCH):
                    for kind in "KQ":
                        f = FILL[kind, b]
                        pe.wait_ge(s_twice, i * 4 + ((2 if kind == "K" else 4) + HEAD))
                        pe.wait_ge(c.s_lo, done(i * c.fills + f - 2))
                        for r in range(QT):
                            last = pe.transpose(c.out[f % 2][:, r, :],
                                                twice[kind][:, b * QT + r, :, :, :].rearrange("p g c x -> p (g c x)"),
                                                m.ident[:, :])
                        last.then_inc(c.s_fill, 1)
                for s in range(PER + 8):
                    if s < PER:
                        b, qt, j = units[s]
                        rows = slice(32 * j, 32 * j + 32)
                        if s % (QT * G) == 0:
                            pe.wait_ge(s_mixed, i * BATCH + (b + 1))
                        c.score(pe, m, i, s, qt, (q_mixed[rows, b * QT + qt, :], None),
                                lambda w: tuple(x[rows, b * QT:b * QT + w // P, :].rearrange("p t q -> p (t q)")
                                                for x in (kT_hi, kT_lo)),
                                m.mask[:, 1, :], ident408[:, :])
                    if 2 <= s < PER + 2:
                        c.turn(pe, m, i, s - 2, units[s - 2][1])
                    if 4 <= s < PER + 4 and (s - 4) % G == G - 1:
                        b, qt, j = units[s - 4]
                        if s == G + 3:
                            pe.wait_ge(s_vnow, i + 1)
                        c.times_v(pe, i, s - 4, qt, FILL["O", b], lambda e, k: v_now[:, b * QT + k, e, :])
                    if s in (22, 38):
                        back_to_tokens(i, (s - 22) // 16)


def lay_out_attention(o, a):
    t = np.transpose
    kv, q = a["L0_attn_a_Wkv_d"], a["L0_attn_a_Wq_d"]
    rows = np.zeros((DIM, 4, 32), np.float32)
    rows[:, :, 0:12] = np.tile(kv, 3)[:, None, :]
    both = np.zeros((DIM, P), np.float32)
    both[:, 0:12], both[:, 32:36] = q, kv
    o["a0_down"] = np.concatenate([rows.reshape(DIM, P), both], 1)
    bias = np.zeros((P, 2), np.float32)
    bias.reshape(4, 32, 2)[:, 0:12, 0] = np.tile(a["L0_attn_a_bkv_d"], 3)
    bias[0:12, 1], bias[12, 1], bias[32:36, 1] = a["L0_attn_a_bq_d"], 1.0, a["L0_attn_a_bkv_d"]
    o["a0_down_bias"] = bias
    wqk = np.concatenate([a["L0_attn_a_W_qk"], a["L0_attn_a_b_qk"][None]], 0).reshape(13, 8, 4, 1, 4)
    spread = np.zeros((13, 8, 4, 8, 4), np.float32)
    spread[:, :, :, 0:3, :] = wqk
    o["a0_wqk"] = spread.reshape(13, 8 * P)
    o["a0_wv"], o["a0_bv"] = a["L0_attn_a_Wv_u"], a["L0_attn_a_bv_u"]
    o["a0_wo"], o["a0_bo"] = a["L0_attn_a_Wo"], a["L0_attn_a_bo"]

    order = np.concatenate([np.arange(0, 32), np.arange(64, 96), np.arange(32, 64), np.arange(96, 128)])
    o["b0_down"] = a["L0_attn_b_Wdk"]
    upk = t(a["L0_attn_b_Wupk"].reshape(8, 64, DIM), (0, 2, 1))
    upv = t(a["L0_attn_b_Wupv"].reshape(8, 128, DIM), (0, 2, 1))
    o["b0_up"] = np.concatenate([upk, upv], 2)
    o["b0_rot"] = t(a["L0_attn_b_Wkr"].reshape(8, 64, DIM), (0, 2, 1))
    wq = a["L0_attn_b_Wq"].reshape(8, 4, 128, DIM)[:, :, order]
    o["b0_q"] = t(wq.reshape(8, DIM, DIM), (0, 2, 1))
    o["b0_o"] = t(a["L0_attn_b_Wo"]).reshape(8, DIM, DIM)

    turned = np.concatenate([np.arange(0, 64, 2), np.arange(1, 64, 2)])
    kva = a["L1_attn_a_wkv_a"]
    o["b1_down"] = t(np.concatenate([a["L1_attn_a_wq_a"], kva[0:64], kva[64:128][turned]], 0))
    norm = np.zeros((2, P), np.float32)
    norm.reshape(-1)[0:192] = a["L1_attn_a_q_norm_w"]
    o["b1_q_norm"], o["b1_kv_norm"] = t(norm), a["L1_attn_a_kv_norm_w"]
    wq = a["L1_attn_a_wq_b"].reshape(8, 4, 192, 192)
    o["b1_qn"] = t(wq[:, :, 0:128], (0, 2, 1, 3))
    o["b1_qr"] = t(wq[:, :, 128:192][:, :, turned], (0, 3, 1, 2))
    wkv = a["L1_attn_a_wkv_b"].reshape(8, 4, 256, 64)
    o["b1_k"], o["b1_v"] = t(wkv[:, :, 0:128], (0, 2, 1, 3)), t(wkv[:, :, 128:256], (0, 2, 1, 3))
    o["b1_o"] = t(t(a["L1_attn_a_wo"]).reshape(8, 4, 128, DIM), (0, 2, 1, 3))

    o["c1_w"] = t(a["L1_attn_b_qkv_w"].reshape(DIM, 3, DIM), (1, 0, 2))
    o["c1_bias"] = a["L1_attn_b_qkv_b"]
    o["c1_wo"], o["c1_bo"] = a["L1_attn_b_out_w"], a["L1_attn_b_out_b"]


def attn1b(nc, m, d, prefix):
    with nc.sbuf_tensor(f"{prefix}_tok", [P, TILES, DIM], F32) as m.tok:
        attn1b_block(nc, m, d, prefix)
        project_block(nc, m, d, prefix + "o", "c1_wo", "c1_bo")


def attn0a(nc, m, d, prefix):
    with nc.sbuf_tensor(f"{prefix}_tok", [P, TILES, DIM], F32) as m.tok:
        attn0a_block(nc, m, d, prefix)
        project_block(nc, m, d, prefix + "o", "a0_wo", "a0_bo")


BLOCKS = {"ffn0": ffn0_block, "ffn1": ffn1_block, "attn0a": attn0a, "attn0b": attn0b_block, "attn1a": attn1a_block,
          "attn1b": attn1b}


class Model:
    pass


PHASES = ["attn0a", "ffn0", "attn0b", "ffn0", "attn1a", "ffn1", "attn1b", "ffn1"]


def build(nc, d):
    with ExitStack() as ctx:
        m = Model()
        m.x = ctx.enter_context(nc.sbuf_tensor("x_resident", [P, TILES, DIM], F32))
        m.xnT_hi = ctx.enter_context(nc.sbuf_tensor("xnT_hi", [P, KT, TILES * P], F32R))
        m.xnT_lo = ctx.enter_context(nc.sbuf_tensor("xnT_lo", [P, KT, TILES * P], F32R))
        m.ident = ctx.enter_context(nc.sbuf_tensor("ident_f32", [P, P], F32))
        m.ident16 = ctx.enter_context(nc.sbuf_tensor("ident_bf16", [P, P], BF16))
        m.mask = ctx.enter_context(nc.sbuf_tensor("mask_bf16", [P, 2, P], BF16))
        load_block(nc, m, d)
        for i, phase in enumerate(PHASES):
            layernorm_block(nc, m, f"ln{i}")
            BLOCKS[phase](nc, m, d, f"{phase}_{i}")
        store_block(nc, m, d)


def shape_constants():
    bf16 = lambda x: (x.astype(np.float32).view(np.uint32) >> 16).astype(np.uint16)
    c = {}
    c["ident"] = np.eye(P, dtype=np.float32)
    c["ident16"] = bf16(np.eye(P))
    later = np.triu(np.ones((P, P), np.float32), 1)
    c["mask"] = bf16(np.stack([later * np.float32(-1e30), later * np.float32(-163.0)], 1))
    c["adapter_of_row"] = (np.arange(48, dtype=np.float32) // 16).reshape(48, 1)
    kind = np.arange(P) % 32 // 4
    c["a0_row_kind"] = np.stack([kind < 2, kind == 2, 0.5 * (kind % 2 == 0) * (kind < 3), kind == 1],
                                1).astype(np.float32)
    inv = 1.0 / 10000.0 ** (np.arange(0, 128, 2, dtype=np.float32) / 128)
    ang = np.outer(np.arange(SEQ, dtype=np.float32), inv)
    cos, sin = np.cos(ang), np.sin(ang)
    pairs = lambda lo, hi: np.concatenate([lo[:, 0:32], hi[:, 0:32], lo[:, 32:64], hi[:, 32:64]], 1)
    tiles = lambda x: np.ascontiguousarray(x.reshape(QT, P, -1).transpose(1, 0, 2).astype(np.float32))
    scale = np.float32(1.0 / np.sqrt(128.0))
    c["b0_cos_q"], c["b0_sin_q"] = tiles(pairs(cos, cos) * scale), tiles(pairs(-sin, sin) * scale)
    c["b0_cos_k"], c["b0_sin_k"] = tiles(pairs(cos, cos)[:, 0:64]), tiles(pairs(-sin, sin)[:, 0:64])
    freq = 1.0 / 10000.0 ** (np.arange(0, 64, 2, dtype=np.float32) / 64)
    ang = np.outer(np.arange(SEQ, dtype=np.float32), freq)
    cos, sin = np.cos(ang), np.sin(ang)
    scale = np.float32(1.0 / np.sqrt(np.float32(192.0)))
    both, signed = np.concatenate([cos, cos], 1), np.concatenate([-sin, sin], 1)
    c["b1_cos_q"], c["b1_sin_q"] = tiles(both * scale), tiles(signed * scale)
    c["b1_cos_k"], c["b1_sin_k"] = tiles(both), tiles(signed)
    ang = np.arange(SEQ, dtype=np.float32)[:, None] * (1.0 / 10000.0 ** (np.arange(0, 8, dtype=np.float32) / 8))
    cos, sin = np.cos(ang), np.sin(ang)
    table = np.stack([cos, -sin, sin], 1).reshape(QT, P, 3, 8).transpose(1, 0, 2, 3)
    c["c1_cos_sin"] = np.stack([table * np.float32(0.25), table], 1).astype(np.float32)
    half = np.arange(P) % 32 // 16
    c["c1_row_kind"] = np.stack([half == 0, half == 1], 1).astype(np.float32)
    c["ident408"] = bf16(np.eye(P) * 408)
    c["expert_no"] = np.arange(8, dtype=np.float32)
    return c


def laid_out(inp):
    t = np.transpose
    a = {k: np.asarray(v) for k, v in inp.items()}
    o = {}
    o["x"] = a["L0_attn_a_x"]
    o["ffn0_w"] = t(a["L0_ffn_weight"])
    o["ffn0_bias"] = a["L0_ffn_bias"]
    o["lora_a"] = a["L0_ffn_lora_A"].reshape(48, DIM)
    o["lora_b"] = t(a["L0_ffn_lora_B"], (0, 2, 1)).reshape(48, DIM)
    o["lora_starts"] = a["L0_ffn_lora_start_indices"]
    o["ffn1_w"] = t(a["L1_ffn_W_base"])
    o["ffn1_bias"] = a["L1_ffn_b_base"]
    o["ffn1_a"] = np.concatenate([t(a["L1_ffn_A"].reshape(128, DIM)), t(a["L1_ffn_W_router"])], 1)
    o["ffn1_b"] = t(a["L1_ffn_B"], (0, 2, 1)).reshape(128, DIM)
    lay_out_attention(o, a)
    return o


def kernel(**inputs):
    import concourse.bacc as bacc
    from concourse.bass_utils import run_bass_kernel_spmd

    nc = bacc.Bacc("TRN2", target_bir_lowering=False, num_devices=1)
    arrays, d = {}, {}
    for name, v in {**laid_out(inputs), **shape_constants()}.items():
        v = np.ascontiguousarray(v)
        arrays[f"in_{name}"] = v
        d[name] = nc.dram_tensor(f"in_{name}", v.shape, mybir.dt.from_np(v.dtype), kind="ExternalInput").ap()
    d["out"] = nc.dram_tensor("out_y", (BATCH, SEQ, DIM), F32, kind="ExternalOutput").ap()
    build(nc, d)
    return run_bass_kernel_spmd(nc, [arrays], core_ids=[0]).results[0]["out_y"]
```

```python
from contextlib import ExitStack

import numpy as np
import concourse.bass as bass
from concourse import mybir

F32 = mybir.dt.float32
F32R = mybir.dt.float32r
BF16 = mybir.dt.bfloat16
I32 = mybir.dt.int32
U16 = mybir.dt.uint16
U32 = mybir.dt.uint32
ALU = mybir.AluOpType
ACT = mybir.ActivationFunctionType
AX = mybir.AxisListType

P = 128
BATCH, SEQ, DIM = 2, 512, 512
TILES = BATCH * SEQ // P
QT = SEQ // P
KT = DIM // P
HEADS = 32
LN_EPS = 1e-5


def mm3(pe, out, lhs, rhs, start, stop):
    pe.matmul(out, lhs[0], rhs[0], start=start, stop=False)
    pe.matmul(out, lhs[1], rhs[0], start=False, stop=False)
    return pe.matmul(out, lhs[0], rhs[1], start=False, stop=stop)


def pair(hi, lo, *idx):
    return hi[idx], lo[idx]


class Names:

    def __init__(self, nc, ctx, prefix):
        self.nc, self.ctx, self.prefix, self.sems = nc, ctx, prefix, []
        ctx.callback(self.release)

    def sb(self, name, shape, dt=F32):
        return self.ctx.enter_context(self.nc.sbuf_tensor(f"{self.prefix}_{name}", shape, dt))

    def early(self, name, shape, dt=F32):
        with self.nc.sbuf_tensor(f"{self.prefix}_{name}", shape, dt) as buffer:
            return buffer

    def ps(self, name, shape, dt=F32):
        return self.ctx.enter_context(self.nc.psum_tensor(f"{self.prefix}_{name}", shape, dt))

    def sem(self, name):
        self.sems.append(self.nc.alloc_semaphore(f"{self.prefix}_{name}"))
        return self.sems[-1]

    def release(self):
        self.nc.clear_and_free_semaphores(self.sems)
        self.nc.all_engine_barrier()


def load_block(nc, m, d):
    with ExitStack() as ctx:
        n = Names(nc, ctx, "load")
        loaded = n.sem("loaded")
        block = ctx.enter_context(nc.Block())

        @block.sync
        def _(sp):
            sp.dma_start(m.x[:, :, :], d["x"].rearrange("b (t p) c -> p (b t) c", p=P)).then_inc(loaded, 16)
            sp.dma_start(m.ident[:, :], d["ident"]).then_inc(loaded, 16)
            sp.dma_start(m.ident16[:, :].bitcast(U16), d["ident16"]).then_inc(loaded, 16)
            sp.dma_start(m.mask[:, :, :].bitcast(U16), d["mask"]).then_inc(loaded, 16)
            sp.wait_ge(loaded, 64)


def layernorm_block(nc, m, prefix):
    with ExitStack() as ctx:
        n = Names(nc, ctx, prefix)
        stats = n.sb("stats", [P, TILES, 6])
        meanvar = n.sb("meanvar", [P, TILES, 2])
        var_eps = n.sb("var_eps", [P, TILES])
        std = n.sb("std", [P, TILES])
        rstd = n.sb("rstd", [P, TILES])
        xn = n.sb("xn", [P, 2, DIM])
        turned = [n.ps(f"turned{i}", [P, KT, P]) for i in range(2)]
        s_stats, s_aggr, s_var, s_std, s_rstd = [n.sem(k) for k in ("stats", "aggr", "var", "std", "rstd")]
        s_xn, s_turned, s_hi, s_lo = [n.sem(k) for k in ("xn", "turned", "hi", "lo")]
        block = ctx.enter_context(nc.Block())

        @block.vector
        def _(dve):
            for t in range(TILES):
                dve.bn_stats(stats[:, t, :], m.x[:, t, :]).then_inc(s_stats, 1)
            for t in range(TILES):
                dve.wait_ge(s_stats, t + 1)
                dve.bn_aggr(meanvar[:, t, :], stats[:, t, :]).then_inc(s_aggr, 1)
            dve.wait_ge(s_aggr, TILES)
            dve.tensor_scalar(var_eps[:, :], meanvar[:, :, 1], LN_EPS, None, ALU.add).then_inc(s_var, 1)
            dve.wait_ge(s_std, 1)
            dve.reciprocal(rstd[:, :], std[:, :]).then_inc(s_rstd, 1)
            dve.wait_ge(s_rstd, 1)

            def normalise(t):
                if t >= 2:
                    dve.wait_ge(s_turned, t - 1)
                dve.tensor_scalar(xn[:, t % 2, :], m.x[:, t, :], meanvar[:, t, 0:1], rstd[:, t:t + 1],
                                  ALU.subtract, ALU.mult).then_inc(s_xn, 1)

            normalise(0)
            for t in range(TILES):
                if t + 1 < TILES:
                    normalise(t + 1)
                dve.wait_ge(s_turned, t + 1)
                dve.wait_ge(s_hi, t + 1)
                dve.tensor_tensor(m.xnT_lo[:, :, t * P:(t + 1) * P], turned[t % 2][:, :, :],
                                  m.xnT_hi[:, :, t * P:(t + 1) * P].bitcast(F32), ALU.subtract).then_inc(s_lo, 1)

        @block.scalar
        def _(act):
            act.wait_ge(s_var, 1)
            act.activation(std[:, :], var_eps[:, :], ACT.Sqrt).then_inc(s_std, 1)
            for t in range(TILES):
                act.wait_ge(s_turned, t + 1)
                act.activation(m.xnT_hi[:, :, t * P:(t + 1) * P], turned[t % 2][:, :, :],
                               ACT.Copy).then_inc(s_hi, 1)

        @block.tensor
        def _(pe):
            for t in range(TILES):
                pe.wait_ge(s_xn, t + 1)
                if t >= 2:
                    pe.wait_ge(s_lo, t - 1)
                for k in range(KT):
                    last = pe.transpose(turned[t % 2][:, k, :], xn[:, t % 2, k * P:(k + 1) * P], m.ident[:, :])
                last.then_inc(s_turned, 1)


def store_block(nc, m, d):
    with ExitStack() as ctx:
        n = Names(nc, ctx, "store")
        stored = n.sem("stored")
        block = ctx.enter_context(nc.Block())

        @block.sync
        def _(sp):
            sp.dma_start(d["out"].rearrange("b (t p) c -> p (b t) c", p=P), m.x[:, :, :]).then_inc(stored, 16)
            sp.wait_ge(stored, 16)


def ffn0_block(nc, m, d, prefix):
    ADAPTERS, RANK = 3, 16
    AR = ADAPTERS * RANK
    STARTS = 4
    CHUNKS = BATCH * KT
    with ExitStack() as ctx:
        n = Names(nc, ctx, prefix)
        w = n.sb("w", [P, KT, DIM])
        bias = n.sb("bias", [P, DIM])
        lora_a = n.sb("lora_a", [AR, DIM])
        lora_b = n.sb("lora_b", [AR, DIM])
        starts_i = n.sb("starts_i", [AR, STARTS], I32)
        starts = n.sb("starts", [AR, STARTS])
        adapter_of_row = n.sb("adapter_of_row", [AR, 1])
        begun = n.sb("begun", [AR, BATCH, STARTS])
        count = n.sb("count", [AR, BATCH])
        clipped = n.sb("clipped", [AR, BATCH])
        chosen = n.sb("chosen", [AR, BATCH])
        used = n.sb("used", [AR, BATCH])
        gate = n.sb("gate", [AR, BATCH])
        gated_a = n.sb("gated_a", [AR, BATCH, DIM])
        merged = n.sb("merged", [P, 2, DIM])
        w_hi = n.sb("w_hi", [P, BATCH, KT, DIM], F32R)
        w_lo = n.sb("w_lo", [P, BATCH, KT, DIM], F32R)
        delta = [n.ps(f"delta{i}", [P, DIM]) for i in range(2)]
        y = [n.ps(f"y{i}", [P, DIM]) for i in range(2)]
        s_load, s_gate, s_ga, s_delta, s_merged, s_hi, s_lo = [
            n.sem(k) for k in ("load", "gate", "ga", "delta", "merged", "hi", "lo")]
        s_bias, s_y, s_x = [n.sem(k) for k in ("bias", "y", "x")]
        block = ctx.enter_context(nc.Block())

        @block.sync
        def _(sp):
            sp.dma_start(starts_i[:, :], d["lora_starts"].partition_broadcast(AR)).then_inc(s_load, 16)
            sp.dma_start(adapter_of_row[:, :], d["adapter_of_row"]).then_inc(s_load, 16)
            sp.dma_start(lora_a[:, :], d["lora_a"]).then_inc(s_load, 16)
            sp.dma_start(lora_b[:, :], d["lora_b"]).then_inc(s_load, 16)
            sp.dma_start(w[:, :, :], d["ffn0_w"].rearrange("(k p) o -> p k o", p=P)).then_inc(s_load, 16)
            sp.dma_start(bias[:, :], d["ffn0_bias"].partition_broadcast(P)).then_inc(s_load, 16)

        @block.gpsimd
        def _(pool):
            pool.wait_ge(s_load, 96)
            for t in range(TILES):
                pool.tensor_tensor(m.x[:, t, :], m.x[:, t, :], bias[:, :], ALU.add).then_inc(s_bias, 1)

        @block.vector
        def _(dve):
            step = [0]

            def then(ins):
                ins.then_inc(s_gate, 1)
                step[0] += 1
                dve.wait_ge(s_gate, step[0])

            dve.wait_ge(s_load, 96)
            then(dve.tensor_copy(starts[:, :], starts_i[:, :]))
            for b in range(BATCH):
                then(dve.tensor_scalar(begun[:, b, :], starts[:, :], float(b), None, ALU.is_le))
                then(dve.tensor_reduce(count[:, b:b + 1], begun[:, b, :], AX.X, ALU.add))
            then(dve.tensor_scalar(clipped[:, :], count[:, :], -2.0, 0.0, ALU.add, ALU.max))
            then(dve.tensor_scalar(clipped[:, :], clipped[:, :], float(ADAPTERS - 1), None, ALU.min))
            then(dve.tensor_scalar(chosen[:, :], clipped[:, :], adapter_of_row[:, 0:1], None, ALU.is_equal))
            then(dve.tensor_scalar(used[:, :], count[:, :], 2.0, None, ALU.is_ge))
            then(dve.tensor_tensor(gate[:, :], chosen[:, :], used[:, :], ALU.mult))
            for b in range(BATCH):
                dve.tensor_scalar(gated_a[:, b, :], lora_a[:, :], gate[:, b:b + 1], None,
                                  ALU.mult).then_inc(s_ga, 1)

            def merge(c):
                dve.wait_ge(s_delta, c + 1)
                if c >= 2:
                    dve.wait_ge(s_hi, c - 1)
                    dve.wait_ge(s_lo, c - 1)
                dve.tensor_tensor(merged[:, c % 2, :], w[:, c % KT, :], delta[c % 2][:, :],
                                  ALU.add).then_inc(s_merged, 1)

            merge(0)
            for c in range(CHUNKS):
                if c + 1 < CHUNKS:
                    merge(c + 1)
                dve.wait_ge(s_hi, c + 1)
                dve.wait_ge(s_merged, c + 1)
                dve.tensor_tensor(w_lo[:, c // KT, c % KT, :], merged[:, c % 2, :],
                                  w_hi[:, c // KT, c % KT, :].bitcast(F32), ALU.subtract).then_inc(s_lo, 1)
            for t in range(TILES):
                dve.wait_ge(s_bias, t + 1)
                dve.wait_ge(s_y, t + 1)
                dve.tensor_tensor(m.x[:, t, :], m.x[:, t, :], y[t % 2][:, :], ALU.add).then_inc(s_x, 1)

        @block.scalar
        def _(act):
            for c in range(CHUNKS):
                act.wait_ge(s_merged, c + 1)
                act.activation(w_hi[:, c // KT, c % KT, :], merged[:, c % 2, :], ACT.Copy).then_inc(s_hi, 1)

        @block.tensor
        def _(pe):
            for c in range(CHUNKS):
                b, k = divmod(c, KT)
                pe.wait_ge(s_ga, b + 1)
                if c >= 2:
                    pe.wait_ge(s_merged, c - 1)
                pe.matmul(delta[c % 2][:, :], gated_a[:, b, k * P:(k + 1) * P], lora_b[:, :],
                          start=True, stop=True).then_inc(s_delta, 1)
            for t in range(TILES):
                b = t // QT
                pe.wait_ge(s_lo, KT * (b + 1))
                if t >= 2:
                    pe.wait_ge(s_x, t - 1)
                for k in range(KT):
                    last = mm3(pe, y[t % 2][:, :], pair(m.xnT_hi, m.xnT_lo, slice(None), k, bass.ts(t, P)),
                               pair(w_hi, w_lo, slice(None), b, k), start=k == 0, stop=k == KT - 1)
                last.then_inc(s_y, 1)


def ffn1_block(nc, m, d, prefix):
    EXPERTS, RANK, SCALING = 8, 16, 2.0
    ER = EXPERTS * RANK
    NA = ER + EXPERTS
    GAP = 7 * TILES + 3
    with ExitStack() as ctx:
        n = Names(nc, ctx, prefix)
        w = n.sb("w", [P, KT, DIM])
        wa = n.sb("wa", [P, KT, NA])
        wb = n.sb("wb", [ER, DIM])
        bias = n.sb("bias", [P, DIM])
        expert_no = n.sb("expert_no", [P, EXPERTS])
        w_hi, w_lo = n.sb("w_hi", [P, KT, DIM], F32R), n.sb("w_lo", [P, KT, DIM], F32R)
        wa_hi, wa_lo = n.sb("wa_hi", [P, KT, NA], F32R), n.sb("wa_lo", [P, KT, NA], F32R)
        wb_hi, wb_lo = n.sb("wb_hi", [ER, DIM], F32R), n.sb("wb_lo", [ER, DIM], F32R)
        logit = n.sb("logit", [P, TILES, EXPERTS])
        rest = n.sb("rest", [P, TILES, EXPERTS])
        top1, top2 = n.sb("top1", [P, TILES, 8]), n.sb("top2", [P, TILES, 8])
        at1, at2 = n.sb("at1", [P, TILES, 8], U32), n.sb("at2", [P, TILES, 8], U32)
        at1f, at2f = n.sb("at1f", [P, TILES, 1]), n.sb("at2f", [P, TILES, 1])
        hot1, hot2 = n.sb("hot1", [P, TILES, EXPERTS]), n.sb("hot2", [P, TILES, EXPERTS])
        gap, ratio = n.sb("gap", [P, TILES, 1]), n.sb("ratio", [P, TILES, 1])
        denom, first = n.sb("denom", [P, TILES, 1]), n.sb("first", [P, TILES, 1])
        second = n.sb("second", [P, TILES, 1])
        combine = n.sb("combine", [P, TILES, EXPERTS])
        h = n.sb("h", [P, TILES, ER])
        hw = n.sb("hw", [P, TILES, ER])
        hwT_hi, hwT_lo = n.sb("hwT_hi", [ER, 2, P], F32R), n.sb("hwT_lo", [ER, 2, P], F32R)
        proj = [n.ps(f"proj{i}", [P, DIM]) for i in range(2)]
        turned = [n.ps(f"turned{i}", [P, DIM]) for i in range(2)]
        y = [n.ps(f"y{i}", [P, DIM]) for i in range(2)]
        s_load, s_whi, s_wlo, s_proj, s_h, s_r, s_ratio, s_hw, s_turned, s_thi, s_tlo, s_bias, s_y, s_x = [
            n.sem(k) for k in ("load", "whi", "wlo", "proj", "h", "route", "ratio", "hw", "turned", "thi", "tlo",
                               "bias", "y", "x")]
        block = ctx.enter_context(nc.Block())

        @block.sync
        def _(sp):
            sp.dma_start(wa[:, :, :], d["ffn1_a"].rearrange("(k p) o -> p k o", p=P)).then_inc(s_load, 16)
            sp.dma_start(wb[:, :], d["ffn1_b"]).then_inc(s_load, 16)
            sp.dma_start(w[:, :, :], d["ffn1_w"].rearrange("(k p) o -> p k o", p=P)).then_inc(s_load, 16)
            sp.dma_start(bias[:, :], d["ffn1_bias"].partition_broadcast(P)).then_inc(s_load, 16)
            sp.dma_start(expert_no[:, :], d["expert_no"].partition_broadcast(P)).then_inc(s_load, 16)

        @block.gpsimd
        def _(pool):
            pool.wait_ge(s_load, 80)
            for t in range(TILES):
                pool.tensor_tensor(m.x[:, t, :], m.x[:, t, :], bias[:, :], ALU.add).then_inc(s_bias, 1)

        @block.scalar
        def _(act):
            act.wait_ge(s_load, 80)
            act.activation(wa_hi[:, :, :], wa[:, :, :], ACT.Copy).then_inc(s_whi, 1)
            act.activation(wb_hi[:, :], wb[:, :], ACT.Copy).then_inc(s_whi, 1)
            act.activation(w_hi[:, :, :], w[:, :, :], ACT.Copy).then_inc(s_whi, 1)
            for t in range(TILES):
                act.wait_ge(s_proj, t + 1)
                act.activation(h[:, t, :], proj[t % 2][:, 0:ER], ACT.Copy, scale=SCALING).then_inc(s_h, 1)
                act.wait_ge(s_h, 2 * t + 1)
                act.activation(logit[:, t, :], proj[t % 2][:, ER:NA], ACT.Copy).then_inc(s_h, 1)
            act.wait_ge(s_r, GAP)
            act.activation(ratio[:, :, :], gap[:, :, :], ACT.Exp).then_inc(s_ratio, 1)
            for t in range(TILES):
                act.wait_ge(s_turned, t + 1)
                if t >= 2:
                    act.wait_ge(s_y, t - 1)
                act.activation(hwT_hi[:, t % 2, :], turned[t % 2][:, 0:P], ACT.Copy).then_inc(s_thi, 1)

        @block.vector
        def _(dve):
            step = [0]

            def note(ins):
                ins.then_inc(s_r, 1)
                step[0] += 1

            def settle():
                dve.wait_ge(s_r, step[0])

            for i, (lo, full, hi) in enumerate(((wa_lo, wa, wa_hi), (wb_lo, wb, wb_hi), (w_lo, w, w_hi))):
                dve.wait_ge(s_whi, i + 1)
                dve.tensor_tensor(lo[:], full[:], hi[:].bitcast(F32), ALU.subtract).then_inc(s_wlo, 1)
            dve.wait_ge(s_h, 2 * TILES)
            for t in range(TILES):
                note(dve.max(top1[:, t, :], logit[:, t, :]))
            settle()
            for t in range(TILES):
                note(dve.max_index(at1[:, t, :], top1[:, t, :], logit[:, t, :]))
            settle()
            note(dve.tensor_copy(at1f[:, :, :], at1[:, :, 0:1]))
            settle()
            for t in range(TILES):
                note(dve.tensor_scalar(hot1[:, t, :], expert_no[:, :], at1f[:, t, :], None, ALU.is_equal))
            settle()
            for t in range(TILES):
                note(dve.scalar_tensor_tensor(rest[:, t, :], hot1[:, t, :], -3.0e38, logit[:, t, :],
                                              ALU.mult, ALU.add))
            settle()
            for t in range(TILES):
                note(dve.max(top2[:, t, :], rest[:, t, :]))
            settle()
            for t in range(TILES):
                note(dve.max_index(at2[:, t, :], top2[:, t, :], rest[:, t, :]))
            settle()
            note(dve.tensor_copy(at2f[:, :, :], at2[:, :, 0:1]))
            settle()
            for t in range(TILES):
                note(dve.tensor_scalar(hot2[:, t, :], expert_no[:, :], at2f[:, t, :], None, ALU.is_equal))
            note(dve.tensor_tensor(gap[:, :, :], top2[:, :, 0:1], top1[:, :, 0:1], ALU.subtract))
            assert step[0] == GAP
            settle()
            dve.wait_ge(s_ratio, 1)
            note(dve.tensor_scalar(denom[:, :, :], ratio[:, :, :], 1.0, None, ALU.add))
            settle()
            note(dve.reciprocal(first[:, :, :], denom[:, :, :]))
            settle()
            note(dve.tensor_tensor(second[:, :, :], first[:, :, :], ratio[:, :, :], ALU.mult))
            settle()
            for t in range(TILES):
                note(dve.tensor_scalar(hot1[:, t, :], hot1[:, t, :], first[:, t, :], None, ALU.mult))
            settle()
            for t in range(TILES):
                note(dve.scalar_tensor_tensor(combine[:, t, :], hot2[:, t, :], second[:, t, :], hot1[:, t, :],
                                              ALU.mult, ALU.add))
            settle()
            for t in range(TILES):
                dve.tensor_tensor(hw[:, t, :].rearrange("p (e r) -> p e r", e=EXPERTS),
                                  h[:, t, :].rearrange("p (e r) -> p e r", e=EXPERTS),
                                  combine[:, t, :].unsqueeze(2).broadcast_to([P, EXPERTS, RANK]),
                                  ALU.mult).then_inc(s_hw, 1)

            def add_y(t):
                dve.wait_ge(s_y, t + 1)
                dve.wait_ge(s_bias, t + 1)
                dve.tensor_tensor(m.x[:, t, :], m.x[:, t, :], y[t % 2][:, :], ALU.add).then_inc(s_x, 1)

            for t in range(TILES):
                dve.wait_ge(s_thi, t + 1)
                if t >= 2:
                    dve.wait_ge(s_y, t - 1)
                dve.tensor_tensor(hwT_lo[:, t % 2, :], turned[t % 2][:, 0:P], hwT_hi[:, t % 2, :].bitcast(F32),
                                  ALU.subtract).then_inc(s_tlo, 1)
                if t >= 1:
                    add_y(t - 1)
            add_y(TILES - 1)

        @block.tensor
        def _(pe):
            pe.wait_ge(s_wlo, 1)
            for t in range(TILES):
                if t >= 2:
                    pe.wait_ge(s_h, 2 * (t - 1))
                for k in range(KT):
                    last = mm3(pe, proj[t % 2][:, 0:NA], pair(m.xnT_hi, m.xnT_lo, slice(None), k, bass.ts(t, P)),
                               pair(wa_hi, wa_lo, slice(None), k), start=k == 0, stop=k == KT - 1)
                last.then_inc(s_proj, 1)

            def turn(t):
                pe.wait_ge(s_hw, t + 1)
                if t >= 2:
                    pe.wait_ge(s_tlo, t - 1)
                pe.transpose(turned[t % 2][:, 0:P], hw[:, t, :], m.ident[:, :]).then_inc(s_turned, 1)

            pe.wait_ge(s_wlo, 3)
            for t in range(TILES):
                if t >= 2:
                    pe.wait_ge(s_x, t - 1)
                for k in range(KT):
                    mm3(pe, y[t % 2][:, :], pair(m.xnT_hi, m.xnT_lo, slice(None), k, bass.ts(t, P)),
                        pair(w_hi, w_lo, slice(None), k), start=k == 0, stop=False)
                turn(t)
                pe.wait_ge(s_tlo, t + 1)
                mm3(pe, y[t % 2][:, :], pair(hwT_hi, hwT_lo, slice(None), t % 2), (wb_hi[:, :], wb_lo[:, :]),
                    start=False, stop=True).then_inc(s_y, 1)


HEAD = 8


def done(step):
    return step + (1 + HEAD)


class Units:
    def __init__(self, n, per_turn, fills, together, vdim, causal=True, sum_in_v=False,
                 probs=None, o_sb=None, probsT_odd=None, score_banks=2):
        self.per_turn, self.fills, self.together, self.vdim = per_turn, fills, together, vdim
        self.causal, self.sum_in_v = causal, sum_in_v
        self.per_batch = QT * together
        self.batches = per_turn // self.per_batch
        self.scores = [n.ps(f"scores{i}", [P, SEQ]) for i in range(score_banks)]
        self.turned = [n.ps(f"probsT_ps{i}", [P, QT, P]) for i in range(2)]
        self.out = [n.ps(f"out{i}", [P, QT, P]) for i in range(4 - score_banks)]
        self.negmax = n.sb("negmax", [P, 4])
        if sum_in_v:
            self.recip = n.sb("recip", [P, BATCH, QT, together])
            self.o_sb = n.sb("o_sb", [P, BATCH, QT, P]) if o_sb is None else o_sb
        else:
            self.sum, self.recip = n.sb("sum", [P, 4]), n.sb("recip", [P, 4])
        self.probs = n.sb("probs", [P, 4, SEQ]) if probs is None else probs
        if together == 1:
            self.probsT = n.sb("probsT", [P, 4, QT, P])
        else:
            shape = [P, QT, together, QT, P]
            self.probsT = [n.sb("probsT", shape), n.sb("probsT_odd", shape) if probsT_odd is None else probsT_odd]
        self.s_scores, self.s_max, self.s_exp, self.s_recip, self.s_turned = [
            n.sem(k) for k in ("scores", "max", "exp", "recip", "turned")]
        self.s_scaled = [n.sem("scaled_even"), n.sem("scaled_odd")]
        self.s_copied = [n.sem("copied_even"), n.sem("copied_odd")]
        self.s_pv, self.s_fill, self.s_hi, self.s_lo = [n.sem(k) for k in ("pv", "fill", "outhi", "outlo")]

    def pe_start(self, pe):
        for s in (self.s_scores, self.s_turned, self.s_pv, self.s_fill):
            pe.sem_inc(s, HEAD)

    def dve_start(self, dve):
        for s in (self.s_max, self.s_recip, self.s_scaled[0], self.s_copied[0], self.s_lo):
            dve.sem_inc(s, HEAD)

    def act_start(self, act):
        for s in (self.s_exp, self.s_copied[1], self.s_hi):
            act.sem_inc(s, HEAD)

    def pool_start(self, pool):
        pool.sem_inc(self.s_scaled[1], HEAD)

    def keys(self, qt):
        return qt + 1 if self.causal else QT

    def wait_scores_bank(self, pe, i, u):
        pe.wait_ge(self.s_exp, done(i * self.per_turn + u - len(self.scores)))

    def score(self, pe, m, i, u, qt, q, k_of, mask, mask_by):
        self.wait_scores_bank(pe, i, u)
        width = (qt + 1) * P
        s, k = self.scores[u % len(self.scores)][:, 0:width], k_of(width)
        pe.matmul(s, q[0], k[0], start=True, stop=False)
        pe.matmul(s[:, qt * P:width], mask_by, mask, start=False, stop=False)
        if q[1] is not None:
            pe.matmul(s, q[1], k[0], start=False, stop=False)
        pe.matmul(s, q[0], k[1], start=False, stop=True).then_inc(self.s_scores, 1)

    def turn(self, pe, m, i, u, qt):
        if self.sum_in_v:
            pe.wait_ge(self.s_exp, done(i * self.per_turn + u))
        else:
            pe.wait_ge(self.s_scaled[u % 2], done(i * (self.per_turn // 2) + u // 2))
        pe.wait_ge(self.s_copied[u % 2], done(i * (self.per_turn // 2) + (u // 2 - 1)))
        for k in range(self.keys(qt)):
            last = pe.transpose(self.turned[u % 2][:, k, :], self.probs[:, u % 4, k * P:(k + 1) * P], m.ident[:, :])
        last.then_inc(self.s_turned, 1)

    def times_v(self, pe, i, u, qt, fill, v_of):
        pe.wait_ge(self.s_copied[u % 2], done(i * (self.per_turn // 2) + u // 2))
        if qt == 0:
            pe.wait_ge(self.s_lo, done(i * self.fills + fill - len(self.out)))
        for k in range(self.keys(qt)):
            last = pe.matmul(self.out[fill % len(self.out)][:, qt, :], v_of(k), self.probsT[:, u % 4, k, :], start=k == 0,
                             stop=k == self.keys(qt) - 1)
        last.then_inc(self.s_fill if qt == QT - 1 else self.s_pv, 1)

    def wait_probs(self, pe, i, h):
        for copied in self.s_copied:
            pe.wait_ge(copied, done(i * (self.per_turn // 2) + (h + 1) * (self.per_batch // 2) - 1))

    def times_v_together(self, pe, i, h, fill, v_of):
        self.wait_probs(pe, i, h)
        pe.wait_ge(self.s_lo, done(i * self.fills + fill - len(self.out)))
        for k in range(QT):
            first = k if self.causal else 0
            for e in range(self.together):
                last = pe.matmul(self.out[fill % len(self.out)][e * self.vdim:(e + 1) * self.vdim, first:QT, :].rearrange(
                    "v t q -> v (t q)"), v_of(e, k), self.probsT[h % 2][:, k, e, first:QT, :].rearrange(
                    "p t q -> p (t q)"), start=k == 0, stop=k == QT - 1)
        last.then_inc(self.s_fill, 1)

    def back_to_tokens(self, pe, m, i, b, fill):
        pe.wait_ge(self.s_lo, done(i * self.fills + fill - 1))
        for qt in range(QT):
            last = pe.transpose(self.out[fill % len(self.out)][:, qt, :], self.o_sb[:, b, qt, :], m.ident[:, :])
        last.then_inc(self.s_fill, 1)

    def maximum(self, dve, i, u, qt):
        dve.wait_ge(self.s_scores, done(i * self.per_turn + u))
        dve.wait_ge(self.s_exp, done(i * self.per_turn + u - 4))
        dve.tensor_reduce(self.negmax[:, u % 4:u % 4 + 1], self.scores[u % len(self.scores)][:, 0:self.keys(qt) * P],
                          AX.X, ALU.max, negate=True).then_inc(self.s_max, 1)

    def invert(self, dve, i, u):
        dve.wait_ge(self.s_exp, done(i * self.per_turn + u))
        dve.reciprocal(self.recip[:, u % 4:u % 4 + 1], self.sum[:, u % 4:u % 4 + 1]).then_inc(self.s_recip, 1)

    def scale(self, eng, i, u, qt):
        eng.wait_ge(self.s_recip, done(i * self.per_turn + u))
        p = self.probs[:, u % 4, 0:self.keys(qt) * P]
        recip = self.recip[:, u % 4:u % 4 + 1]
        if u % 2:
            eng.tensor_tensor(p, p, recip.broadcast_to([P, self.keys(qt) * P]), ALU.mult).then_inc(self.s_scaled[1], 1)
        else:
            eng.tensor_scalar(p, p, recip, None, ALU.mult).then_inc(self.s_scaled[0], 1)

    def copy(self, eng, copy, i, u, qt, wait_slot):
        eng.wait_ge(self.s_turned, done(i * self.per_turn + u))
        wait_slot(eng)
        copy(self.slot(u, qt), self.turned[u % 2][:, 0:self.keys(qt), :]).then_inc(self.s_copied[u % 2], 1)

    def slot(self, u, qt):
        if self.together == 1:
            return self.probsT[:, u % 4, 0:self.keys(qt), :]
        return self.probsT[u // self.per_batch % 2][:, 0:self.keys(qt), u % self.together, qt, :]

    def wait_slot(self, eng, i, u, fill):
        turn, h = divmod(u // self.per_batch - 2, self.batches)
        eng.wait_ge(self.s_fill, done(i * self.fills + fill["O", h] + turn * self.fills))

    def lo(self, dve, i, fill, into_lo, into_hi, full):
        dve.wait_ge(self.s_hi, done(i * self.fills + fill))
        dve.tensor_tensor(into_lo, full, into_hi.bitcast(F32), ALU.subtract).then_inc(self.s_lo, 1)

    def output(self, dve, i, b, fill):
        dve.wait_ge(self.s_fill, done(i * self.fills + fill))
        dve.tensor_copy(self.o_sb[:, b, :, :], self.out[fill % len(self.out)][:, :, :]).then_inc(self.s_lo, 1)

    def to_tokens(self, dve, i, b, fill, into):
        dve.wait_ge(self.s_fill, done(i * self.fills + fill))
        dims = self.vdim // 2
        x = self.out[fill % len(self.out)][:, :, :].rearrange("p t (g x) -> p t g x", g=self.together)
        dve.reciprocal(self.recip[:, b, :, :], x[:, :, :, dims]).then_inc(self.s_recip, 1)
        dve.wait_ge(self.s_recip, done(i * BATCH + b))
        dve.tensor_tensor(into.rearrange("p t (g x) -> p t g x", x=dims), x[:, :, :, 0:dims],
                          self.recip[:, b, :, :].unsqueeze(3).broadcast_to([P, QT, self.together, dims]),
                          ALU.mult).then_inc(self.s_lo, 1)

    def exponential(self, act, i, u, qt):
        act.wait_ge(self.s_max, done(i * self.per_turn + u))
        act.wait_ge(self.s_turned, done(i * self.per_turn + u - 4))
        width = self.keys(qt) * P
        into = {} if self.sum_in_v else {"accum_out": self.sum[:, u % 4:u % 4 + 1]}
        act.activation(self.probs[:, u % 4, 0:width], self.scores[u % len(self.scores)][:, 0:width], ACT.Exp,
                       bias=self.negmax[:, u % 4:u % 4 + 1], **into).then_inc(self.s_exp, 1)

    def hi(self, act, i, fill, into_hi, full):
        act.wait_ge(self.s_fill, done(i * self.fills + fill))
        act.activation(into_hi, full, ACT.Copy).then_inc(self.s_hi, 1)


class TwoPassUnits(Units):
    def __init__(self, n, fills, together, vdim, probsT_odd):
        self.fills, self.together, self.vdim, self.causal = fills, together, vdim, False
        self.by_query = [n.ps(f"by_query{i}", [P, SEQ]) for i in range(2)]
        self.by_key = [n.ps(f"by_key{i}", [P, SEQ]) for i in range(2)]
        self.maxT = n.ps("maxT", [P, QT, P])
        self.out = [n.ps("out", [P, QT, P])]
        self.negmax = n.sb("negmax", [P, BATCH, QT, P])
        self.recip = n.sb("recip", [P, BATCH, QT, together])
        self.o_sb = n.sb("o_sb", [P, BATCH, QT, P])
        self.shifted = n.sb("shifted", [P, BATCH, QT, P], F32R)
        self.probsT = [n.sb("probsT", [P, QT, together, QT, P]), probsT_odd]
        self.s_scores, self.s_max, self.s_maxT, self.s_shifted, self.s_by_key, self.s_exp = [
            n.sem(k) for k in ("scores", "max", "maxT", "shifted", "by_key", "exp")]
        self.s_fill, self.s_lo, self.s_recip = [n.sem(k) for k in ("fill", "outlo", "recip")]

    def pe_start(self, pe):
        for s in (self.s_scores, self.s_maxT, self.s_by_key, self.s_fill):
            pe.sem_inc(s, HEAD)

    def dve_start(self, dve):
        for s in (self.s_max, self.s_shifted, self.s_lo, self.s_recip):
            dve.sem_inc(s, HEAD)

    def act_start(self, act):
        act.sem_inc(self.s_exp, HEAD)

    def of(self, i, b, u):
        return i * (BATCH * QT * self.together) + (b * (QT * self.together) + u)

    def score(self, pe, i, b, u, queries, keys):
        pe.wait_ge(self.s_max, done(self.of(i, b, u - 2)))
        pe.matmul(self.by_query[u % 2][:, :], queries, keys, start=True, stop=True).then_inc(self.s_scores, 1)

    def transpose_maxima(self, pe, m, i, b):
        pe.wait_ge(self.s_max, done(self.of(i, b, QT * self.together - 1)))
        pe.wait_ge(self.s_shifted, done(i * BATCH + b - 1))
        for qt in range(QT):
            last = pe.transpose(self.maxT[:, qt, :], self.negmax[:, b, qt, :], m.ident[:, :])
        last.then_inc(self.s_maxT, 1)

    def score_by_key(self, pe, i, b, u, keys, rows):
        if u == 0:
            pe.wait_ge(self.s_shifted, done(i * BATCH + b))
        pe.wait_ge(self.s_exp, done(self.of(i, b, u - 2)))
        pe.matmul(self.by_key[u % 2][:, :], keys, self.shifted[rows, b, :, :].rearrange("p t q -> p (t q)"),
                  start=True, stop=True).then_inc(self.s_by_key, 1)

    def wait_probs(self, pe, i, b):
        pe.wait_ge(self.s_exp, done(self.of(i, b, QT * self.together - 1)))

    def maximum(self, dve, i, b, u, column):
        dve.wait_ge(self.s_scores, done(self.of(i, b, u)))
        dve.tensor_reduce(self.negmax[:, b, u // self.together, column:column + 1], self.by_query[u % 2][:, :],
                          AX.X, ALU.max, negate=True).then_inc(self.s_max, 1)

    def shift(self, dve, i, b, queries):
        dve.wait_ge(self.s_maxT, done(i * BATCH + b))
        dve.tensor_tensor(self.shifted[:, b, :, :].rearrange("p t q -> p (t q)"),
                          self.maxT[:, :, :].rearrange("p t q -> p (t q)"), queries.bitcast(F32),
                          ALU.add).then_inc(self.s_shifted, 1)

    def exponential(self, act, i, b, u, fill):
        act.wait_ge(self.s_by_key, done(self.of(i, b, u)))
        act.wait_ge(self.s_fill, done(i * self.fills + fill - self.fills))
        act.activation(self.probsT[b][:, u // self.together, u % self.together, :, :].rearrange("p t q -> p (t q)"),
                       self.by_key[u % 2][:, :], ACT.Exp).then_inc(self.s_exp, 1)


def project_block(nc, m, d, prefix, w_name, bias_name):
    with ExitStack() as ctx:
        n = Names(nc, ctx, prefix)
        w = n.sb("w", [P, KT, DIM])
        w_hi, w_lo = n.sb("w_hi", [P, KT, DIM], F32R), n.sb("w_lo", [P, KT, DIM], F32R)
        bias = n.sb("bias", [P, DIM])
        turned = [n.ps(f"turned{i}", [P, KT, P]) for i in range(2)]
        y = [n.ps(f"y{i}", [P, DIM]) for i in range(2)]
        s_load, s_whi, s_wlo, s_turned, s_hi, s_lo, s_bias, s_y, s_x = [
            n.sem(k) for k in ("load", "whi", "wlo", "turned", "hi", "lo", "bias", "y", "x")]
        block = ctx.enter_context(nc.Block())

        @block.sync
        def _(sp):
            sp.dma_start(w[:, :, :], d[w_name].rearrange("(k p) o -> p k o", p=P)).then_inc(s_load, 16)
            sp.dma_start(bias[:, :], d[bias_name].partition_broadcast(P)).then_inc(s_load, 16)

        @block.gpsimd
        def _(pool):
            pool.wait_ge(s_load, 32)
            for t in range(TILES):
                pool.tensor_tensor(m.x[:, t, :], m.x[:, t, :], bias[:, :], ALU.add).then_inc(s_bias, 1)

        @block.scalar
        def _(act):
            act.wait_ge(s_load, 32)
            act.activation(w_hi[:, :, :], w[:, :, :], ACT.Copy).then_inc(s_whi, 1)
            for t in range(TILES):
                act.wait_ge(s_turned, t + 1)
                act.activation(m.xnT_hi[:, :, t * P:(t + 1) * P], turned[t % 2][:, :, :],
                               ACT.Copy).then_inc(s_hi, 1)

        @block.vector
        def _(dve):
            dve.wait_ge(s_whi, 1)
            dve.tensor_tensor(w_lo[:, :, :], w[:, :, :], w_hi[:, :, :].bitcast(F32), ALU.subtract).then_inc(s_wlo, 1)

            def add_y(t):
                dve.wait_ge(s_y, t + 1)
                dve.wait_ge(s_bias, t + 1)
                dve.tensor_tensor(m.x[:, t, :], m.x[:, t, :], y[t % 2][:, :], ALU.add).then_inc(s_x, 1)

            for t in range(TILES):
                dve.wait_ge(s_hi, t + 1)
                dve.tensor_tensor(m.xnT_lo[:, :, t * P:(t + 1) * P], turned[t % 2][:, :, :],
                                  m.xnT_hi[:, :, t * P:(t + 1) * P].bitcast(F32), ALU.subtract).then_inc(s_lo, 1)
                if t >= 1:
                    add_y(t - 1)
            add_y(TILES - 1)

        @block.tensor
        def _(pe):
            def turn(t):
                if t >= 2:
                    pe.wait_ge(s_lo, t - 1)
                for k in range(KT):
                    last = pe.transpose(turned[t % 2][:, k, :], m.tok[:, t, k * P:(k + 1) * P], m.ident[:, :])
                last.then_inc(s_turned, 1)

            turn(0)
            pe.wait_ge(s_wlo, 1)
            for t in range(TILES):
                if t + 1 < TILES:
                    turn(t + 1)
                pe.wait_ge(s_lo, t + 1)
                if t >= 2:
                    pe.wait_ge(s_x, t - 1)
                for k in range(KT):
                    last = mm3(pe, y[t % 2][:, :], pair(m.xnT_hi, m.xnT_lo, slice(None), k, bass.ts(t, P)),
                               pair(w_hi, w_lo, slice(None), k), start=k == 0, stop=k == KT - 1)
                last.then_inc(s_y, 1)


def attn0a_block(nc, m, d, prefix):
    QLAT, KVLAT, HD = 12, 4, 16
    ROWS = 3 * KVLAT
    MAX_ROW = ROWS
    TURNS, PER = HEADS // 4, 4 * QT
    N = BATCH * SEQ
    G = 4
    FILL = {s: n for n, s in enumerate([("O", 0), ("T", 0), ("O", 1), ("T", 1)])}
    with ExitStack() as ctx:
        n = Names(nc, ctx, prefix)
        down = n.sb("down", [P, KT, 2 * P])
        down_hi, down_lo = n.sb("down_hi", [P, KT, 2 * P], F32R), n.sb("down_lo", [P, KT, 2 * P], F32R)
        down_bias = n.sb("down_bias", [P, 2])
        wqk = n.sb("wqk", [QLAT + 1, TURNS * P])
        wqk_hi, wqk_lo = n.sb("wqk_hi", [QLAT + 1, TURNS * P], F32R), n.sb("wqk_lo", [QLAT + 1, TURNS * P], F32R)
        wqk_now_hi, wqk_now_lo = n.sb("wqk_now_hi", [QLAT + 1, P], F32R), n.sb("wqk_now_lo", [QLAT + 1, P], F32R)
        wv = n.sb("wv", [P, DIM])
        wv_hi, wv_lo = n.sb("wv_hi", [P, DIM], F32R), n.sb("wv_lo", [P, DIM], F32R)
        bv = n.sb("bv", [P, DIM])
        row_kind = n.sb("row_kind", [P, 4])
        lat = n.sb("lat", [P, 2, N])
        lat_hi, lat_lo = n.sb("lat_hi", [P, N], F32R), n.sb("lat_lo", [P, N], F32R)
        part_hi = n.sb("part_hi", [P, N], F32R)
        part_sel = n.sb("part_sel", [P, N], F32R)
        part_lo = n.sb("part_lo", [P, N])
        keys = n.sb("keys", [P, N], F32R)
        queries = n.sb("queries", [P, N], F32R)
        v_tok = n.sb("v_tok", [P, TILES, DIM])
        v_now = n.sb("v_now", [P, TILES, G, 2 * HD])
        c = TwoPassUnits(n, len(FILL), G, 2 * HD, m.probsT_odd)
        proj = [n.ps(f"proj{i}", [P, SEQ]) for i in range(2)]
        s_load, s_ones, s_hi, s_lo, s_lat, s_latev, s_kmix, s_vps, s_v = [
            n.sem(k) for k in ("load", "ones", "hi", "lo", "lat", "latev", "kmix", "vps", "vready")]
        s_now, s_vnow, s_qps, s_qhi, s_qlo, s_q = [n.sem(k) for k in ("now", "vnow", "qps", "qhi", "qlo", "q")]
        block = ctx.enter_context(nc.Block())
        LOADS = 6

        @block.sync
        def _(sp):
            for dst, name in ((down[:, :, :], "a0_down"), (down_bias[:, :], "a0_down_bias"), (wqk[:, :], "a0_wqk"),
                              (wv[32:32 + KVLAT, :], "a0_wv"), (row_kind[:, :], "a0_row_kind")):
                src = d[name].rearrange("(k p) o -> p k o", p=P) if name == "a0_down" else d[name]
                sp.dma_start(dst, src).then_inc(s_load, 16)
            sp.dma_start(bv[:, :], d["a0_bv"].partition_broadcast(P)).then_inc(s_load, 16)

        @block.gpsimd
        def _(pool):
            pool.memset(v_now[:, :, :, HD:2 * HD], 0.0).then_inc(s_ones, 1)
            pool.wait_ge(s_ones, 1)
            pool.memset(v_now[:, :, :, HD:HD + 1], 1.0).then_inc(s_ones, 1)
            pool.memset(c.negmax[:, :, :, :], 0.0).then_inc(s_ones, 1)
            pool.wait_ge(s_lo, 3)
            pool.sem_inc(s_now, HEAD)
            with pool.Fori(0, TURNS) as i:
                pool.wait_ge(s_qps, 2 * i + HEAD)
                pool.tensor_copy(wqk_now_hi[:, :], wqk_hi[:, bass.ds(i * P, P)].bitcast(F32)).then_inc(s_now, 1)
                pool.tensor_copy(wqk_now_lo[:, :], wqk_lo[:, bass.ds(i * P, P)].bitcast(F32)).then_inc(s_now, 1)
                pool.wait_ge(s_v, TILES)
                pool.wait_ge(c.s_fill, done(i * c.fills + FILL["O", 1] - c.fills))
                pool.tensor_copy(v_now[:, :, :, 0:HD],
                                 v_tok[:, :, bass.ds(i * (G * HD), G * HD)].rearrange("p t (g x) -> p t g x", g=G))\
                    .then_inc(s_vnow, 1)

        @block.scalar
        def _(act):
            act.wait_ge(s_load, 16 * LOADS)
            act.activation(down_hi[:, :, :], down[:, :, :], ACT.Copy).then_inc(s_hi, 1)
            act.activation(wqk_hi[:, :], wqk[:, :], ACT.Copy).then_inc(s_hi, 1)
            act.activation(wv_hi[32:32 + KVLAT, :], wv[32:32 + KVLAT, :], ACT.Copy).then_inc(s_hi, 1)
            for g in range(4):
                act.wait_ge(s_lat, g + 1)
                act.activation(lat[:, g // 2, bass.ts(g % 2, SEQ)], proj[g % 2][:, :], ACT.Identity,
                               bias=down_bias[:, g // 2:g // 2 + 1]).then_inc(s_latev, 1)
            act.wait_ge(s_latev, 4)
            act.activation(lat_hi[:, :], lat[:, 1, :], ACT.Copy).then_inc(s_hi, 1)
            act.activation(part_hi[:, :], lat[:, 0, :], ACT.Copy).then_inc(s_hi, 1)
            act.activation(part_sel[:, :], lat[:, 0, :], ACT.Copy, scale=row_kind[:, 0:1]).then_inc(s_hi, 1)
            act.wait_ge(s_kmix, 2)
            c.act_start(act)
            act.sem_inc(s_qhi, HEAD)

            def split_queries(i):
                for b in range(BATCH):
                    act.wait_ge(s_qps, 2 * i + (b + 1 + HEAD))
                    act.wait_ge(s_q, 2 * i + (b - 1 + HEAD))
                    act.activation(part_hi[:, bass.ts(b, SEQ)], proj[b][:, :], ACT.Copy, scale=0.5).then_inc(s_qhi, 1)
                    act.activation(part_sel[:, bass.ts(b, SEQ)], proj[b][:, :], ACT.Copy,
                                   scale=row_kind[:, 2:3]).then_inc(s_qhi, 1)

            def turn(i, last):
                for b in range(BATCH):
                    for u in range(PER):
                        c.exponential(act, i, b, u, FILL["O", b])
                        if (b, u) == (0, 5) and not last:
                            split_queries(i + 1)

            split_queries(0)
            with act.Fori(0, TURNS - 1) as i:
                turn(i, False)
            turn(TURNS - 1, True)

        @block.vector
        def _(dve):
            for g, (lo, full, hi) in enumerate(((down_lo[:, :, :], down[:, :, :], down_hi[:, :, :]),
                                                (wqk_lo[:, :], wqk[:, :], wqk_hi[:, :]),
                                                (wv_lo[32:32 + KVLAT, :], wv[32:32 + KVLAT, :],
                                                 wv_hi[32:32 + KVLAT, :]))):
                dve.wait_ge(s_hi, g + 1)
                dve.tensor_tensor(lo, full, hi.bitcast(F32), ALU.subtract).then_inc(s_lo, 1)
            dve.wait_ge(s_hi, 4)
            dve.tensor_tensor(lat_lo[:, :], lat[:, 1, :], lat_hi[:, :].bitcast(F32), ALU.subtract).then_inc(s_lo, 1)
            dve.wait_ge(s_hi, 5)
            dve.tensor_tensor(part_lo[:, :], lat[:, 0, :], part_hi[:, :].bitcast(F32),
                              ALU.subtract).then_inc(s_kmix, 1)
            dve.wait_ge(s_kmix, 1)
            dve.wait_ge(s_hi, 6)
            dve.scalar_tensor_tensor(keys[:, :], part_lo[:, :], row_kind[:, 1:2], part_sel[:, :].bitcast(F32),
                                     ALU.mult, ALU.add).then_inc(s_kmix, 1)
            for t in range(TILES):
                dve.wait_ge(s_vps, t + 1)
                dve.tensor_tensor(v_tok[:, t, :], proj[t % 2][:, :], bv[:, :], ALU.add).then_inc(s_v, 1)
            dve.wait_ge(s_kmix, 2)
            c.dve_start(dve)
            dve.sem_inc(s_qlo, HEAD)
            dve.sem_inc(s_q, HEAD)

            def split_queries(i):
                for b in range(BATCH):
                    dve.wait_ge(s_qhi, 4 * i + (2 * b + 2 + HEAD))
                    dve.wait_ge(s_q, 2 * i + (b - 1 + HEAD))
                    dve.scalar_tensor_tensor(part_lo[:, bass.ts(b, SEQ)], proj[b][:, :], 0.5,
                                             part_hi[:, bass.ts(b, SEQ)].bitcast(F32),
                                             ALU.mult, ALU.subtract).then_inc(s_qlo, 1)

            def mix_queries(i, b):
                dve.wait_ge(c.s_shifted, done(i * BATCH + b - 2))
                dve.wait_ge(s_qlo, 2 * i + (b + 1 + HEAD))
                dve.scalar_tensor_tensor(queries[:, bass.ts(b, SEQ)], part_lo[:, bass.ts(b, SEQ)],
                                         row_kind[:, 3:4], part_sel[:, bass.ts(b, SEQ)].bitcast(F32),
                                         ALU.mult, ALU.add).then_inc(s_q, 1)

            def output(i, b):
                c.output(dve, i, b, FILL["O", b])

            def to_tokens(i, b):
                c.to_tokens(dve, i, b, FILL["T", b], m.tok[:, b * QT:(b + 1) * QT, bass.ds(i * (G * HD), G * HD)])

            def turn(i, first, last):
                for b in range(BATCH):
                    before = (i - 1, 1) if b == 0 else (i, 0)
                    after = (i, 1) if b == 0 else (i + 1, 0)
                    c.shift(dve, i, b, queries[:, bass.ts(b, SEQ)])
                    if b == 1 and not last:
                        mix_queries(i + 1, 1)
                    for u in range(PER):
                        if not (last and b == 1):
                            c.maximum(dve, *after, u, MAX_ROW + 32 * (u % G))
                        if u == 4 and not (first and b == 0):
                            output(*before)
                        if u == 7 and not (first and b == 0):
                            to_tokens(*before)
                        if (b, u) == (0, 6) and not last:
                            split_queries(i + 1)
                        if (b, u) == (0, 9) and not last:
                            mix_queries(i + 1, 0)

            dve.wait_ge(s_ones, 3)
            split_queries(0)
            mix_queries(0, 0)
            mix_queries(0, 1)
            for u in range(PER):
                c.maximum(dve, 0, 0, u, MAX_ROW + 32 * (u % G))
            turn(0, True, False)
            with dve.Fori(1, TURNS - 1) as i:
                turn(i, False, False)
            turn(TURNS - 1, False, True)
            output(TURNS - 1, 1)
            to_tokens(TURNS - 1, 1)

        @block.tensor
        def _(pe):
            pe.wait_ge(s_lo, 1)
            for g in range(4):
                if g >= 2:
                    pe.wait_ge(s_latev, g - 1)
                for k in range(KT):
                    last = mm3(pe, proj[g % 2][:, :], pair(down_hi, down_lo, slice(None), k, bass.ts(g // 2, P)),
                               pair(m.xnT_hi, m.xnT_lo, slice(None), k, bass.ts(g % 2, SEQ)),
                               start=k == 0, stop=k == KT - 1)
                last.then_inc(s_lat, 1)
            pe.wait_ge(s_lo, 4)
            pe.wait_ge(s_latev, 4)
            for t in range(TILES):
                if t >= 2:
                    pe.wait_ge(s_v, t - 1)
                mm3(pe, proj[t % 2][:, :], pair(lat_hi, lat_lo, slice(32, 32 + KVLAT), bass.ts(t, P)),
                    pair(wv_hi, wv_lo, slice(32, 32 + KVLAT)), start=True, stop=True).then_inc(s_vps, 1)
            pe.wait_ge(s_v, TILES)
            pe.wait_ge(s_ones, 3)
            c.pe_start(pe)
            pe.sem_inc(s_qps, HEAD)

            def project_queries(i):
                pe.wait_ge(s_now, 2 * i + (2 + HEAD))
                for b in range(BATCH):
                    pe.wait_ge(s_q, 2 * i + (b - 1 + HEAD))
                    mm3(pe, proj[b][:, :], (wqk_now_hi[:, :], wqk_now_lo[:, :]),
                        pair(lat_hi, lat_lo, slice(0, QLAT + 1), bass.ts(b, SEQ)), start=True, stop=True)\
                        .then_inc(s_qps, 1)

            def scores(i, b, u):
                qt, j = divmod(u, G)
                rows = slice(32 * j, 32 * j + ROWS)
                if u == 0:
                    pe.wait_ge(s_q, 2 * i + (b + 1 + HEAD))
                c.score(pe, i, b, u, queries[rows, bass.ts(b * QT + qt, P)], keys[rows, bass.ts(b, SEQ)])

            def scores_by_key(i, b, u):
                kt, j = divmod(u, G)
                rows = slice(32 * j, 32 * j + MAX_ROW + 1)
                c.score_by_key(pe, i, b, u, keys[rows, bass.ts(b * QT + kt, P)], rows)

            def times_v(i, b):
                c.times_v_together(pe, i, b, FILL["O", b], lambda e, k: v_now[:, b * QT + k, e, :])

            def turn(i, first, last):
                for b in range(BATCH):
                    before = (i - 1, 1) if b == 0 else (i, 0)
                    after = (i, 1) if b == 0 else (i + 1, 0)
                    for u in range(PER):
                        scores_by_key(i, b, u)
                        if not (last and b == 1):
                            scores(*after, u)
                        if u == 2 and not (first and b == 0):
                            if b == 1:
                                pe.wait_ge(s_vnow, i + 1)
                            times_v(*before)
                        if u == 6 and not (first and b == 0):
                            c.back_to_tokens(pe, m, *before, FILL["T", before[1]])
                        if (b, u) == (0, 4) and not last:
                            project_queries(i + 1)
                    if not (last and b == 1):
                        c.transpose_maxima(pe, m, *after)

            project_queries(0)
            for u in range(PER):
                scores(0, 0, u)
            c.transpose_maxima(pe, m, 0, 0)
            turn(0, True, False)
            with pe.Fori(1, TURNS - 1) as i:
                turn(i, False, False)
            turn(TURNS - 1, False, True)
            times_v(TURNS - 1, 1)
            c.back_to_tokens(pe, m, TURNS - 1, 1, FILL["T", 1])


def attn0b_block(nc, m, d, prefix):
    G = HEADS // 8
    HD, ROT = 128, 64
    KV = 2 * HD
    UP = KV - ROT
    TURNS, PER = 8, BATCH * G * QT
    STEPS = [("W", k) for k in range(KT)] + [("B", t) for t in range(6)] + [("K", 0), ("B", 6), ("B", 7)]
    STEPS += [("C", 0), ("C", 1), ("K", 1)]
    for t in range(2, TILES):
        STEPS += [("C", t), ("Q", t - 2)]
    STEPS += [("Q", TILES - 2), ("Q", TILES - 1)]
    PROJ = {s: n for n, s in enumerate([s for s in STEPS if s[0] in "WBC"] + [("E", t) for t in range(TILES)])}
    order = sorted(PROJ, key=PROJ.get)
    ROTATED = {s: n for n, s in enumerate([s for s in order if s[0] in "BC"])}
    FREES = {s: n for n, s in enumerate([s for s in order if s[0] in "WE"])}
    FILL = {s: n for n, s in enumerate([s for s in STEPS if s[0] in "KQ"] + [("O", h) for h in range(BATCH * G)])}
    units = [(b, j, qt) for b in range(BATCH) for j in range(G) for qt in range(QT)]
    LAG = 4
    with ExitStack() as ctx:
        n = Names(nc, ctx, prefix)
        down = n.sb("down", [P, KT, DIM])
        down_hi, down_lo = n.sb("down_hi", [P, KT, DIM], F32R), n.sb("down_lo", [P, KT, DIM], F32R)
        up_in, rot_in = n.sb("up_in", [P, KT, UP]), n.sb("rot_in", [P, KT, ROT])
        big_in = down
        up_hi, up_lo = n.sb("up_hi", [P, KT, UP], F32R), n.sb("up_lo", [P, KT, UP], F32R)
        wkv_hi, wkv_lo = n.sb("wkv_hi", [P, KT, KV], F32R), n.sb("wkv_lo", [P, KT, KV], F32R)
        wq_hi, wq_lo = n.sb("wq_hi", [P, KT, DIM], F32R), n.sb("wq_lo", [P, KT, DIM], F32R)
        wo_hi, wo_lo = n.sb("wo_hi", [P, G, DIM], F32R), n.sb("wo_lo", [P, G, DIM], F32R)
        cos_q, sin_q = n.sb("cos_q", [P, QT, HD]), n.sb("sin_q", [P, QT, HD])
        cos_k, sin_k = n.sb("cos_k", [P, QT, ROT]), n.sb("sin_k", [P, QT, ROT])
        part_a, part_b = n.sb("part_a", [P, 2, DIM]), n.sb("part_b", [P, 2, DIM])
        kv_tok = n.sb("kv_tok", [P, TILES, KV])
        q_tok = n.sb("q_tok", [P, 2, DIM])
        kT_hi, kT_lo = n.sb("kT_hi", [P, TILES * P], F32R), n.sb("kT_lo", [P, TILES * P], F32R)
        qT_hi, qT_lo = n.sb("qT_hi", [P, G, TILES * P], F32R), n.sb("qT_lo", [P, G, TILES * P], F32R)
        oT_hi, oT_lo = qT_hi, qT_lo
        c = Units(n, PER, len(FILL), 1, HD)
        proj = [n.ps(f"proj{i}", [P, DIM]) for i in range(2)]
        c.scores.append(proj[1])
        s_down, s_tables, s_small, s_big, s_dhi, s_dlo = [
            n.sem(k) for k in ("down", "tables", "small_in", "big_in", "down_hi", "down_lo")]
        s_shi, s_slo, s_bhi, s_blo = [n.sem(k) for k in ("small_hi", "small_lo", "big_hi", "big_lo")]
        s_proj, s_projfree, s_projhi, s_rope, s_added = [
            n.sem(k) for k in ("proj", "projfree", "projhi", "rope", "added")]
        block = ctx.enter_context(nc.Block())
        NP = len(PROJ)

        def bank(kind, t):
            if kind == "E":
                return t % 2 if t >= QT - 1 else 0
            return PROJ[kind, t] % 2

        @block.sync
        def _(sp):
            sp.dma_start(down[:, :, :], d["b0_down"].rearrange("(k p) o -> p k o", p=P)).then_inc(s_down, 16)
            for dst, name in ((cos_q, "b0_cos_q"), (sin_q, "b0_sin_q"), (cos_k, "b0_cos_k"), (sin_k, "b0_sin_k")):
                sp.dma_start(dst[:, :, :], d[name]).then_inc(s_tables, 16)

            def load(dst, src, i, s):
                sp.dma_start(dst[:, :, :], src[bass.ds(i, 1)].rearrange("g (k p) o -> p (g k) o", p=P)).then_inc(s, 16)

            with sp.Fori(0, TURNS) as i:
                sp.wait_ge(s_slo, 2 * i + 1)
                load(rot_in, d["b0_rot"], i, s_small)
                load(up_in, d["b0_up"], i, s_small)
                sp.wait_ge(s_dlo, 1)
                sp.wait_ge(s_blo, 2 * i + 1)
                load(big_in, d["b0_q"], i, s_big)
                sp.wait_ge(s_blo, 2 * i + 2)
                load(big_in, d["b0_o"], i, s_big)

        def split_small_hi(act, i):
            act.wait_ge(s_small, 32 * i + 32)
            act.activation(wkv_hi[:, :, 0:ROT], rot_in[:, :, :], ACT.Copy).then_inc(s_shi, 1)
            act.activation(up_hi[:, :, :], up_in[:, :, :], ACT.Copy).then_inc(s_shi, 1)

        def split_small_lo(pool, i):
            pool.wait_ge(s_shi, 2 * i + 2)
            pool.tensor_tensor(wkv_lo[:, :, 0:ROT], rot_in[:, :, :], wkv_hi[:, :, 0:ROT].bitcast(F32),
                               ALU.subtract).then_inc(s_slo, 1)
            pool.tensor_tensor(up_lo[:, :, :], up_in[:, :, :], up_hi[:, :, :].bitcast(F32),
                               ALU.subtract).then_inc(s_slo, 1)

        @block.gpsimd
        def _(pool):
            pool.sem_inc(s_added, HEAD)
            c.pool_start(pool)
            pool.sem_inc(s_slo, 1)
            pool.sem_inc(s_blo, 1)

            def prepare(i):
                for kind, t in STEPS:
                    if kind in "BC":
                        pool.wait_ge(s_rope, i * (3 * len(ROTATED)) + 3 * (ROTATED[kind, t] + 1))
                        if kind == "B":
                            pool.tensor_tensor(kv_tok[:, t, 0:ROT], part_a[:, t % 2, 0:ROT], part_b[:, t % 2, 0:ROT],
                                               ALU.add).then_inc(s_added, 1)
                        else:
                            pool.wait_ge(c.s_fill, done(i * c.fills + FILL["Q", 0] + t - 2))
                            pool.tensor_tensor(q_tok[:, t % 2, :], part_a[:, t % 2, :], part_b[:, t % 2, :],
                                               ALU.add).then_inc(s_added, 1)

            def split_big_lo(i, which, hi, lo):
                pool.wait_ge(s_bhi, 2 * i + (which + 1))
                pool.tensor_tensor(lo[:, :, :], big_in[:, :, :], hi[:, :, :].bitcast(F32),
                                   ALU.subtract).then_inc(s_blo, 1)

            def turn(i, last):
                prepare(i)
                for s in range(1, PER, 2):
                    c.scale(pool, i, s, units[s][2])
                    if s == 5:
                        split_big_lo(i, 1, wo_hi, wo_lo)
                    if s == 15 and not last:
                        split_small_lo(pool, i + 1)
                    if s == 21 and not last:
                        split_big_lo(i + 1, 0, wq_hi, wq_lo)

            split_small_lo(pool, 0)
            split_big_lo(0, 0, wq_hi, wq_lo)
            with pool.Fori(0, TURNS - 1) as i:
                turn(i, False)
            turn(TURNS - 1, True)

        def slot_free(eng, i, u):
            q = PER // QT
            batch, r = divmod(u - 4, QT)
            if r == QT - 1:
                last_fill = FILL["O", batch] if batch >= 0 else FILL["O", q + batch] - c.fills
                eng.wait_ge(c.s_fill, done(i * c.fills + last_fill))
            else:
                eng.wait_ge(c.s_pv, i * (q * (QT - 1)) + (batch * (QT - 1) + r + 1 + HEAD))

        def output(eng, i, h, high):
            b, j = divmod(h, G)
            f = FILL["O", h]
            view = lambda x: x[:, j, bass.ts(b, SEQ)].rearrange("p (t q) -> p t q", q=P)
            if high:
                c.hi(eng, i, f, view(oT_hi), c.out[f % 2][:, :, :])
            else:
                c.lo(eng, i, f, view(oT_lo), view(oT_hi), c.out[f % 2][:, :, :])

        @block.scalar
        def _(act):
            def split_big_hi(i, which, hi):
                act.wait_ge(s_big, 32 * i + 16 * (which + 1))
                act.activation(hi[:, :, :], big_in[:, :, :], ACT.Copy).then_inc(s_bhi, 1)

            def prepare(i):
                for kind, t in STEPS:
                    if kind == "W":
                        act.wait_ge(s_proj, i * NP + (PROJ[kind, t] + 1))
                        act.activation(wkv_hi[:, t, ROT:KV], proj[t % 2][:, 0:UP], ACT.Copy).then_inc(s_projhi, 1)
                    elif kind == "B":
                        act.wait_ge(s_proj, i * NP + (PROJ[kind, t] + 1))
                        act.activation(kv_tok[:, t, ROT:KV], proj[t % 2][:, ROT:KV], ACT.Copy).then_inc(s_projhi, 1)
                    elif kind == "K":
                        c.hi(act, i, FILL[kind, t], kT_hi[:, bass.ts(t, SEQ)].rearrange("p (t q) -> p t q", q=P),
                             c.out[FILL[kind, t] % 2][:, :, :])
                    elif kind == "Q":
                        c.hi(act, i, FILL[kind, t], qT_hi[:, :, bass.ts(t, P)], c.out[FILL[kind, t] % 2][:, :, :])

            def turn(i, last):
                prepare(i)
                for s in range(PER + 7):
                    if LAG <= s < PER + LAG and (s - LAG) % 2:
                        c.copy(act, lambda o, x: act.activation(o, x, ACT.Copy), i, s - LAG, units[s - LAG][2],
                               lambda e: slot_free(e, i, s - LAG))
                    if s < PER:
                        c.exponential(act, i, s, units[s][2])
                    if s == 4:
                        act.wait_ge(s_projfree, done(i * len(FREES) - 1))
                        split_big_hi(i, 1, wo_hi)
                    if s == 12 and not last:
                        split_small_hi(act, i + 1)
                    if s == 16 and not last:
                        split_big_hi(i + 1, 0, wq_hi)
                    if s >= 9 and s % QT == 1:
                        output(act, i, s // QT - 2, True)

            act.wait_ge(s_down, 16)
            act.activation(down_hi[:, :, :], down[:, :, :], ACT.Copy).then_inc(s_dhi, 1)
            split_small_hi(act, 0)
            split_big_hi(0, 0, wq_hi)
            c.act_start(act)
            with act.Fori(0, TURNS - 1) as i:
                turn(i, False)
            turn(TURNS - 1, True)

        @block.vector
        def _(dve):
            dve.wait_ge(s_dhi, 1)
            dve.tensor_tensor(down_lo[:, :, :], down[:, :, :], down_hi[:, :, :].bitcast(F32),
                              ALU.subtract).then_inc(s_dlo, 1)
            dve.wait_ge(s_tables, 64)
            c.dve_start(dve)
            dve.sem_inc(s_projfree, HEAD)

            def rotate(i, kind, t, heads, width, cos, sin):
                n_rot = ROTATED[kind, t]
                if kind == "B":
                    dve.wait_ge(s_projhi, i * (KT + TILES) + (KT + t + 1))
                dve.wait_ge(s_added, done(i * len(ROTATED) + n_rot - 2))
                flat = lambda x: x[:, 0:heads * width].rearrange("p (g x) -> p g x", g=heads)
                x, a, b = proj[t % 2], part_a[:, t % 2, :], part_b[:, t % 2, :]
                dve.tensor_tensor(flat(a), flat(x), cos[:, t % QT, :].unsqueeze(1).broadcast_to([P, heads, width]),
                                  ALU.mult).then_inc(s_rope, 1)
                half = lambda y, h: y[:, 0:heads * width].rearrange("p (g r h x) -> p g r h x", g=heads, h=2,
                                                                    x=32)[:, :, :, h, :]
                runs = width // 64
                for h in range(2):
                    table = sin[:, t % QT, :].rearrange("p (r h x) -> p r h x", h=2, x=32)[:, :, h, :]
                    dve.tensor_tensor(half(b, h), half(x, 1 - h),
                                      table.unsqueeze(1).broadcast_to([P, heads, runs, 32]),
                                      ALU.mult).then_inc(s_rope, 1)

            def prepare(i):
                for kind, t in STEPS:
                    if kind in "WBC":
                        dve.wait_ge(s_proj, i * NP + (PROJ[kind, t] + 1))
                    if kind == "W":
                        dve.wait_ge(s_projhi, i * (KT + TILES) + (t + 1))
                        dve.tensor_tensor(wkv_lo[:, t, ROT:KV], proj[t % 2][:, 0:UP],
                                          wkv_hi[:, t, ROT:KV].bitcast(F32), ALU.subtract).then_inc(s_projfree, 1)
                    elif kind == "B":
                        rotate(i, kind, t, 1, ROT, cos_k, sin_k)
                    elif kind == "C":
                        rotate(i, kind, t, G, HD, cos_q, sin_q)
                    elif kind == "K":
                        view = lambda x: x[:, bass.ts(t, SEQ)].rearrange("p (t q) -> p t q", q=P)
                        c.lo(dve, i, FILL[kind, t], view(kT_lo), view(kT_hi), c.out[FILL[kind, t] % 2][:, :, :])
                    elif kind == "Q":
                        c.lo(dve, i, FILL[kind, t], qT_lo[:, :, bass.ts(t, P)], qT_hi[:, :, bass.ts(t, P)],
                             c.out[FILL[kind, t] % 2][:, :, :])

            def add_output(i, t):
                f = PROJ["E", t]
                dve.wait_ge(s_proj, i * NP + (f + 1))
                dve.tensor_tensor(m.x[:, t, :], m.x[:, t, :], proj[bank("E", t)][:, :], ALU.add).then_inc(s_projfree, 1)

            def turn(i):
                prepare(i)
                for s in range(PER + 7):
                    if LAG <= s < PER + LAG and (s - LAG) % 2 == 0:
                        c.copy(dve, dve.tensor_copy, i, s - LAG, units[s - LAG][2],
                               lambda e: slot_free(e, i, s - LAG))
                    if s < PER:
                        c.maximum(dve, i, s, units[s][2])
                    if 1 <= s < PER + 1:
                        c.invert(dve, i, s - 1)
                        if s % 2:
                            c.scale(dve, i, s - 1, units[s - 1][2])
                    if s >= 9 and s % QT == 1:
                        output(dve, i, s // QT - 2, False)
                    if s >= 27 and s % 3 == 0 and (s - 27) // 3 < QT - 1:
                        add_output(i, (s - 27) // 3)
                for t in range(QT - 1, TILES):
                    add_output(i, t)

            with dve.Fori(0, TURNS) as i:
                turn(i)

        @block.tensor
        def _(pe):
            pe.wait_ge(s_dlo, 1)
            c.pe_start(pe)

            def project(i, kind, t, width, lhs, rhs, n_k):
                f = PROJ[kind, t]
                projection_taken(i, f - 1 if kind == "E" and t < QT - 1 else f - 2)
                for k in range(n_k):
                    last = mm3(pe, proj[bank(kind, t)][:, 0:width], lhs(k), rhs(k), start=k == 0, stop=k == n_k - 1)
                last.then_inc(s_proj, 1)

            def projection_taken(i, f):
                back = 1 if f < 0 else 0
                kind, t = order[f % NP]
                if kind in "WE":
                    pe.wait_ge(s_projfree, done(i * len(FREES) + (FREES[kind, t] - back * len(FREES))))
                else:
                    pe.wait_ge(s_rope, i * (3 * len(ROTATED)) + 3 * (ROTATED[kind, t] + 1))

            def prepare(i):
                for kind, t in STEPS:
                    if kind == "W":
                        if t == 0:
                            pe.wait_ge(s_slo, 2 * i + 3)
                        project(i, kind, t, UP, lambda k: pair(down_hi, down_lo, slice(None), k, bass.ts(t, P)),
                                lambda k: pair(up_hi, up_lo, slice(None), k), KT)
                    elif kind == "B":
                        if t == 0:
                            pe.wait_ge(s_projfree, done(i * len(FREES) + FREES["W", KT - 1]))
                        project(i, kind, t, KV, lambda k: pair(m.xnT_hi, m.xnT_lo, slice(None), k, bass.ts(t, P)),
                                lambda k: pair(wkv_hi, wkv_lo, slice(None), k), KT)
                    elif kind == "C":
                        if t == 0:
                            pe.wait_ge(s_blo, 2 * i + 2)
                        project(i, kind, t, DIM, lambda k: pair(m.xnT_hi, m.xnT_lo, slice(None), k, bass.ts(t, P)),
                                lambda k: pair(wq_hi, wq_lo, slice(None), k), KT)
                    else:
                        f = FILL[kind, t]
                        pe.wait_ge(c.s_lo, done(i * c.fills + f - 2))
                        if kind == "K":
                            pe.wait_ge(s_added, done(i * (2 * TILES) + (QT * t + QT - 1)))
                            pe.wait_ge(s_projhi, i * (KT + TILES) + (KT + QT * t + QT))
                            for r in range(QT):
                                last = pe.transpose(c.out[f % 2][:, r, :], kv_tok[:, QT * t + r, 0:HD], m.ident[:, :])
                        else:
                            pe.wait_ge(s_added, done(i * (2 * TILES) + (TILES + t)))
                            for r in range(G):
                                last = pe.transpose(c.out[f % 2][:, r, :], q_tok[:, t % 2, r * HD:(r + 1) * HD],
                                                    m.ident[:, :])
                        last.then_inc(c.s_fill, 1)

            def project_output(i, t):
                if t == 0:
                    pe.wait_ge(s_blo, 2 * i + 3)
                if t % QT == 0:
                    pe.wait_ge(c.s_lo, done(i * c.fills + FILL["O", G * (t // QT) + G - 1]))
                project(i, "E", t, DIM, lambda j: pair(oT_hi, oT_lo, slice(None), j, bass.ts(t, P)),
                        lambda j: pair(wo_hi, wo_lo, slice(None), j), G)

            def turn(i):
                prepare(i)
                for s in range(PER + 5):
                    if s < PER:
                        b, j, qt = units[s]
                        if s == 0:
                            pe.wait_ge(c.s_lo, done(i * c.fills + FILL["Q", TILES - 1]))
                        c.score(pe, m, i, s, qt,
                                pair(qT_hi, qT_lo, slice(None), j, bass.ts(b * QT + qt, P)),
                                lambda w: pair(kT_hi, kT_lo, slice(None), bass.ds(b * SEQ, w)),
                                m.mask[:, 0, :], m.ident16[:, :])
                    if 3 <= s < PER + 3:
                        c.turn(pe, m, i, s - 3, units[s - 3][2])
                    if s >= 5:
                        b, j, qt = units[s - 5]
                        c.times_v(pe, i, s - 5, qt, FILL["O", b * G + j],
                                  lambda k: kv_tok[:, b * QT + k, HD:KV])
                    if s >= 26 and (s - 26) % 3 == 0 and (s - 26) // 3 < QT - 1:
                        project_output(i, (s - 26) // 3)
                for t in range(QT - 1, TILES):
                    project_output(i, t)

            with pe.Fori(0, TURNS) as i:
                turn(i)


def attn1a_block(nc, m, d, prefix):
    G, TURNS = 4, HEADS // 4
    QLORA, LAT, ROT, HD = 192, 64, 64, 128
    Q2 = QLORA - P
    NA = QLORA + LAT + ROT
    RMS_EPS = 1e-6
    PER = BATCH * G * QT
    STEPS = [("W", 0), ("W", 1), ("C", 0), ("C", 1)]
    for t in range(2, TILES):
        STEPS += [("C", t), ("Q", t - 2)] + ([("G", t - 3)] if t in (3, 4) else [])
    STEPS += [("Q", TILES - 2), ("Q", TILES - 1)]
    PROJ = {s: n for n, s in enumerate([s for s in STEPS if s[0] != "Q"] + [("E", t) for t in range(TILES)])}
    order = sorted(PROJ, key=PROJ.get)
    ACTS = {s: n for n, s in enumerate([s for s in order if s[0] in "WCG"])}
    FREES = {s: n for n, s in enumerate([s for s in order if s[0] in "WGE"])}
    FILL = {s: n for n, s in enumerate([("Q", t) for t in range(TILES)] + [("O", h) for h in range(BATCH * 2)])}
    NP = len(PROJ)
    units = [(b, 2 * pr + e, qt) for b in range(BATCH) for pr in range(2) for qt in range(QT) for e in range(2)]
    SCALE = float(1.0 / np.sqrt(np.float32(HD + ROT)))
    LAG = 4
    with ExitStack() as ctx:
        n = Names(nc, ctx, prefix)
        wa = n.sb("wa", [P, KT, NA])
        wa_hi, wa_lo = n.sb("wa_hi", [P, KT, NA], F32R), n.sb("wa_lo", [P, KT, NA], F32R)
        q_norm, kv_norm = n.sb("q_norm", [P, 2]), n.sb("kv_norm", [P, LAT])
        cos_q, sin_q = n.sb("cos_q", [P, QT, ROT]), n.sb("sin_q", [P, QT, ROT])
        cos_k, sin_k = n.sb("cos_k", [P, QT, ROT]), n.sb("sin_k", [P, QT, ROT])
        lat_tok = n.sb("lat_tok", [P, TILES, NA])
        squares = n.sb("squares", [P, 2, QLORA])
        sumsq, meansq = n.sb("sumsq", [P, 2, TILES]), n.sb("meansq", [P, 2, TILES])
        rms, rrms = n.sb("rms", [P, 2, TILES]), n.sb("rrms", [P, 2, TILES])
        wn_in, wk_in = n.sb("wn_in", [P, G, QLORA]), n.sb("wk_in", [P, G, LAT])
        wr_in = n.sb("wr_in", [P, 2, G, ROT])
        wv_in, wo_in = n.sb("wv_in", [P, G, LAT]), n.sb("wo_in", [P, G, DIM])
        wq_hi, wq_lo = n.sb("wq_hi", [P, 2, G, HD], F32R), n.sb("wq_lo", [P, 2, G, HD], F32R)
        wo_hi, wo_lo = n.sb("wo_hi", [P, 2, DIM], F32R), n.sb("wo_lo", [P, 2, DIM], F32R)
        part_a, part_b = n.sb("part_a", [P, 2, G * ROT]), n.sb("part_b", [P, 2, G * ROT])
        q_tok = n.sb("q_tok", [P, 2, G, HD])
        qT_hi, qT_lo = n.sb("qT_hi", [P, G, TILES * P], F32R), n.sb("qT_lo", [P, G, TILES * P], F32R)
        c = Units(n, PER, len(FILL), 2, LAT)
        proj = [n.ps(f"proj{i}", [P, DIM]) for i in range(2)]
        c.scores.append(proj[1])
        latT_hi, latT_lo = m.xnT_hi, m.xnT_lo
        s_wa, s_tables, s_wahi, s_walo, s_a, s_acopy, s_sq, s_ms, s_rms, s_rrms, s_ln, s_krot, s_kadd, s_lat, s_lhi, \
            s_llo = [n.sem(k) for k in ("wa", "tables", "wahi", "walo", "a", "acopy", "sq", "ms", "rms", "rrms",
                                        "ln", "krot", "kadd", "lat", "lhi", "llo")]
        s_in, s_rhi, s_rlo, s_proj, s_projhi, s_free, s_rope, s_added = [
            n.sem(k) for k in ("in", "rhi", "rlo", "proj", "projhi", "free", "rope", "added")]
        block = ctx.enter_context(nc.Block())
        IN = 6

        def half(y, heads, h):
            return y.rearrange("p (g h x) -> p g h x", g=heads, h=2)[:, :, h, :]

        def bank(kind, t):
            if kind == "E":
                return t % 2 if t >= QT - 1 else 0
            return PROJ[kind, t] % 2

        @block.sync
        def _(sp):
            sp.dma_start(wa[:, :, :], d["b1_down"].rearrange("(k p) o -> p k o", p=P)).then_inc(s_wa, 16)
            for dst, name in ((cos_q, "b1_cos_q"), (sin_q, "b1_sin_q"), (cos_k, "b1_cos_k"), (sin_k, "b1_sin_k")):
                sp.dma_start(dst[:, :, :], d[name]).then_inc(s_tables, 16)
            sp.dma_start(q_norm[:, :], d["b1_q_norm"]).then_inc(s_tables, 16)
            sp.dma_start(kv_norm[:, :], d["b1_kv_norm"].partition_broadcast(P)).then_inc(s_tables, 16)
            with sp.Fori(0, TURNS) as i:
                sp.wait_ge(s_free, done(i * len(FREES) + FREES["G", 1] - len(FREES)))
                sp.wait_ge(s_rlo, 2 * i + 1)
                one = bass.ds(i, 1)
                for dst, name in ((wn_in, "b1_qn"), (wk_in, "b1_k"), (wv_in, "b1_v"), (wo_in, "b1_o")):
                    sp.dma_start(dst[:, :, :], d[name][one].rearrange("g p j o -> p (g j) o")).then_inc(s_in, 16)
                sp.dma_start(wr_in[:, 0, :, :], d["b1_qr"][one, 0:P].rearrange("g p j o -> p (g j) o"))\
                    .then_inc(s_in, 16)
                sp.dma_start(wr_in[0:Q2, 1, :, :], d["b1_qr"][one, P:QLORA].rearrange("g p j o -> p (g j) o"))\
                    .then_inc(s_in, 16)

        @block.gpsimd
        def _(pool):
            pool.sem_inc(s_added, HEAD)
            c.pool_start(pool)
            for t in range(TILES):
                pool.wait_ge(s_krot, 3 * t + 3)
                pool.tensor_tensor(lat_tok[:, t, QLORA + LAT:NA], part_a[:, t % 2, 0:ROT], part_b[:, t % 2, 0:ROT],
                                   ALU.add).then_inc(s_kadd, 1)
            with pool.Fori(0, TURNS) as i:
                for t in range(TILES):
                    pool.wait_ge(s_rope, i * (3 * TILES) + 3 * (t + 1))
                    pool.wait_ge(c.s_fill, done(i * c.fills + FILL["Q", 0] + t - 2))
                    pool.tensor_tensor(q_tok[:, t % 2, :, HD - ROT:HD],
                                       part_a[:, t % 2, :].rearrange("p (g x) -> p g x", g=G),
                                       part_b[:, t % 2, :].rearrange("p (g x) -> p g x", g=G),
                                       ALU.add).then_inc(s_added, 1)
                for s in range(1, PER, 2):
                    c.scale(pool, i, s, units[s][2])

        def out_view(x, h):
            b, pr = divmod(h, 2)
            return x[:, 2 * pr, bass.ts(b, SEQ)].rearrange("p (t q) -> p t q", q=P)

        @block.scalar
        def _(act):
            act.wait_ge(s_wa, 16)
            act.activation(wa_hi[:, :, :], wa[:, :, :], ACT.Copy).then_inc(s_wahi, 1)
            for t in range(TILES):
                act.wait_ge(s_a, t + 1)
                act.activation(lat_tok[:, t, :], proj[t % 2][:, 0:NA], ACT.Copy).then_inc(s_acopy, 1)
                act.wait_ge(s_acopy, t + 1)
                if t >= 1:
                    act.wait_ge(s_sq, 2 * t)
                act.activation(squares[:, 0, :], lat_tok[:, t, 0:QLORA], ACT.Square,
                               accum_out=sumsq[:, 0, t:t + 1]).then_inc(s_sq, 1)
                act.activation(squares[:, 1, 0:LAT], lat_tok[:, t, QLORA:QLORA + LAT], ACT.Square,
                               accum_out=sumsq[:, 1, t:t + 1]).then_inc(s_sq, 1)
            act.wait_ge(s_ms, 2)
            act.activation(rms[:, :, :], meansq[:, :, :], ACT.Sqrt).then_inc(s_rms, 1)
            for t in range(TILES):
                act.wait_ge(s_lat, t + 1)
                act.activation(latT_hi[:, 0:3, bass.ts(t, P)], c.out[t % 2][:, 0:3, :], ACT.Copy).then_inc(s_lhi, 1)
            c.act_start(act)

            def split_rotary(i):
                act.wait_ge(s_in, i * (16 * IN) + 16 * IN)
                for k, rows in ((0, P), (1, Q2)):
                    act.activation(wq_hi[0:rows, k, :, LAT:HD], wr_in[0:rows, k, :, :], ACT.Copy,
                                   scale=q_norm[0:rows, k:k + 1]).then_inc(s_rhi, 1)

            with act.Fori(0, TURNS) as i:
                split_rotary(i)
                for kind, t in STEPS:
                    if kind != "Q":
                        f = PROJ[kind, t]
                        act.wait_ge(s_proj, i * NP + (f + 1))
                    if kind == "W":
                        rows = (P, Q2)[t]
                        act.activation(wq_hi[0:rows, t, :, 0:LAT], proj[f % 2][0:rows, 0:G * LAT].rearrange(
                            "p (g x) -> p g x", g=G), ACT.Copy, scale=q_norm[0:rows, t:t + 1]).then_inc(s_projhi, 1)
                    elif kind == "G":
                        act.activation(wo_hi[:, t, :], proj[f % 2][:, :], ACT.Copy).then_inc(s_projhi, 1)
                    elif kind == "C":
                        act.wait_ge(c.s_fill, done(i * c.fills + FILL["Q", 0] + t - 2))
                        act.activation(q_tok[:, t % 2, :, 0:LAT], proj[f % 2][:, :].rearrange(
                            "p (g x) -> p g x", g=G)[:, :, 0:LAT], ACT.Copy, scale=SCALE).then_inc(s_projhi, 1)
                    else:
                        c.hi(act, i, FILL[kind, t], qT_hi[:, :, bass.ts(t, P)], c.out[FILL[kind, t] % 2][:, :, :])
                for s in range(PER + 7):
                    if LAG <= s < PER + LAG and (s - LAG) % 2:
                        c.copy(act, lambda o, x: act.activation(o, x, ACT.Copy), i, s - LAG, units[s - LAG][2],
                               lambda e: c.wait_slot(e, i, s - LAG, FILL))
                    if s < PER:
                        c.exponential(act, i, s, units[s][2])
                    if s >= 14 and (s - 14) % 8 == 0:
                        h = (s - 14) // 8
                        c.hi(act, i, FILL["O", h], out_view(qT_hi, h), c.out[FILL["O", h] % 2][:, :, :])

        @block.vector
        def _(dve):
            dve.wait_ge(s_wahi, 1)
            dve.tensor_tensor(wa_lo[:, :, :], wa[:, :, :], wa_hi[:, :, :].bitcast(F32), ALU.subtract).then_inc(s_walo, 1)
            dve.wait_ge(s_tables, 96)
            dve.wait_ge(s_sq, 2 * TILES)
            for k, size in ((0, QLORA), (1, LAT)):
                dve.tensor_scalar(meansq[:, k, :], sumsq[:, k, :], 1.0 / size, RMS_EPS, ALU.mult,
                                  ALU.add).then_inc(s_ms, 1)
            dve.wait_ge(s_rms, 1)
            dve.reciprocal(rrms[:, :, :], rms[:, :, :]).then_inc(s_rrms, 1)
            dve.wait_ge(s_rrms, 1)

            def rotate_key(t):
                x, a, b = lat_tok[:, t, QLORA + LAT:NA], part_a[:, t % 2, 0:ROT], part_b[:, t % 2, 0:ROT]
                if t >= 2:
                    dve.wait_ge(s_kadd, t - 1)
                dve.tensor_tensor(a, x, cos_k[:, t % QT, :], ALU.mult).then_inc(s_krot, 1)
                for h in range(2):
                    dve.tensor_tensor(half(b, 1, h), half(x, 1, 1 - h), half(sin_k[:, t % QT, :], 1, h),
                                      ALU.mult).then_inc(s_krot, 1)

            def transposed_lo(t):
                dve.wait_ge(s_lhi, t + 1)
                dve.tensor_tensor(latT_lo[:, 0:3, bass.ts(t, P)], c.out[t % 2][:, 0:3, :],
                                  latT_hi[:, 0:3, bass.ts(t, P)].bitcast(F32), ALU.subtract).then_inc(s_llo, 1)

            for t in range(TILES):
                dve.tensor_scalar(lat_tok[:, t, 0:QLORA], lat_tok[:, t, 0:QLORA], rrms[:, 0, t:t + 1], None,
                                  ALU.mult).then_inc(s_ln, 1)
                dve.scalar_tensor_tensor(lat_tok[:, t, QLORA:QLORA + LAT], lat_tok[:, t, QLORA:QLORA + LAT],
                                         rrms[:, 1, t:t + 1], kv_norm[:, :], ALU.mult, ALU.mult).then_inc(s_ln, 1)
                rotate_key(t)
                if t >= 1:
                    transposed_lo(t - 1)
            transposed_lo(TILES - 1)
            c.dve_start(dve)
            dve.sem_inc(s_free, HEAD)
            dve.sem_inc(s_rlo, 1)

            def rotate(i, t):
                f = PROJ["C", t]
                dve.wait_ge(s_projhi, i * len(ACTS) + (ACTS["C", t] + 1))
                dve.wait_ge(s_added, done(i * TILES + t - 2))
                x = proj[f % 2][:, :].rearrange("p (g x) -> p g x", g=G)[:, :, LAT:HD]
                a, b = part_a[:, t % 2, :], part_b[:, t % 2, :]
                dve.tensor_tensor(a.rearrange("p (g x) -> p g x", g=G), x,
                                  cos_q[:, t % QT, :].unsqueeze(1).broadcast_to([P, G, ROT]),
                                  ALU.mult).then_inc(s_rope, 1)
                for h in range(2):
                    dve.tensor_tensor(half(b, G, h), x[:, :, (1 - h) * 32:(2 - h) * 32],
                                      sin_q[:, t % QT, h * 32:h * 32 + 32].unsqueeze(1).broadcast_to([P, G, 32]),
                                      ALU.mult).then_inc(s_rope, 1)

            def add_output(i, t):
                f = PROJ["E", t]
                dve.wait_ge(s_proj, i * NP + (f + 1))
                dve.tensor_tensor(m.x[:, t, :], m.x[:, t, :], proj[bank("E", t)][:, :], ALU.add).then_inc(s_free, 1)

            with dve.Fori(0, TURNS) as i:
                dve.wait_ge(s_rhi, 2 * i + 2)
                for k, rows in ((0, P), (1, Q2)):
                    dve.scalar_tensor_tensor(wq_lo[0:rows, k, :, LAT:HD], wr_in[0:rows, k, :, :],
                                             q_norm[0:rows, k:k + 1], wq_hi[0:rows, k, :, LAT:HD].bitcast(F32),
                                             ALU.mult, ALU.subtract).then_inc(s_rlo, 1)
                for kind, t in STEPS:
                    if kind == "C":
                        rotate(i, t)
                    elif kind == "Q":
                        c.lo(dve, i, FILL[kind, t], qT_lo[:, :, bass.ts(t, P)], qT_hi[:, :, bass.ts(t, P)],
                             c.out[FILL[kind, t] % 2][:, :, :])
                    else:
                        f = PROJ[kind, t]
                        dve.wait_ge(s_projhi, i * len(ACTS) + (ACTS[kind, t] + 1))
                        if kind == "W":
                            rows = (P, Q2)[t]
                            dve.scalar_tensor_tensor(
                                wq_lo[0:rows, t, :, 0:LAT],
                                proj[f % 2][0:rows, 0:G * LAT].rearrange("p (g x) -> p g x", g=G),
                                q_norm[0:rows, t:t + 1], wq_hi[0:rows, t, :, 0:LAT].bitcast(F32),
                                ALU.mult, ALU.subtract).then_inc(s_free, 1)
                        else:
                            dve.tensor_tensor(wo_lo[:, t, :], proj[f % 2][:, :], wo_hi[:, t, :].bitcast(F32),
                                              ALU.subtract).then_inc(s_free, 1)
                for s in range(PER + 7):
                    if LAG <= s < PER + LAG and (s - LAG) % 2 == 0:
                        c.copy(dve, dve.tensor_copy, i, s - LAG, units[s - LAG][2],
                               lambda e: c.wait_slot(e, i, s - LAG, FILL))
                    if s < PER:
                        c.maximum(dve, i, s, units[s][2])
                    if 1 <= s < PER + 1:
                        c.invert(dve, i, s - 1)
                        if s % 2:
                            c.scale(dve, i, s - 1, units[s - 1][2])
                    if s >= 14 and (s - 14) % 8 == 0:
                        h = (s - 14) // 8
                        c.lo(dve, i, FILL["O", h], out_view(qT_lo, h), out_view(qT_hi, h),
                             c.out[FILL["O", h] % 2][:, :, :])
                    if s >= 27 and s % 3 == 0 and (s - 27) // 3 < QT - 1:
                        add_output(i, (s - 27) // 3)
                for t in range(QT - 1, TILES):
                    add_output(i, t)

        @block.tensor
        def _(pe):
            pe.wait_ge(s_walo, 1)
            for t in range(TILES):
                if t >= 2:
                    pe.wait_ge(s_acopy, t - 1)
                for k in range(KT):
                    last = mm3(pe, proj[t % 2][:, 0:NA], pair(m.xnT_hi, m.xnT_lo, slice(None), k, bass.ts(t, P)),
                               pair(wa_hi, wa_lo, slice(None), k), start=k == 0, stop=k == KT - 1)
                last.then_inc(s_a, 1)
            for t in range(TILES):
                pe.wait_ge(s_ln, 2 * t + 2)
                pe.wait_ge(s_kadd, t + 1)
                if t >= 2:
                    pe.wait_ge(s_llo, t - 1)
                for r, at in enumerate((0, P, QLORA)):
                    last = pe.transpose(c.out[t % 2][:, r, :], lat_tok[:, t, at:at + P], m.ident[:, :])
                last.then_inc(s_lat, 1)
            pe.wait_ge(s_llo, TILES)
            c.pe_start(pe)

            def bank_taken(i, f):
                back = len(FREES) if f < 0 else 0
                kind, t = order[f % NP]
                if kind == "C":
                    pe.wait_ge(s_rope, i * (3 * TILES) + 3 * (t + 1))
                else:
                    pe.wait_ge(s_free, done(i * len(FREES) + (FREES[kind, t] - back)))

            def project(i, kind, t, rows):
                f = PROJ[kind, t]
                bank_taken(i, f - 1 if kind == "E" and t < QT - 1 else f - 2)
                for k, (lhs, rhs) in enumerate(rows):
                    last = mm3(pe, proj[bank(kind, t)][:, :], lhs, rhs, start=k == 0, stop=k == len(rows) - 1)
                last.then_inc(s_proj, 1)

            def project_output(i, t):
                if t % QT == 0:
                    pe.wait_ge(c.s_lo, done(i * c.fills + FILL["O", 2 * (t // QT) + 1]))
                project(i, "E", t, [(pair(qT_hi, qT_lo, slice(None), 2 * p, bass.ts(t, P)),
                                     pair(wo_hi, wo_lo, slice(None), p)) for p in range(2)])

            with pe.Fori(0, TURNS) as i:
                pe.wait_ge(s_in, i * (16 * IN) + 16 * IN)
                for kind, t in STEPS:
                    if kind == "W":
                        f = PROJ[kind, t]
                        bank_taken(i, f - 2)
                        rows = (P, Q2)[t]
                        for j in range(G):
                            last = pe.matmul(proj[f % 2][0:rows, j * LAT:(j + 1) * LAT],
                                             wn_in[:, j, t * P:t * P + rows], wk_in[:, j, :], start=True, stop=True)
                        last.then_inc(s_proj, 1)
                    elif kind == "G":
                        f = PROJ[kind, t]
                        bank_taken(i, f - 2)
                        for e in range(2):
                            last = pe.matmul(proj[f % 2][e * LAT:(e + 1) * LAT, :], wv_in[:, 2 * t + e, :],
                                             wo_in[:, 2 * t + e, :], start=True, stop=True)
                        last.then_inc(s_proj, 1)
                    elif kind == "C":
                        if t == 0:
                            pe.wait_ge(s_free, done(i * len(FREES) + FREES["W", 1]))
                            pe.wait_ge(s_rlo, 2 * i + 3)
                        project(i, kind, t, [
                            (pair(latT_hi, latT_lo, slice(0, rows), k, bass.ts(t, P)),
                             (wq_hi[0:rows, k, :, :].rearrange("p g x -> p (g x)"),
                              wq_lo[0:rows, k, :, :].rearrange("p g x -> p (g x)")))
                            for k, rows in ((0, P), (1, Q2))])
                    else:
                        f = FILL[kind, t]
                        pe.wait_ge(c.s_lo, done(i * c.fills + f - 2))
                        pe.wait_ge(s_projhi, i * len(ACTS) + (ACTS["C", t] + 1))
                        pe.wait_ge(s_added, done(i * TILES + t))
                        for r in range(G):
                            last = pe.transpose(c.out[f % 2][:, r, :], q_tok[:, t % 2, r, :], m.ident[:, :])
                        last.then_inc(c.s_fill, 1)
                for s in range(PER + 6):
                    if s < PER:
                        b, j, qt = units[s]
                        if s == 0:
                            pe.wait_ge(c.s_lo, done(i * c.fills + FILL["Q", TILES - 1]))
                        c.score(pe, m, i, s, qt, pair(qT_hi, qT_lo, slice(None), j, bass.ts(b * QT + qt, P)),
                                lambda w: pair(latT_hi, latT_lo, slice(None), 2, bass.ds(b * SEQ, w)),
                                m.mask[:, 0, :], m.ident16[:, :])
                    if 3 <= s < PER + 3:
                        c.turn(pe, m, i, s - 3, units[s - 3][2])
                    if s >= 13 and (s - 13) % 8 == 0:
                        h = (s - 13) // 8
                        c.times_v_together(pe, i, h, FILL["O", h],
                                           lambda e, k: lat_tok[:, h // 2 * QT + k, QLORA:QLORA + LAT])
                    if s >= 26 and (s - 26) % 3 == 0 and (s - 26) // 3 < QT - 1:
                        project_output(i, (s - 26) // 3)
                for t in range(QT - 1, TILES):
                    project_output(i, t)


def attn1b_block(nc, m, d, prefix):
    G, TURNS, HD = 4, HEADS // 4, 16
    PER = BATCH * QT * G
    THIRDS = 3
    units = [(b, qt, j) for b in range(BATCH) for qt in range(QT) for j in range(G)]
    FILL = {s: n for n, s in enumerate([("K", 0), ("Q", 0), ("K", 1), ("Q", 1), ("O", 0), ("T", 0), ("O", 1),
                                        ("T", 1)])}
    LAG = 4
    with ExitStack() as ctx:
        n = Names(nc, ctx, prefix)
        w_in = n.sb("w_in", [P, KT, DIM])
        w_hi = n.early("w_hi", [P, KT, DIM], F32R)
        o_sb, q_part_lo = n.sb("o_sb", [P, BATCH, QT, P]), n.sb("q_part_lo", [P, TILES, P])
        w_lo = n.sb("w_lo", [P, KT, DIM], F32R)
        bias = n.sb("bias", [P, THIRDS * DIM])
        cos_sin = n.sb("cos_sin", [P, 2, QT, 3, HD // 2])
        row_kind = n.sb("row_kind", [P, 2])
        ident408 = n.sb("ident408", [P, P], BF16)
        raw = n.sb("raw", [P, 2, DIM])
        part_a, part_b = n.sb("part_a", [P, 2, DIM]), n.sb("part_b", [P, 2, DIM])
        k_tok, v_tok = n.sb("k_tok", [P, TILES, DIM]), n.sb("v_tok", [P, TILES, DIM])
        twice = {"Q": n.sb("q_twice", [P, TILES, G, 2, HD]), "K": n.sb("k_twice", [P, TILES, G, 2, HD])}
        v_now = n.sb("v_now", [P, TILES, G, 2 * HD])
        q_part_hi, q_part_sel = n.sb("q_part_hi", [P, TILES, P], F32R), n.sb("q_part_sel", [P, TILES, P], F32R)
        q_mixed = n.sb("q_mixed", [P, TILES, P], F32R)
        kT_hi, kT_lo = n.sb("kT_hi", [P, TILES, P], F32R), n.sb("kT_lo", [P, TILES, P], F32R)
        c = Units(n, PER, len(FILL), G, 2 * HD, sum_in_v=True, probs=w_in, o_sb=o_sb, probsT_odd=m.probsT_odd)
        proj = [n.ps(f"proj{i}", [P, DIM]) for i in range(2)]
        c.scores += proj
        s_load, s_w, s_whi, s_wlo, s_proj, s_raw, s_rope, s_tok, s_zero, s_vnow = [
            n.sem(k) for k in ("load", "w", "whi", "wlo", "proj", "raw", "rope", "tok", "zero", "vnow")]
        s_twice, s_split, s_mixed = [n.sem(k) for k in ("twice", "split", "mixed")]
        block = ctx.enter_context(nc.Block())

        @block.sync
        def _(sp):
            for dst, name in ((cos_sin[:, :, :, :, :], "c1_cos_sin"), (row_kind[:, :], "c1_row_kind"),
                              (ident408[:, :].bitcast(U16), "ident408")):
                sp.dma_start(dst, d[name]).then_inc(s_load, 16)
            sp.dma_start(bias[:, :], d["c1_bias"].partition_broadcast(P)).then_inc(s_load, 16)
            for third in range(THIRDS):
                if third:
                    sp.wait_ge(s_wlo, third)
                sp.dma_start(w_in[:, :, :], d["c1_w"][third].rearrange("(k p) o -> p k o", p=P)).then_inc(s_w, 16)

        @block.gpsimd
        def _(pool):
            pool.memset(v_now[:, :, :, HD:2 * HD], 0.0).then_inc(s_zero, 1)
            pool.wait_ge(s_zero, 1)
            pool.memset(v_now[:, :, :, HD:HD + 1], 1.0).then_inc(s_zero, 1)
            for n_rot in range(2 * TILES):
                third, t = divmod(n_rot, TILES)
                into = (m.tok, k_tok)[third]
                pool.wait_ge(s_rope, 3 * n_rot + 3)
                pool.tensor_tensor(into[:, t, :], part_a[:, n_rot % 2, :], part_b[:, n_rot % 2, :],
                                   ALU.add).then_inc(s_tok, 1)
            pool.wait_ge(s_tok, 2 * TILES)
            pool.wait_ge(s_raw, 3 * TILES)
            pool.sem_inc(s_twice, HEAD)
            with pool.Fori(0, TURNS) as i:
                columns = bass.ds(i * (G * HD), G * HD)
                for kind, src in (("K", k_tok), ("Q", m.tok)):
                    pool.wait_ge(c.s_fill, done(i * c.fills + FILL[kind, 1] - c.fills))
                    for copy in range(2):
                        pool.tensor_copy(twice[kind][:, :, :, copy, :],
                                         src[:, :, columns].rearrange("p t (g x) -> p t g x", g=G))\
                            .then_inc(s_twice, 1)
                pool.wait_ge(c.s_fill, done(i * c.fills + FILL["O", 1] - c.fills))
                pool.tensor_copy(v_now[:, :, :, 0:HD],
                                 v_tok[:, :, columns].rearrange("p t (g x) -> p t g x", g=G)).then_inc(s_vnow, 1)

        SPLITS = [("K", 0), ("Qhi", 0), ("Qsel", 0), ("K", 1), ("Qhi", 1), ("Qsel", 1)]

        @block.scalar
        def _(act):
            for third in range(THIRDS):
                act.wait_ge(s_w, 16 * (third + 1))
                if third:
                    act.wait_ge(s_proj, TILES * third)
                act.activation(w_hi[:, :, :], w_in[:, :, :], ACT.Copy).then_inc(s_whi, 1)
            c.act_start(act)
            with act.Fori(0, TURNS) as i:
                for b in range(BATCH):
                    tiles = slice(b * QT, (b + 1) * QT)
                    k_bank, q_bank = c.out[FILL["K", b] % 2], c.out[FILL["Q", b] % 2]
                    act.wait_ge(c.s_fill, done(i * c.fills + FILL["K", b]))
                    act.activation(kT_hi[:, tiles, :], k_bank[:, :, :], ACT.Copy).then_inc(s_split, 1)
                    act.wait_ge(c.s_fill, done(i * c.fills + FILL["Q", b]))
                    act.activation(q_part_hi[:, tiles, :], q_bank[:, :, :], ACT.Copy).then_inc(s_split, 1)
                    act.activation(q_part_sel[:, tiles, :], q_bank[:, :, :], ACT.Copy,
                                   scale=row_kind[:, 0:1]).then_inc(s_split, 1)
                for s in range(PER + LAG):
                    if s >= LAG and (s - LAG) % 2:
                        c.copy(act, lambda o, x: act.activation(o, x, ACT.Copy), i, s - LAG, units[s - LAG][1],
                               lambda e: c.wait_slot(e, i, s - LAG, FILL))
                    if s < PER:
                        c.exponential(act, i, s, units[s][1])

        @block.vector
        def _(dve):
            dve.wait_ge(s_load, 64)

            def split_weights(third):
                dve.wait_ge(s_whi, third + 1)
                dve.tensor_tensor(w_lo[:, :, :], w_in[:, :, :], w_hi[:, :, :].bitcast(F32),
                                  ALU.subtract).then_inc(s_wlo, 1)

            def take(step):
                third, t = divmod(step, TILES)
                dve.wait_ge(s_proj, step + 1)
                into = v_tok[:, t, :] if third == 2 else raw[:, step % 2, :]
                dve.tensor_tensor(into, proj[step % 2][:, :], bias[:, bass.ts(third, DIM)], ALU.add).then_inc(s_raw, 1)
                if third == 2:
                    return
                if step >= 2:
                    dve.wait_ge(s_tok, step - 1)
                dve.wait_ge(s_raw, step + 1)
                x, a, b = raw[:, step % 2, :], part_a[:, step % 2, :], part_b[:, step % 2, :]
                table = cos_sin[:, third, t % QT, :, :]
                dve.tensor_tensor(a.rearrange("p (g x) -> p g x", x=HD // 2), x.rearrange("p (g x) -> p g x", x=HD // 2),
                                  table[:, 0, :].unsqueeze(1).broadcast_to([P, 2 * HEADS, HD // 2]),
                                  ALU.mult).then_inc(s_rope, 1)
                halves = lambda y, h: y.rearrange("p (g h x) -> p g h x", h=2, x=HD // 2)[:, :, h, :]
                for h in range(2):
                    dve.tensor_tensor(halves(b, h), halves(x, 1 - h),
                                      table[:, 1 + h, :].unsqueeze(1).broadcast_to([P, HEADS, HD // 2]),
                                      ALU.mult).then_inc(s_rope, 1)

            for third in range(THIRDS):
                split_weights(third)
                for t in range(TILES):
                    take(third * TILES + t)
            c.dve_start(dve)

            with dve.Fori(0, TURNS) as i:
                for b in range(BATCH):
                    tiles = slice(b * QT, (b + 1) * QT)
                    k_bank, q_bank = c.out[FILL["K", b] % 2], c.out[FILL["Q", b] % 2]
                    dve.wait_ge(s_split, i * len(SPLITS) + (3 * b + 1))
                    dve.tensor_tensor(kT_lo[:, tiles, :], k_bank[:, :, :], kT_hi[:, tiles, :].bitcast(F32),
                                      ALU.subtract).then_inc(c.s_lo, 1)
                    dve.wait_ge(s_split, i * len(SPLITS) + (3 * b + 3))
                    dve.tensor_tensor(q_part_lo[:, tiles, :], q_bank[:, :, :], q_part_hi[:, tiles, :].bitcast(F32),
                                      ALU.subtract).then_inc(c.s_lo, 1)
                    dve.wait_ge(c.s_lo, done(i * c.fills + FILL["Q", b]))
                    dve.scalar_tensor_tensor(q_mixed[:, tiles, :], q_part_lo[:, tiles, :], row_kind[:, 1:2],
                                             q_part_sel[:, tiles, :].bitcast(F32), ALU.mult,
                                             ALU.add).then_inc(s_mixed, 1)
                for s in range(PER + 11):
                    if LAG <= s < PER + LAG and (s - LAG) % 2 == 0:
                        c.copy(dve, dve.tensor_copy, i, s - LAG, units[s - LAG][1],
                               lambda e: c.wait_slot(e, i, s - LAG, FILL))
                    if s < PER:
                        c.maximum(dve, i, s, units[s][1])
                    b = (s - 23) // 16
                    if s in (23, 39):
                        c.output(dve, i, b, FILL["O", b])
                    if s in (26, 42):
                        c.to_tokens(dve, i, b, FILL["T", b],
                                    m.tok[:, b * QT:(b + 1) * QT, bass.ds(i * (G * HD), G * HD)])

        @block.tensor
        def _(pe):
            for step in range(THIRDS * TILES):
                third, t = divmod(step, TILES)
                if t == 0:
                    pe.wait_ge(s_wlo, third + 1)
                if step >= 2:
                    pe.wait_ge(s_raw, step - 1)
                for k in range(KT):
                    last = mm3(pe, proj[step % 2][:, :], pair(m.xnT_hi, m.xnT_lo, slice(None), k, bass.ts(t, P)),
                               pair(w_hi, w_lo, slice(None), k), start=k == 0, stop=k == KT - 1)
                last.then_inc(s_proj, 1)
            pe.wait_ge(s_zero, 2)
            pe.wait_ge(s_raw, THIRDS * TILES)
            c.pe_start(pe)

            with pe.Fori(0, TURNS) as i:
                for b in range(BATCH):
                    for kind in "KQ":
                        f = FILL[kind, b]
                        pe.wait_ge(s_twice, i * 4 + ((2 if kind == "K" else 4) + HEAD))
                        pe.wait_ge(c.s_lo, done(i * c.fills + f - 2))
                        for r in range(QT):
                            last = pe.transpose(c.out[f % 2][:, r, :],
                                                twice[kind][:, b * QT + r, :, :, :].rearrange("p g c x -> p (g c x)"),
                                                m.ident[:, :])
                        last.then_inc(c.s_fill, 1)
                for s in range(PER + 10):
                    if s < PER:
                        b, qt, j = units[s]
                        rows = slice(32 * j, 32 * j + 32)
                        if s % (QT * G) == 0:
                            pe.wait_ge(s_mixed, i * BATCH + (b + 1))
                        c.score(pe, m, i, s, qt, (q_mixed[rows, b * QT + qt, :], None),
                                lambda w: tuple(x[rows, b * QT:b * QT + w // P, :].rearrange("p t q -> p (t q)")
                                                for x in (kT_hi, kT_lo)),
                                m.mask[:, 1, :], ident408[:, :])
                    if 3 <= s < PER + 3:
                        c.turn(pe, m, i, s - 3, units[s - 3][1])
                    if s in (22, 38):
                        b = (s - 22) // 16
                        if b == 0:
                            pe.wait_ge(s_vnow, i + 1)
                        c.times_v_together(pe, i, b, FILL["O", b], lambda e, k: v_now[:, b * QT + k, e, :])
                    if s in (24, 40):
                        b = (s - 24) // 16
                        c.back_to_tokens(pe, m, i, b, FILL["T", b])


def lay_out_attention(o, a):
    t = np.transpose
    kv, q = a["L0_attn_a_Wkv_d"], a["L0_attn_a_Wq_d"]
    rows = np.zeros((DIM, 4, 32), np.float32)
    rows[:, :, 0:12] = np.tile(kv, 3)[:, None, :]
    both = np.zeros((DIM, P), np.float32)
    both[:, 0:12], both[:, 32:36] = q, kv
    o["a0_down"] = np.concatenate([rows.reshape(DIM, P), both], 1)
    bias = np.zeros((P, 2), np.float32)
    bias.reshape(4, 32, 2)[:, 0:12, 0] = np.tile(a["L0_attn_a_bkv_d"], 3)
    bias.reshape(4, 32, 2)[:, 12, 0] = 1.0
    bias[0:12, 1], bias[12, 1], bias[32:36, 1] = a["L0_attn_a_bq_d"], 1.0, a["L0_attn_a_bkv_d"]
    o["a0_down_bias"] = bias
    wqk = np.concatenate([a["L0_attn_a_W_qk"], a["L0_attn_a_b_qk"][None]], 0).reshape(13, 8, 4, 1, 4)
    spread = np.zeros((13, 8, 4, 8, 4), np.float32)
    spread[:, :, :, 0:3, :] = wqk
    o["a0_wqk"] = spread.reshape(13, 8 * P)
    o["a0_wv"], o["a0_bv"] = a["L0_attn_a_Wv_u"], a["L0_attn_a_bv_u"]
    o["a0_wo"], o["a0_bo"] = a["L0_attn_a_Wo"], a["L0_attn_a_bo"]

    order = np.concatenate([np.arange(0, 32), np.arange(64, 96), np.arange(32, 64), np.arange(96, 128)])
    o["b0_down"] = a["L0_attn_b_Wdk"]
    upk = t(a["L0_attn_b_Wupk"].reshape(8, 64, DIM), (0, 2, 1))
    upv = t(a["L0_attn_b_Wupv"].reshape(8, 128, DIM), (0, 2, 1))
    o["b0_up"] = np.concatenate([upk, upv], 2)
    o["b0_rot"] = t(a["L0_attn_b_Wkr"].reshape(8, 64, DIM), (0, 2, 1))
    wq = a["L0_attn_b_Wq"].reshape(8, 4, 128, DIM)[:, :, order]
    o["b0_q"] = t(wq.reshape(8, DIM, DIM), (0, 2, 1))
    o["b0_o"] = t(a["L0_attn_b_Wo"]).reshape(8, DIM, DIM)

    turned = np.concatenate([np.arange(0, 64, 2), np.arange(1, 64, 2)])
    kva = a["L1_attn_a_wkv_a"]
    o["b1_down"] = t(np.concatenate([a["L1_attn_a_wq_a"], kva[0:64], kva[64:128][turned]], 0))
    norm = np.zeros((2, P), np.float32)
    norm.reshape(-1)[0:192] = a["L1_attn_a_q_norm_w"]
    o["b1_q_norm"], o["b1_kv_norm"] = t(norm), a["L1_attn_a_kv_norm_w"]
    wq = a["L1_attn_a_wq_b"].reshape(8, 4, 192, 192)
    o["b1_qn"] = t(wq[:, :, 0:128], (0, 2, 1, 3))
    o["b1_qr"] = t(wq[:, :, 128:192][:, :, turned], (0, 3, 1, 2))
    wkv = a["L1_attn_a_wkv_b"].reshape(8, 4, 256, 64)
    o["b1_k"], o["b1_v"] = t(wkv[:, :, 0:128], (0, 2, 1, 3)), t(wkv[:, :, 128:256], (0, 2, 1, 3))
    o["b1_o"] = t(t(a["L1_attn_a_wo"]).reshape(8, 4, 128, DIM), (0, 2, 1, 3))

    o["c1_w"] = t(a["L1_attn_b_qkv_w"].reshape(DIM, 3, DIM), (1, 0, 2))
    o["c1_bias"] = a["L1_attn_b_qkv_b"]
    o["c1_wo"], o["c1_bo"] = a["L1_attn_b_out_w"], a["L1_attn_b_out_b"]


def attn1b(nc, m, d, prefix):
    with nc.sbuf_tensor(f"{prefix}_tok", [P, TILES, DIM], F32) as m.tok:
        attn1b_block(nc, m, d, prefix)
        project_block(nc, m, d, prefix + "o", "c1_wo", "c1_bo")


def attn0a(nc, m, d, prefix):
    with nc.sbuf_tensor(f"{prefix}_tok", [P, TILES, DIM], F32) as m.tok:
        attn0a_block(nc, m, d, prefix)
        project_block(nc, m, d, prefix + "o", "a0_wo", "a0_bo")


BLOCKS = {"ffn0": ffn0_block, "ffn1": ffn1_block, "attn0a": attn0a, "attn0b": attn0b_block, "attn1a": attn1a_block,
          "attn1b": attn1b}


class Model:
    pass


PHASES = ["attn0a", "ffn0", "attn0b", "ffn0", "attn1a", "ffn1", "attn1b", "ffn1"]


def build(nc, d):
    with ExitStack() as ctx:
        m = Model()
        m.x = ctx.enter_context(nc.sbuf_tensor("x_resident", [P, TILES, DIM], F32))
        with nc.sbuf_tensor("xnT", [P, 2, KT, TILES * P], F32R) as xnT:
            m.xnT_hi, m.xnT_lo = xnT[:, 0], xnT[:, 1]
        m.probsT_odd = ctx.enter_context(nc.sbuf_tensor("probsT_odd", [P, QT, 4, QT, P], F32))
        m.ident = ctx.enter_context(nc.sbuf_tensor("ident_f32", [P, P], F32))
        m.ident16 = ctx.enter_context(nc.sbuf_tensor("ident_bf16", [P, P], BF16))
        m.mask = ctx.enter_context(nc.sbuf_tensor("mask_bf16", [P, 2, P], BF16))
        load_block(nc, m, d)
        for i, phase in enumerate(PHASES):
            layernorm_block(nc, m, f"ln{i}")
            BLOCKS[phase](nc, m, d, f"{phase}_{i}")
        store_block(nc, m, d)


def shape_constants():
    bf16 = lambda x: (x.astype(np.float32).view(np.uint32) >> 16).astype(np.uint16)
    c = {}
    c["ident"] = np.eye(P, dtype=np.float32)
    c["ident16"] = bf16(np.eye(P))
    later = np.triu(np.ones((P, P), np.float32), 1)
    c["mask"] = bf16(np.stack([later * np.float32(-1e30), later * np.float32(-163.0)], 1))
    c["adapter_of_row"] = (np.arange(48, dtype=np.float32) // 16).reshape(48, 1)
    kind = np.arange(P) % 32 // 4
    c["a0_row_kind"] = np.stack([(kind < 2) | (np.arange(P) % 32 == 12), kind == 2, 0.5 * (kind % 2 == 0) * (kind < 3), kind == 1],
                                1).astype(np.float32)
    inv = 1.0 / 10000.0 ** (np.arange(0, 128, 2, dtype=np.float32) / 128)
    ang = np.outer(np.arange(SEQ, dtype=np.float32), inv)
    cos, sin = np.cos(ang), np.sin(ang)
    pairs = lambda lo, hi: np.concatenate([lo[:, 0:32], hi[:, 0:32], lo[:, 32:64], hi[:, 32:64]], 1)
    tiles = lambda x: np.ascontiguousarray(x.reshape(QT, P, -1).transpose(1, 0, 2).astype(np.float32))
    scale = np.float32(1.0 / np.sqrt(128.0))
    c["b0_cos_q"], c["b0_sin_q"] = tiles(pairs(cos, cos) * scale), tiles(pairs(-sin, sin) * scale)
    c["b0_cos_k"], c["b0_sin_k"] = tiles(pairs(cos, cos)[:, 0:64]), tiles(pairs(-sin, sin)[:, 0:64])
    freq = 1.0 / 10000.0 ** (np.arange(0, 64, 2, dtype=np.float32) / 64)
    ang = np.outer(np.arange(SEQ, dtype=np.float32), freq)
    cos, sin = np.cos(ang), np.sin(ang)
    scale = np.float32(1.0 / np.sqrt(np.float32(192.0)))
    both, signed = np.concatenate([cos, cos], 1), np.concatenate([-sin, sin], 1)
    c["b1_cos_q"], c["b1_sin_q"] = tiles(both * scale), tiles(signed * scale)
    c["b1_cos_k"], c["b1_sin_k"] = tiles(both), tiles(signed)
    ang = np.arange(SEQ, dtype=np.float32)[:, None] * (1.0 / 10000.0 ** (np.arange(0, 8, dtype=np.float32) / 8))
    cos, sin = np.cos(ang), np.sin(ang)
    table = np.stack([cos, -sin, sin], 1).reshape(QT, P, 3, 8).transpose(1, 0, 2, 3)
    c["c1_cos_sin"] = np.stack([table * np.float32(0.25), table], 1).astype(np.float32)
    half = np.arange(P) % 32 // 16
    c["c1_row_kind"] = np.stack([half == 0, half == 1], 1).astype(np.float32)
    c["ident408"] = bf16(np.eye(P) * 408)
    c["expert_no"] = np.arange(8, dtype=np.float32)
    return c


def laid_out(inp):
    t = np.transpose
    a = {k: np.asarray(v) for k, v in inp.items()}
    o = {}
    o["x"] = a["L0_attn_a_x"]
    o["ffn0_w"] = t(a["L0_ffn_weight"])
    o["ffn0_bias"] = a["L0_ffn_bias"]
    o["lora_a"] = a["L0_ffn_lora_A"].reshape(48, DIM)
    o["lora_b"] = t(a["L0_ffn_lora_B"], (0, 2, 1)).reshape(48, DIM)
    o["lora_starts"] = a["L0_ffn_lora_start_indices"]
    o["ffn1_w"] = t(a["L1_ffn_W_base"])
    o["ffn1_bias"] = a["L1_ffn_b_base"]
    o["ffn1_a"] = np.concatenate([t(a["L1_ffn_A"].reshape(128, DIM)), t(a["L1_ffn_W_router"])], 1)
    o["ffn1_b"] = t(a["L1_ffn_B"], (0, 2, 1)).reshape(128, DIM)
    lay_out_attention(o, a)
    return o


def kernel(**inputs):
    import concourse.bacc as bacc
    from concourse.bass_utils import run_bass_kernel_spmd

    nc = bacc.Bacc("TRN2", target_bir_lowering=False, num_devices=1)
    arrays, d = {}, {}
    for name, v in {**laid_out(inputs), **shape_constants()}.items():
        v = np.ascontiguousarray(v)
        arrays[f"in_{name}"] = v
        d[name] = nc.dram_tensor(f"in_{name}", v.shape, mybir.dt.from_np(v.dtype), kind="ExternalInput").ap()
    d["out"] = nc.dram_tensor("out_y", (BATCH, SEQ, DIM), F32, kind="ExternalOutput").ap()
    build(nc, d)
    return run_bass_kernel_spmd(nc, [arrays], core_ids=[0]).results[0]["out_y"]
```
